# Optimizing a Trainium2 kernel written in Bass

```python
import numpy as np
import jax
import jax.numpy as jnp

def _softmax(x, axis=-1):
    return jax.nn.softmax(x, axis=axis)

def _gelu(x):
    return jax.nn.gelu(x, approximate=True)

def _silu(x):
    return jax.nn.silu(x)

def _sigmoid(x):
    return jax.nn.sigmoid(x)

def _layernorm(x, axis=-1, eps=1e-05):
    m = jnp.mean(x, axis=axis, keepdims=True)
    v = jnp.var(x, axis=axis, keepdims=True)
    return (x - m) / jnp.sqrt(v + eps)

def _scatter_add(tgt, idx, src, axis=0):
    return tgt.at[idx].add(src)

def _segment_sum(src, seg, n):
    return jax.ops.segment_sum(src, seg, n)
kernel_name = 'mk_conv_seq_d4_conv_nhwc768_r4_d43897'

def setup_inputs(seed: int=0):
    np.random.seed(seed)
    _w = jnp.asarray

    def _rec_inputs():
        import jax
        import jax.numpy as jnp
        _gk = jax.random.key(seed)
        x = -0.0004039 + 1 * jax.random.normal(jax.random.fold_in(_gk, 1), (4, 16, 16, 192), jnp.float32)
        return x
    x = _rec_inputs()

    def _L0_conv_setup():
        import jax, jax.numpy as jnp
        import numpy as np
        B, H, W, C = (4, 16, 16, 192)
        HEADS, HD = (12, 16)
        WS = 14
        HID = 768
        EPS = 1e-06

        def _layer_norm(x, scale, bias):
            mu = jnp.mean(x, axis=-1, keepdims=True)
            var = jnp.mean(jnp.square(x - mu), axis=-1, keepdims=True)
            return (x - mu) * jax.lax.rsqrt(var + EPS) * scale + bias
        key = jax.random.key(seed)
        ks = jax.random.split(key, 8)
        w = lambda k, shape: jax.random.normal(k, shape, jnp.float32) * 0.02
        return {'x': jax.random.normal(ks[0], (B, H, W, C), jnp.float32), 'norm1_scale': jnp.ones((C,), jnp.float32), 'norm1_bias': jnp.zeros((C,), jnp.float32), 'qkv_w': w(ks[1], (C, 3 * C)), 'qkv_b': jnp.zeros((3 * C,), jnp.float32), 'rel_pos_h': w(ks[2], (2 * WS - 1, HD)), 'rel_pos_w': w(ks[3], (2 * WS - 1, HD)), 'proj_w': w(ks[4], (C, C)), 'proj_b': jnp.zeros((C,), jnp.float32), 'norm2_scale': jnp.ones((C,), jnp.float32), 'norm2_bias': jnp.zeros((C,), jnp.float32), 'fc1_w': w(ks[5], (C, HID)), 'fc1_b': jnp.zeros((HID,), jnp.float32), 'fc2_w': w(ks[6], (HID, C)), 'fc2_b': jnp.zeros((C,), jnp.float32)}
    _L0_conv_all = _L0_conv_setup()
    _L0_conv_in = {k: v for k, v in _L0_conv_all.items() if k in ('norm1_scale', 'norm1_bias', 'qkv_w', 'qkv_b', 'rel_pos_h', 'rel_pos_w', 'proj_w', 'proj_b', 'norm2_scale', 'norm2_bias', 'fc1_w', 'fc1_b', 'fc2_w', 'fc2_b')}
    del _L0_conv_all

    def _L1_conv_setup():
        import jax, jax.numpy as jnp
        import numpy as np
        SPARSITY_THRESHOLD = 0.01
        HARD_THRESH_FRAC = 1.0

        def softshrink(x, lam):
            return jnp.where(x > lam, x - lam, jnp.where(x < -lam, x + lam, jnp.zeros_like(x)))

        def compl_mul_add_act(a, b, c):
            tmp = jnp.einsum('bxykis,kiot->stbxyko', a, b)
            real = tmp[0, 0] - tmp[1, 1]
            imag = tmp[1, 0] + tmp[0, 1]
            return jnp.stack([real, imag], axis=-1) + c
        key = jax.random.key(seed)
        k = jax.random.split(key, 5)
        B, H, W, C = (1, 64, 64, 192)
        nb, bs, factor = (8, 24, 1)
        scale = 0.02
        return {'x': jax.random.normal(k[0], (B, H, W, C), dtype=jnp.float32), 'w1': scale * jax.random.normal(k[1], (nb, bs, bs * factor, 2), dtype=jnp.float32), 'b1': scale * jax.random.normal(k[2], (nb, bs * factor, 2), dtype=jnp.float32), 'w2': scale * jax.random.normal(k[3], (nb, bs * factor, bs, 2), dtype=jnp.float32), 'b2': scale * jax.random.normal(k[4], (nb, bs, 2), dtype=jnp.float32)}
    _L1_conv_all = _L1_conv_setup()
    _L1_conv_in = {k: v for k, v in _L1_conv_all.items() if k in ('w1', 'b1', 'w2', 'b2')}
    del _L1_conv_all

    def _L2_conv_setup():
        import jax, jax.numpy as jnp
        import numpy as np
        DIM = 192
        NH = 12
        HD = DIM // NH
        WS = 14
        EPS = 1e-05

        def _ln(x, w, b):
            m = jnp.mean(x, -1, keepdims=True)
            v = jnp.var(x, -1, keepdims=True)
            return (x - m) * jax.lax.rsqrt(v + EPS) * w + b

        def _block(x, ln1_w, ln1_b, qkv_w, qkv_b, proj_w, proj_b, rel_pos_h, rel_pos_w, ln2_w, ln2_b, fc1_w, fc1_b, fc2_w, fc2_b):
            B, H, W, C = x.shape
            shortcut = x
            xn = _ln(x, ln1_w, ln1_b)
            pad_h = -H % WS
            pad_w = -W % WS
            xp = jnp.pad(xn, ((0, 0), (0, pad_h), (0, pad_w), (0, 0)))
            Hp, Wp = (H + pad_h, W + pad_w)
            nh, nw = (Hp // WS, Wp // WS)
            xw = xp.reshape(B, nh, WS, nw, WS, C).transpose(0, 1, 3, 2, 4, 5)
            xw = xw.reshape(B * nh * nw, WS, WS, C)
            Bw = B * nh * nw
            N = WS * WS
            qkv = xw.reshape(Bw, N, C) @ qkv_w + qkv_b
            qkv = qkv.reshape(Bw, N, 3, NH, HD).transpose(2, 0, 3, 1, 4)
            q, k, v = (qkv[0], qkv[1], qkv[2])
            scale = HD ** (-0.5)
            attn = jnp.einsum('bhnd,bhmd->bhnm', q * scale, k)
            idx = jnp.arange(WS)[:, None] - jnp.arange(WS)[None, :] + (WS - 1)
            Rh = rel_pos_h[idx]
            Rw = rel_pos_w[idx]
            rq = q.reshape(Bw, NH, WS, WS, HD)
            rel_h = jnp.einsum('bnhwc,hkc->bnhwk', rq, Rh)
            rel_w = jnp.einsum('bnhwc,wkc->bnhwk', rq, Rw)
            attn = (attn.reshape(Bw, NH, WS, WS, WS, WS) + rel_h[..., :, None] + rel_w[..., None, :]).reshape(Bw, NH, N, N)
            attn = jax.nn.softmax(attn, axis=-1)
            out = jnp.einsum('bhnm,bhmd->bhnd', attn, v)
            out = out.transpose(0, 2, 1, 3).reshape(Bw, WS, WS, C)
            out = out @ proj_w + proj_b
            out = out.reshape(B, nh, nw, WS, WS, C).transpose(0, 1, 3, 2, 4, 5)
            out = out.reshape(B, Hp, Wp, C)[:, :H, :W, :]
            x = shortcut + out
            h = _ln(x, ln2_w, ln2_b)
            h = jax.nn.gelu(h @ fc1_w + fc1_b, approximate=False)
            x = x + (h @ fc2_w + fc2_b)
            return x
        key = jax.random.key(seed)
        ks = jax.random.split(key, 8)

        def n(k, shape, s=0.02):
            return jax.random.normal(k, shape, jnp.float32) * s
        return {'x': jax.random.normal(ks[0], (4, 16, 16, DIM), jnp.float32), 'ln1_w': jnp.ones((DIM,), jnp.float32), 'ln1_b': jnp.zeros((DIM,), jnp.float32), 'qkv_w': n(ks[1], (DIM, 3 * DIM)), 'qkv_b': jnp.zeros((3 * DIM,), jnp.float32), 'proj_w': n(ks[2], (DIM, DIM)), 'proj_b': jnp.zeros((DIM,), jnp.float32), 'rel_pos_h': n(ks[3], (2 * WS - 1, HD)), 'rel_pos_w': n(ks[4], (2 * WS - 1, HD)), 'ln2_w': jnp.ones((DIM,), jnp.float32), 'ln2_b': jnp.zeros((DIM,), jnp.float32), 'fc1_w': n(ks[5], (DIM, 4 * DIM)), 'fc1_b': jnp.zeros((4 * DIM,), jnp.float32), 'fc2_w': n(ks[6], (4 * DIM, DIM)), 'fc2_b': jnp.zeros((DIM,), jnp.float32)}
    _L2_conv_all = _L2_conv_setup()
    _L2_conv_in = {k: v for k, v in _L2_conv_all.items() if k in ('ln1_w', 'ln1_b', 'qkv_w', 'qkv_b', 'proj_w', 'proj_b', 'rel_pos_h', 'rel_pos_w', 'ln2_w', 'ln2_b', 'fc1_w', 'fc1_b', 'fc2_w', 'fc2_b')}
    del _L2_conv_all

    def _L3_conv_setup():
        import jax, jax.numpy as jnp
        import numpy as np

        def _dht(x):
            f = jnp.fft.fftn(x)
            return f.real + f.imag
        key = jax.random.key(seed)
        ks = jax.random.split(key, 5)
        B, H, W, C = (2, 32, 64, 192)
        nb, fac = (8, 1)
        bs = C // nb
        scale = 0.02
        x = jax.random.normal(ks[0], (B, H, W, C), dtype=jnp.float32)
        w1 = scale * jax.random.normal(ks[1], (2, nb, bs, bs * fac), dtype=jnp.float32)
        b1 = scale * jax.random.normal(ks[2], (2, nb, bs * fac), dtype=jnp.float32)
        w2 = scale * jax.random.normal(ks[3], (2, nb, bs * fac, bs), dtype=jnp.float32)
        b2 = scale * jax.random.normal(ks[4], (2, nb, bs), dtype=jnp.float32)
        return {'x': x, 'w1': w1, 'b1': b1, 'w2': w2, 'b2': b2}
    _L3_conv_all = _L3_conv_setup()
    _L3_conv_in = {k: v for k, v in _L3_conv_all.items() if k in ('w1', 'b1', 'w2', 'b2')}
    del _L3_conv_all
    return {'x': x, 'L0_conv_norm1_scale': _L0_conv_in['norm1_scale'], 'L0_conv_norm1_bias': _L0_conv_in['norm1_bias'], 'L0_conv_qkv_w': _L0_conv_in['qkv_w'], 'L0_conv_qkv_b': _L0_conv_in['qkv_b'], 'L0_conv_rel_pos_h': _L0_conv_in['rel_pos_h'], 'L0_conv_rel_pos_w': _L0_conv_in['rel_pos_w'], 'L0_conv_proj_w': _L0_conv_in['proj_w'], 'L0_conv_proj_b': _L0_conv_in['proj_b'], 'L0_conv_norm2_scale': _L0_conv_in['norm2_scale'], 'L0_conv_norm2_bias': _L0_conv_in['norm2_bias'], 'L0_conv_fc1_w': _L0_conv_in['fc1_w'], 'L0_conv_fc1_b': _L0_conv_in['fc1_b'], 'L0_conv_fc2_w': _L0_conv_in['fc2_w'], 'L0_conv_fc2_b': _L0_conv_in['fc2_b'], 'L1_conv_w1': _L1_conv_in['w1'], 'L1_conv_b1': _L1_conv_in['b1'], 'L1_conv_w2': _L1_conv_in['w2'], 'L1_conv_b2': _L1_conv_in['b2'], 'L2_conv_ln1_w': _L2_conv_in['ln1_w'], 'L2_conv_ln1_b': _L2_conv_in['ln1_b'], 'L2_conv_qkv_w': _L2_conv_in['qkv_w'], 'L2_conv_qkv_b': _L2_conv_in['qkv_b'], 'L2_conv_proj_w': _L2_conv_in['proj_w'], 'L2_conv_proj_b': _L2_conv_in['proj_b'], 'L2_conv_rel_pos_h': _L2_conv_in['rel_pos_h'], 'L2_conv_rel_pos_w': _L2_conv_in['rel_pos_w'], 'L2_conv_ln2_w': _L2_conv_in['ln2_w'], 'L2_conv_ln2_b': _L2_conv_in['ln2_b'], 'L2_conv_fc1_w': _L2_conv_in['fc1_w'], 'L2_conv_fc1_b': _L2_conv_in['fc1_b'], 'L2_conv_fc2_w': _L2_conv_in['fc2_w'], 'L2_conv_fc2_b': _L2_conv_in['fc2_b'], 'L3_conv_w1': _L3_conv_in['w1'], 'L3_conv_b1': _L3_conv_in['b1'], 'L3_conv_w2': _L3_conv_in['w2'], 'L3_conv_b2': _L3_conv_in['b2']}

def reference(x, L0_conv_norm1_scale, L0_conv_norm1_bias, L0_conv_qkv_w, L0_conv_qkv_b, L0_conv_rel_pos_h, L0_conv_rel_pos_w, L0_conv_proj_w, L0_conv_proj_b, L0_conv_norm2_scale, L0_conv_norm2_bias, L0_conv_fc1_w, L0_conv_fc1_b, L0_conv_fc2_w, L0_conv_fc2_b, L1_conv_w1, L1_conv_b1, L1_conv_w2, L1_conv_b2, L2_conv_ln1_w, L2_conv_ln1_b, L2_conv_qkv_w, L2_conv_qkv_b, L2_conv_proj_w, L2_conv_proj_b, L2_conv_rel_pos_h, L2_conv_rel_pos_w, L2_conv_ln2_w, L2_conv_ln2_b, L2_conv_fc1_w, L2_conv_fc1_b, L2_conv_fc2_w, L2_conv_fc2_b, L3_conv_w1, L3_conv_b1, L3_conv_w2, L3_conv_b2):
    import jax
    import jax.numpy as jnp

    def _L0_conv_ref(x, norm1_scale, norm1_bias, qkv_w, qkv_b, rel_pos_h, rel_pos_w, proj_w, proj_b, norm2_scale, norm2_bias, fc1_w, fc1_b, fc2_w, fc2_b):
        import jax, jax.numpy as jnp
        import numpy as np
        B, H, W, C = (4, 16, 16, 192)
        HEADS, HD = (12, 16)
        WS = 14
        HID = 768
        EPS = 1e-06

        def _layer_norm(x, scale, bias):
            mu = jnp.mean(x, axis=-1, keepdims=True)
            var = jnp.mean(jnp.square(x - mu), axis=-1, keepdims=True)
            return (x - mu) * jax.lax.rsqrt(var + EPS) * scale + bias
        shortcut = x
        y = _layer_norm(x, norm1_scale, norm1_bias)
        pad = (WS - H % WS) % WS
        Hp, Wp = (H + pad, W + pad)
        nwin = Hp // WS
        y = jnp.pad(y, ((0, 0), (0, pad), (0, pad), (0, 0)))
        win = y.reshape(B, nwin, WS, nwin, WS, C).transpose(0, 1, 3, 2, 4, 5)
        win = win.reshape(-1, WS, WS, C)
        Nw = win.shape[0]
        L = WS * WS
        qkv = win.reshape(Nw, L, C) @ qkv_w + qkv_b
        qkv = qkv.reshape(Nw, L, 3, HEADS, HD).transpose(2, 0, 3, 1, 4)
        qkv = qkv.reshape(3, Nw * HEADS, L, HD)
        q, k, v = (qkv[0], qkv[1], qkv[2])
        scale = HD ** (-0.5)
        attn = jnp.einsum('nqc,nkc->nqk', q, k) * scale
        idx = np.arange(WS)[:, None] - np.arange(WS)[None, :] + (WS - 1)
        r_h = rel_pos_h[idx]
        r_w = rel_pos_w[idx]
        q4 = q.reshape(-1, WS, WS, HD)
        bias_h = jnp.einsum('nhwc,hkc->nhwk', q4, r_h)
        bias_w = jnp.einsum('nhwc,wkc->nhwk', q4, r_w)
        attn = attn.reshape(-1, WS, WS, WS, WS)
        attn = attn + bias_h[..., :, None] + bias_w[..., None, :]
        attn = attn.reshape(-1, L, L)
        attn = jax.nn.softmax(attn, axis=-1)
        o = jnp.einsum('nqk,nkc->nqc', attn, v)
        o = o.reshape(Nw, HEADS, WS, WS, HD).transpose(0, 2, 3, 1, 4).reshape(Nw, WS, WS, C)
        o = o @ proj_w + proj_b
        o = o.reshape(B, nwin, nwin, WS, WS, C).transpose(0, 1, 3, 2, 4, 5)
        o = o.reshape(B, Hp, Wp, C)[:, :H, :W, :]
        x = shortcut + o
        h2 = _layer_norm(x, norm2_scale, norm2_bias)
        m = jax.nn.gelu(h2 @ fc1_w + fc1_b, approximate=False)
        m = m @ fc2_w + fc2_b
        return x + m

    def _L1_conv_ref(x, w1, b1, w2, b2):
        import jax, jax.numpy as jnp
        import numpy as np
        SPARSITY_THRESHOLD = 0.01
        HARD_THRESH_FRAC = 1.0

        def softshrink(x, lam):
            return jnp.where(x > lam, x - lam, jnp.where(x < -lam, x + lam, jnp.zeros_like(x)))

        def compl_mul_add_act(a, b, c):
            tmp = jnp.einsum('bxykis,kiot->stbxyko', a, b)
            real = tmp[0, 0] - tmp[1, 1]
            imag = tmp[1, 0] + tmp[0, 1]
            return jnp.stack([real, imag], axis=-1) + c
        bias = x
        dtype = x.dtype
        B, H, W, C = x.shape
        nb, bs = (w1.shape[0], w1.shape[1])
        total_modes = H // 2 + 1
        kept_modes = int(total_modes * HARD_THRESH_FRAC)
        lo = total_modes - kept_modes
        hi = min(total_modes + kept_modes, H)
        xf = jnp.fft.rfft2(x.astype(jnp.float32), axes=(1, 2), norm='ortho')
        xf = xf.reshape(B, H, W // 2 + 1, nb, bs)
        xs = jnp.stack([xf.real, xf.imag], axis=-1)
        sub = xs[:, lo:hi, :kept_modes]
        o1 = jax.nn.relu(compl_mul_add_act(sub, w1, b1))
        o2 = jnp.zeros_like(xs).at[:, lo:hi, :kept_modes].set(compl_mul_add_act(o1, w2, b2))
        o2 = softshrink(o2, SPARSITY_THRESHOLD)
        xc = (o2[..., 0] + 1j * o2[..., 1]).reshape(B, H, W // 2 + 1, C)
        out = jnp.fft.irfft2(xc, s=(H, W), axes=(1, 2), norm='ortho').astype(dtype)
        return out + bias

    def _L2_conv_ref(x, ln1_w, ln1_b, qkv_w, qkv_b, proj_w, proj_b, rel_pos_h, rel_pos_w, ln2_w, ln2_b, fc1_w, fc1_b, fc2_w, fc2_b):
        import jax, jax.numpy as jnp
        import numpy as np
        DIM = 192
        NH = 12
        HD = DIM // NH
        WS = 14
        EPS = 1e-05

        def _ln(x, w, b):
            m = jnp.mean(x, -1, keepdims=True)
            v = jnp.var(x, -1, keepdims=True)
            return (x - m) * jax.lax.rsqrt(v + EPS) * w + b

        def _block(x, ln1_w, ln1_b, qkv_w, qkv_b, proj_w, proj_b, rel_pos_h, rel_pos_w, ln2_w, ln2_b, fc1_w, fc1_b, fc2_w, fc2_b):
            B, H, W, C = x.shape
            shortcut = x
            xn = _ln(x, ln1_w, ln1_b)
            pad_h = -H % WS
            pad_w = -W % WS
            xp = jnp.pad(xn, ((0, 0), (0, pad_h), (0, pad_w), (0, 0)))
            Hp, Wp = (H + pad_h, W + pad_w)
            nh, nw = (Hp // WS, Wp // WS)
            xw = xp.reshape(B, nh, WS, nw, WS, C).transpose(0, 1, 3, 2, 4, 5)
            xw = xw.reshape(B * nh * nw, WS, WS, C)
            Bw = B * nh * nw
            N = WS * WS
            qkv = xw.reshape(Bw, N, C) @ qkv_w + qkv_b
            qkv = qkv.reshape(Bw, N, 3, NH, HD).transpose(2, 0, 3, 1, 4)
            q, k, v = (qkv[0], qkv[1], qkv[2])
            scale = HD ** (-0.5)
            attn = jnp.einsum('bhnd,bhmd->bhnm', q * scale, k)
            idx = jnp.arange(WS)[:, None] - jnp.arange(WS)[None, :] + (WS - 1)
            Rh = rel_pos_h[idx]
            Rw = rel_pos_w[idx]
            rq = q.reshape(Bw, NH, WS, WS, HD)
            rel_h = jnp.einsum('bnhwc,hkc->bnhwk', rq, Rh)
            rel_w = jnp.einsum('bnhwc,wkc->bnhwk', rq, Rw)
            attn = (attn.reshape(Bw, NH, WS, WS, WS, WS) + rel_h[..., :, None] + rel_w[..., None, :]).reshape(Bw, NH, N, N)
            attn = jax.nn.softmax(attn, axis=-1)
            out = jnp.einsum('bhnm,bhmd->bhnd', attn, v)
            out = out.transpose(0, 2, 1, 3).reshape(Bw, WS, WS, C)
            out = out @ proj_w + proj_b
            out = out.reshape(B, nh, nw, WS, WS, C).transpose(0, 1, 3, 2, 4, 5)
            out = out.reshape(B, Hp, Wp, C)[:, :H, :W, :]
            x = shortcut + out
            h = _ln(x, ln2_w, ln2_b)
            h = jax.nn.gelu(h @ fc1_w + fc1_b, approximate=False)
            x = x + (h @ fc2_w + fc2_b)
            return x
        return _block(x, ln1_w, ln1_b, qkv_w, qkv_b, proj_w, proj_b, rel_pos_h, rel_pos_w, ln2_w, ln2_b, fc1_w, fc1_b, fc2_w, fc2_b)

    def _L3_conv_ref(x, w1, b1, w2, b2):
        import jax, jax.numpy as jnp
        import numpy as np

        def _dht(x):
            f = jnp.fft.fftn(x)
            return f.real + f.imag
        SPARSITY = 0.01
        FRAC = 1.0
        bias = x
        B, H, W, C = x.shape
        nb = w1.shape[1]
        bs = C // nb
        xf = x.astype(jnp.float32)
        X_k = _dht(xf).reshape(B, H, W, nb, bs)
        X_nk = jnp.roll(jnp.flip(xf, axis=(1, 2)), shift=(1, 1), axis=(1, 2)).reshape(B, H, W, nb, bs)
        total = H // 2 + 1
        kept = int(total * FRAC)
        r0, r1 = (total - kept, min(total + kept, H))
        a = X_k[:, r0:r1, :kept]
        an = X_nk[:, r0:r1, :kept]
        ein = lambda t, w: jnp.einsum('bhwni,nio->bhwno', t, w)
        o1_k = jax.nn.relu(0.5 * (ein(a, w1[0]) - ein(an, w1[1]) + ein(a, w1[1]) + ein(an, w1[0])) + b1[0])
        o1_nk = jax.nn.relu(0.5 * (ein(an, w1[0]) - ein(a, w1[1]) + ein(an, w1[1]) + ein(a, w1[0])) + b1[1])
        o2_k = 0.5 * (ein(o1_k, w2[0]) - ein(o1_nk, w2[1]) + ein(o1_k, w2[1]) + ein(o1_nk, w2[0])) + b2[0]
        o2_nk = 0.5 * (ein(o1_nk, w2[0]) - ein(o2_k, w2[1]) + ein(o1_nk, w2[1]) + ein(o2_k, w2[0])) + b2[1]
        s = o2_k + o2_nk
        s = jnp.sign(s) * jnp.maximum(jnp.abs(s) - SPARSITY, 0.0)
        full = jnp.zeros((B, H, W, nb, bs), jnp.float32).at[:, r0:r1, :kept].set(s)
        full = full.reshape(B, H, W, C)
        out = _dht(full) / full.size
        return out.astype(x.dtype) + bias

    def _gn(v, G=32, eps=1e-05):
        B_, H_, W_, C_ = v.shape
        g = v.reshape(B_, H_, W_, G, C_ // G)
        m = jnp.mean(g, axis=(1, 2, 4), keepdims=True)
        s = jnp.var(g, axis=(1, 2, 4), keepdims=True)
        return ((g - m) / jnp.sqrt(s + eps)).reshape(v.shape)

    def _ln_c(v, eps=1e-06):
        m = jnp.mean(v, axis=-1, keepdims=True)
        s = jnp.var(v, axis=-1, keepdims=True)
        return (v - m) / jnp.sqrt(s + eps)

    def _ln_t(v, eps=1e-05):
        m = jnp.mean(v, axis=-1, keepdims=True)
        s = jnp.var(v, axis=-1, keepdims=True)
        return (v - m) / jnp.sqrt(s + eps)

    def _to_tokens(v):
        B_, H_, W_, C_ = v.shape
        return v.reshape(B_, H_ * W_, C_)

    def _from_tokens(t, like):
        return t.reshape(like.shape)
    x = _L0_conv_ref(x, L0_conv_norm1_scale, L0_conv_norm1_bias, L0_conv_qkv_w, L0_conv_qkv_b, L0_conv_rel_pos_h, L0_conv_rel_pos_w, L0_conv_proj_w, L0_conv_proj_b, L0_conv_norm2_scale, L0_conv_norm2_bias, L0_conv_fc1_w, L0_conv_fc1_b, L0_conv_fc2_w, L0_conv_fc2_b)
    x = _L1_conv_ref(x, L1_conv_w1, L1_conv_b1, L1_conv_w2, L1_conv_b2)
    x = _L2_conv_ref(x, L2_conv_ln1_w, L2_conv_ln1_b, L2_conv_qkv_w, L2_conv_qkv_b, L2_conv_proj_w, L2_conv_proj_b, L2_conv_rel_pos_h, L2_conv_rel_pos_w, L2_conv_ln2_w, L2_conv_ln2_b, L2_conv_fc1_w, L2_conv_fc1_b, L2_conv_fc2_w, L2_conv_fc2_b)
    x = _L3_conv_ref(x, L3_conv_w1, L3_conv_b1, L3_conv_w2, L3_conv_b2)
    return x

_drawn_inputs = setup_inputs


def setup_inputs(seed=0):
    import zlib

    import numpy as np

    out = dict(_drawn_inputs(seed))
    spreads = {'L0_conv_norm1_scale': (1.0, 0.6),
     'L0_conv_norm1_bias': (0.0, 0.8),
     'L0_conv_qkv_b': (0.0, 0.29),
     'L0_conv_proj_b': (0.0, 0.1),
     'L0_conv_norm2_scale': (1.0, 0.6),
     'L0_conv_norm2_bias': (0.0, 0.8),
     'L0_conv_fc1_b': (0.0, 0.279),
     'L0_conv_fc2_b': (0.0, 0.1),
     'L2_conv_ln1_w': (1.0, 0.6),
     'L2_conv_ln1_b': (0.0, 0.8),
     'L2_conv_qkv_b': (0.0, 0.295),
     'L2_conv_proj_b': (0.0, 0.1),
     'L2_conv_ln2_w': (1.0, 0.6),
     'L2_conv_ln2_b': (0.0, 0.8),
     'L2_conv_fc1_b': (0.0, 0.293),
     'L2_conv_fc2_b': (0.0, 0.1)}
    factors = {'L0_conv_qkv_w': 6.537,
     'L0_conv_rel_pos_h': 8.0,
     'L0_conv_rel_pos_w': 8.0,
     'L1_conv_w1': 7.266,
     'L1_conv_b1': 8.0,
     'L1_conv_w2': 5.895,
     'L1_conv_b2': 3.077,
     'L2_conv_qkv_w': 5.121,
     'L2_conv_rel_pos_h': 8.0,
     'L2_conv_rel_pos_w': 8.0,
     'L3_conv_w1': 8.0,
     'L3_conv_b1': 64.0,
     'L3_conv_w2': 8.0,
     'L3_conv_b2': 64.0}
    for name, (base, spread) in spreads.items():
        noise = np.random.default_rng([zlib.crc32(name.encode()), seed]).standard_normal(out[name].shape)
        drawn = base * np.exp(spread * noise) if base else spread * noise
        out[name] = jnp.asarray(drawn.astype(out[name].dtype))
    for name, factor in factors.items():
        out[name] = (out[name] * factor).astype(out[name].dtype)
    return out
```

```python
from contextlib import ExitStack

import numpy as np
import concourse.bass as bass
from concourse import mybir

F32 = mybir.dt.float32
ALU = mybir.AluOpType
ACT = mybir.ActivationFunctionType
AX = mybir.AxisListType.X

IMAGES, SIDE, CH = 4, 16, 192
WIN = 14
EDGE = SIDE - WIN
PLACES = SIDE * SIDE
TOKENS = IMAGES * PLACES
TILES = TOKENS // 128
HALF = CH // 2
HEADS, HD = 12, 16
PAIRS = HEADS // 2
GROUP = HALF // HD
HID = 4 * CH
HID_TILES = HID // 128
CODES = 2 * IMAGES
AUG = HD + 2 * WIN + CODES
PAD_RIGHT = WIN * (WIN - EDGE)
PAD_LOW = PAD_RIGHT + EDGE * (WIN - EDGE)
KEYS = TOKENS + PAD_RIGHT + PAD_LOW
HW_ROWS = WIN // 2
HALF_WIN = HW_ROWS * WIN
MAIN = IMAGES * WIN * WIN
RIGHT = IMAGES * WIN * EDGE
LOW = IMAGES * EDGE * SIDE
BIG = 1e30
HALF_COLS = SIDE // 2 + 1
MODES = SIDE * HALF_COLS
MCHUNK = MODES // 2
LAMBDA = 0.01
EPS = (1e-6, 1e-5)


def _places():
    h, w = np.divmod(np.arange(PLACES), SIDE)
    return h, w


def _key_rows():
    out = np.zeros((2 * WIN + CODES, KEYS), np.float32)
    h, w = _places()
    for b in range(IMAGES):
        at = b * PLACES + np.arange(PLACES)
        out[h % WIN, at] = 4.0
        out[WIN + w % WIN, at] = 4.0
        for code in range(CODES):
            right = (h < WIN) & (w >= WIN)
            low = (h >= WIN) & (w < WIN)
            corner = (h >= WIN) & (w >= WIN)
            other = (right & (code != b) & (code < IMAGES)) | (low & (code != b)) | (corner & (code != IMAGES + b))
            out[2 * WIN + code, at[other]] = -BIG
    pads = [(i, j) for i in range(WIN) for j in range(EDGE, WIN)]
    pads += [(i, j) for i in range(EDGE, WIN) for j in range(WIN)]
    pads += [(i, j) for i in range(EDGE) for j in range(EDGE, WIN)]
    for n, (i, j) in enumerate(pads):
        out[i, TOKENS + n] = 4.0
        out[WIN + j, TOKENS + n] = 4.0
    out[2 * WIN:2 * WIN + IMAGES, TOKENS + 2 * PAD_RIGHT:] = -BIG
    return out


def _query_codes():
    out = np.zeros((CODES, TOKENS), np.float32)
    for b in range(IMAGES):
        out[b, MAIN + b * WIN * EDGE:MAIN + (b + 1) * WIN * EDGE] = 1.0
        for r in range(EDGE):
            at = MAIN + RIGHT + (EDGE * b + r) * SIDE
            out[b, at:at + WIN] = 1.0
            out[IMAGES + b, at + WIN:at + SIDE] = 1.0
    return out


def constants():
    h, w = _places()
    kh, kw = np.divmod(np.arange(MODES), HALF_COLS)
    theta = 2 * np.pi * (np.outer(h, kh) + np.outer(w, kw)) / SIDE
    space = np.stack([np.cos(theta), -np.sin(theta)], 1)
    back = np.stack([np.cos(theta) - np.sin(theta), np.cos(theta) + np.sin(theta)], 1)
    flip = np.zeros((PLACES, MODES))
    flip[((-kh) % SIDE) * SIDE + (-kw) % SIDE, np.arange(MODES)] = 1.0
    spec = np.zeros((2 * MODES, SIDE, HALF_COLS), complex)
    spec[np.arange(MODES), kh, kw] = 1.0
    spec[MODES + np.arange(MODES), kh, kw] = 1j
    inverse = np.fft.irfft2(spec, s=(SIDE, SIDE), norm="ortho").reshape(2, 2, MCHUNK, PLACES)
    phi = 2 * np.pi * np.outer(np.arange(CH), np.arange(CH)) / CH
    c, s = np.cos(phi), np.sin(phi)
    chan = np.stack([c - s, c + s], 1).reshape(2, HALF, 2, CH)
    chan_back = np.concatenate([c, -s], 1).reshape(2, HALF, 2 * CH)
    made = {
        "space_fwd": space.reshape(2, 128, 2 * MODES).transpose(1, 0, 2),
        "flip": flip.reshape(2, 128, MODES).transpose(1, 0, 2),
        "inverse": inverse.transpose(2, 0, 1, 3),
        "space_back": back.transpose(2, 1, 0).reshape(2, MCHUNK, 2, PLACES).transpose(1, 0, 2, 3),
        "chan_fwd": chan.transpose(1, 0, 2, 3),
        "chan_back": chan_back.transpose(1, 0, 2),
        "ident": np.eye(128),
        "key_rows": _key_rows(),
        "query_codes": _query_codes(),
    }
    return {k: np.ascontiguousarray(v, np.float32) for k, v in made.items()}


PROJ = []
for _g in range(2):
    PROJ += [("q", _g, 0, "act"), ("q", _g, 1, "act"), ("k", _g, 0, "dve"), ("k", _g, 1, "dve"),
             ("rel_h", _g, 0, "act"), ("rel_h", _g, 1, "act"), ("rel_w", _g, 0, "dve"), ("rel_w", _g, 1, "dve")]
PROJ += [("v", 0, 0, "act"), ("v", 1, 0, "dve"), ("v", 2, 0, "act"), ("v", 3, 0, "dve"), ("v", 4, 0, "dve")]


def taken_out(j):
    who = PROJ[j][3]
    return who, sum(p[3] == who for p in PROJ[:j + 1])


def job(kind, group, part):
    return [p[:3] for p in PROJ].index((kind, group, part))


UNITS = [(b, h) for b in range(IMAGES) for h in range(HEADS)]
UNITS += [(IMAGES + s, h) for h in range(HEADS) for s in range(2)]
N_UNITS = len(UNITS)
LAST = [HEADS * (b + 1) - 1 for b in range(IMAGES)] + [N_UNITS - 1]
RING = 3


def o_set(u):
    return min(UNITS[u][0], IMAGES)


class Named:
    pass


def build(nc, t, out):
    ctx = ExitStack()
    with ctx:
        def sb(name, shape):
            return ctx.enter_context(nc.sbuf_tensor(name, shape, F32))

        def sem(name):
            return ctx.enter_context(nc.semaphore(name))

        m = Named()
        m.bank = [ctx.enter_context(nc.psum_tensor(f"bank{i}", [128, 512], F32)) for i in range(8)]
        m.qaug = sb("qaug", [128, PAIRS, TOKENS])
        m.kaug = sb("kaug", [128, PAIRS, KEYS])
        m.x = sb("x_tok", [128, IMAGES, 2, CH])
        m.xb = sb("x_plus_bias", [128, IMAGES, 2, CH])
        m.yT = sb("yT", [HALF, 2, TOKENS])
        m.norm_o = sb("norm_or_o", [128, 2 * TOKENS])
        m.xn = m.norm_o[:, 0:TILES * CH].rearrange("p (i c) -> p i c", c=CH)
        m.qW = m.norm_o[0:HALF, :].rearrange("p (a n) -> p a n", a=2)
        m.o = m.norm_o[:, 0:(IMAGES + 1) * 2 * CH].rearrange("p (s t c) -> p s t c", t=2, c=CH)
        m.probs = sb("probs", [128, RING, 4 * HALF_WIN])
        m.probsT = sb("probsT", [128, RING, 4 * HALF_WIN])
        m.v = sb("v_ones", [128, 2 * IMAGES + 2, HEADS, HD + 1])
        m.stats = sb("stats", [128, TILES, 6])
        m.meanvar = sb("meanvar", [128, TILES, 2])
        m.var, m.std, m.rstd = (sb(n, [128, TILES]) for n in ("var_eps", "std", "rstd"))
        m.negmax = sb("negmax", [128, RING, 2])
        m.edge_sum = sb("edge_sum", [128, 2, HEADS])
        m.recip = sb("recip", [128, 2, HEADS])
        m.qb4 = sb("qb4", [HALF, 2, 2])
        m.o1 = sb("o1", [HALF + 1, 2, 2, IMAGES * MODES])
        m.yW = m.o1[0:HALF].rearrange("p a b n -> p (a b n)")[:, 0:2 * TOKENS].rearrange("p (a n) -> p a n", a=2)
        arena = sb("arena", [128, 8960])

        def carve(base, at, rows, *dims):
            n = int(np.prod(dims))
            view = base[0:rows, at:at + n]
            names = "abcde"[:len(dims)]
            if len(dims) > 1:
                view = view.rearrange(f"p ({' '.join(names)}) -> p {' '.join(names)}",
                                      **{k: d for k, d in zip(names, dims)})
            return view, at + n

        m.qT, at = carve(arena, 0, HALF, 2, TOKENS)
        m.kT, at = carve(arena, at, HALF, 2, KEYS)
        m.relhT, at = carve(arena, at, GROUP * WIN, 2, TOKENS)
        m.relwT, at = carve(arena, at, GROUP * WIN, 2, TOKENS)
        m.oT, _ = carve(arena, 0, HALF, 2, TOKENS)
        m.hidT, _ = carve(arena, 2 * TOKENS, 128, HID_TILES, TOKENS)
        m.xf, at = carve(arena, 0, HALF, 2, 2, IMAGES * MODES)
        m.o2, at = carve(arena, at, MCHUNK, 2, 2, IMAGES, CH)
        m.clip1, at = carve(arena, at, MCHUNK, 2, 2 * CH)
        m.mix, at = carve(arena, 0, 128, 4, 2, CH)
        m.ef, at = carve(arena, at, 128, 2, 2, CH)
        m.hpart, at = carve(arena, at, 128, 2, 2 * CH)
        m.z, at = carve(arena, at, HALF, 2, 2, IMAGES, MODES)
        m.an, at = carve(arena, at, HALF, 2, IMAGES * MODES)
        m.ak, at = carve(arena, at, HALF, 2, IMAGES * MODES)
        kflat = m.kaug[:, :, :].rearrange("p a b -> p (a b)")
        m.o2k, at = carve(kflat, 0, HALF, 2, IMAGES * MODES)
        m.s, at = carve(kflat, at, HALF, 2, IMAGES * MODES)
        m.clip3, at = carve(kflat, at, HALF, 2, IMAGES * MODES)
        m.hs, at = carve(kflat, at, HALF, 2, 4, MODES)
        m.hef, at = carve(kflat, at, HALF, 2, 2, MODES)
        m.gb, at = carve(kflat, at, MCHUNK, 2, 2, IMAGES, CH)

        c = {name: sb(name, list(t[name].shape))
             for name in ("space_fwd", "flip", "inverse", "space_back", "chan_fwd", "chan_back", "ident")}
        w = [{}, {}]
        ATT = ("vecs", "qkv", "rel", "fc1b", "rows", "proj", "fc1", "fc2")
        for l in range(2):
            for name in ATT:
                shared = l == 1 and name in ("fc1", "fc2")
                w[l][name] = w[0][name] if shared else sb(f"{name}{l}", list(t[f"{name}{l}"].shape))
        f1, f3 = Named(), Named()
        f1.w1 = sb("f1_w1", [HALF, 3, 2, HALF])
        f1.b1 = sb("f1_b1", [HALF, 2, 2])
        f1.w2 = sb("f1_w2", [HALF + 1, 3, 2, HALF])
        f3.w = sb("f3_w", [HALF, 2, 2, 2 * HALF])
        f3.mixw = sb("f3_mixw", [HALF, 2, 2, 2 * HALF])
        f3.b = sb("f3_b", [HALF, 2, 2, 2])

        x_loaded = [sem(f"x_loaded{b}") for b in range(IMAGES)]
        ident_loaded = sem("ident_loaded")
        aug_rows_loaded = sem("aug_rows_loaded")
        spectral_loaded = sem("spectral_loaded")
        ones_set = sem("ones_set")
        o1_ones_set = sem("o1_ones_set")
        weights_mixed = sem("weights_mixed")
        stored = sem("stored")

        def stage(name, takers="act dve"):
            s = Named()
            s.pe = sem(f"{name}_pe")
            s.act = sem(f"{name}_act") if "act" in takers else None
            s.dve = sem(f"{name}_dve") if "dve" in takers else None
            return s

        def attention_sems(l):
            s = Named()
            s.loaded = {n: sem(f"{n}{l}_loaded") for n in ("vecs", "qkv", "rel", "late")}
            s.proj_in, s.out_proj = stage(f"proj_in{l}"), stage(f"out_proj{l}", "dve")
            s.fc1, s.fc2 = stage(f"fc1{l}", "act"), stage(f"fc2{l}", "dve")
            s.ln = []
            for k in range(2):
                n = stage(f"ln{l}_{k}")
                n.stats, n.mean, n.var, n.std, n.rstd, n.done = (sem(f"ln{l}_{k}_{q}") for q in ("stats", "mean", "var", "std", "rstd", "done"))
                s.ln.append(n)
            s.qb_scaled, s.kpad_set, s.bias_added = sem(f"qb_scaled{l}"), sem(f"kpad_set{l}"), sem(f"bias_added{l}")
            s.q_ordered, s.y_ordered = sem(f"q_ordered{l}"), sem(f"y_ordered{l}")
            s.aug = [sem(f"aug{l}_{p}") for p in range(PAIRS)]
            s.scores, s.max, s.probs = sem(f"scores{l}"), sem(f"max{l}"), sem(f"probs{l}")
            s.turned, s.turned_out, s.pv = sem(f"turned{l}"), sem(f"turned_out{l}"), sem(f"pv{l}")
            s.recip, s.o_norm = sem(f"recip{l}"), sem(f"o_norm{l}")
            s.o_turned, s.oT_out = sem(f"o_turned{l}"), sem(f"oT_out{l}")
            return s

        A = [attention_sems(0), attention_sems(1)]
        S1 = Named()
        S1.fwd, S1.mlp1 = stage("s1_fwd"), stage("s1_mlp1")
        S1.mlp2, S1.inv = stage("s1_mlp2", "dve"), stage("s1_inv", "dve")
        S1.clipped = sem("s1_clipped")
        S3 = Named()
        S3.fwd, S3.flip, S3.chan, S3.mlp1 = stage("s3_fwd"), stage("s3_flip"), stage("s3_chan"), stage("s3_mlp1")
        S3.o2k, S3.o2nk = stage("s3_o2k", "act"), stage("s3_o2nk", "dve")
        S3.back, S3.inv = stage("s3_back"), stage("s3_inv", "dve")
        S3.mixed, S3.ef, S3.s, S3.clipped = sem("s3_mixed"), sem("s3_ef"), sem("s3_s"), sem("s3_clipped")
        S3.shrunk, S3.hef, S3.hs = sem("s3_shrunk"), sem("s3_hef"), sem("s3_hs")

        def raster(ap):
            return ap.rearrange("k (b r w) -> k b r w", b=IMAGES, r=SIDE)

        def main(ap):
            return ap[:, 0:MAIN].rearrange("k (b r w) -> k b r w", b=IMAGES, r=WIN)

        def right(ap):
            return ap[:, MAIN:MAIN + RIGHT].rearrange("k (b r w) -> k b r w", b=IMAGES, r=WIN)

        def low(ap):
            return ap[:, MAIN + RIGHT:TOKENS].rearrange("k (b r w) -> k b r w", b=IMAGES, r=EDGE)

        def to_window_order(copy, dst, src, lo, hi):
            top = min(hi, WIN)
            copy(main(dst)[:, :, lo:top], src[:, :, 0:top - lo, 0:WIN])
            last = copy(right(dst)[:, :, lo:top], src[:, :, 0:top - lo, WIN:SIDE])
            return copy(low(dst), src[:, :, top - lo:hi - lo, :]) if hi > WIN else last

        def window(ap, s):
            return raster(ap)[:, :, 0:WIN, WIN:SIDE] if s == 0 else raster(ap)[:, :, WIN:SIDE, :]

        EDGE_TOKENS = (RIGHT, LOW)
        EDGE_AT = (MAIN, MAIN + RIGHT)
        EDGE_PADS = ((TOKENS, PAD_RIGHT), (TOKENS + PAD_RIGHT, PAD_LOW))

        def wait_for(eng, st, who, n):
            eng.wait_ge(st.act if who == "act" else st.dve, n)

        block = ctx.enter_context(nc.Block())

        @block.sync
        def _(sp):
            x_dram = t["x"].rearrange("b h w c -> b (h w) c").rearrange("b (t p) c -> b p t c", p=128)
            for b in range(IMAGES):
                sp.dma_start(m.x[:, b], x_dram[b]).then_inc(x_loaded[b], 16)
            sp.dma_start(c["ident"][:, :], t["ident"]).then_inc(ident_loaded, 16)

            def load(l, name, s):
                sp.dma_start(w[l][name][:], t[f"{name}{l}"]).then_inc(s, 16)

            def load_attention(l):
                load(l, "vecs", A[l].loaded["vecs"])
                load(l, "qkv", A[l].loaded["qkv"])
                load(l, "rel", A[l].loaded["rel"])

            load_attention(0)
            for a in range(2):
                sp.dma_start(m.kaug[64 * a + HD:64 * a + AUG], t["key_rows"].unsqueeze(1).broadcast_to([AUG - HD, PAIRS, KEYS]))\
                  .then_inc(aug_rows_loaded, 16)
                sp.dma_start(m.qaug[64 * a + AUG - CODES:64 * a + AUG], t["query_codes"].unsqueeze(1).broadcast_to([CODES, PAIRS, TOKENS]))\
                  .then_inc(aug_rows_loaded, 16)
            for name in ("rows", "fc1b", "proj", "fc1", "fc2"):
                load(0, name, A[0].loaded["late"])
            sp.dma_start(f1.w1[:, 0:2], t["f1_w1"]).then_inc(spectral_loaded, 16)
            sp.dma_start(f1.w2[:, 0:2], t["f1_w2"]).then_inc(spectral_loaded, 16)
            sp.dma_start(f1.b1[:], t["f1_b1"]).then_inc(spectral_loaded, 16)
            sp.dma_start(f3.w[:], t["f3_w"]).then_inc(spectral_loaded, 16)
            sp.dma_start(f3.b[:], t["f3_b"]).then_inc(spectral_loaded, 16)
            for name in ("space_fwd", "flip", "inverse", "space_back", "chan_fwd", "chan_back"):
                sp.dma_start(c[name][:], t[name]).then_inc(spectral_loaded, 16)
            load_attention(1)
            for name in ("rows", "fc1b", "proj"):
                load(1, name, A[1].loaded["late"])

            for l in range(2):
                s = A[l]
                if l == 1:
                    sp.wait_ge(A[0].fc1.pe, 2 * HID_TILES)
                    load(1, "fc1", s.loaded["late"])
                    sp.wait_ge(A[0].fc2.pe, IMAGES)
                    load(1, "fc2", s.loaded["late"])
                for g in range(2):
                    for kind, src, rows, off, dst in (("q", m.qW, HD, 0, m.qaug), ("k", m.kT, HD, 0, m.kaug),
                                                      ("rel_h", m.relhT, WIN, HD, m.qaug), ("rel_w", m.relwT, WIN, HD + WIN, m.qaug)):
                        if kind == "q":
                            sp.wait_ge(s.q_ordered, g + 1)
                        else:
                            wait_for(sp, s.proj_in, *taken_out(job(kind, g, 1)))
                        if kind == "k":
                            sp.wait_ge(s.kpad_set, g + 1)
                        for n in range(GROUP):
                            head = GROUP * g + n
                            lo = 64 * (head % 2) + off
                            part = src[n:GROUP * WIN:GROUP, g] if kind.startswith("rel") else src[rows * n:rows * (n + 1), g]
                            sp.dma_start(dst[lo:lo + rows, head // 2, 0:part.shape[-1]], part)\
                              .then_inc(s.aug[head // 2], 16)
            out_dram = out.rearrange("b h w c -> b (h w) c").rearrange("b (t p) c -> b p t c", p=128)
            for b in range(IMAGES):
                sp.wait_ge(S3.inv.dve, b + 1)
                sp.dma_start(out_dram[b], m.xb[:, b]).then_inc(stored, 16)
            sp.wait_ge(stored, 16 * IMAGES)

        AUG_LANDED = 16 * 8

        @block.gpsimd
        def _(pool):
            pool.memset(m.v[:], 1.0).then_inc(ones_set, 1)

            def attention(l, x_ready):
                s = A[l]
                pool.wait_ge(s.loaded["vecs"], 16)
                for g in range(2):
                    if l == 1 and g == 0:
                        pool.wait_ge(S1.inv.pe, IMAGES)
                        pool.wait_ge(S1.inv.dve, IMAGES)
                    pool.tensor_copy(m.kT[:, g, TOKENS:KEYS], w[l]["vecs"][:, 6 + g:7 + g].broadcast_to([HALF, KEYS - TOKENS]))\
                        .then_inc(s.kpad_set, 1)
                pool.wait_ge(s.ln[0].act, 2)
                pool.wait_ge(s.ln[0].dve, 2)
                for half in range(2):
                    to_window_order(pool.tensor_copy, m.yW[:, half], raster(m.yT[:, half]), 0, SIDE).then_inc(s.y_ordered, 1)
                for g in range(2):
                    wait_for(pool, s.proj_in, *taken_out(job("q", g, 1)))
                    to_window_order(pool.tensor_copy, m.qW[:, g], raster(m.qT[:, g]), 0, SIDE).then_inc(s.q_ordered, 1)
                pool.wait_ge(s.loaded["late"], 16 * 5)
                for b in range(IMAGES):
                    x_ready(pool, b)
                    pool.tensor_tensor(m.xb[:, b], m.x[:, b], w[l]["rows"][:, 0:1].broadcast_to([128, 2, CH]), ALU.add)\
                        .then_inc(s.bias_added, 1)
                for b in range(IMAGES):
                    pool.wait_ge(s.out_proj.dve, b + 1)
                    pool.tensor_tensor(m.xb[:, b], m.x[:, b], w[l]["rows"][:, 1:2].broadcast_to([128, 2, CH]), ALU.add)\
                        .then_inc(s.bias_added, 1)

            attention(0, lambda eng, b: eng.wait_ge(x_loaded[b], 16))
            pool.wait_ge(spectral_loaded, 16 * 11)
            pool.tensor_scalar(f1.w1[:, 2], f1.w1[:, 1], -1.0, None, ALU.mult).then_inc(weights_mixed, 1)
            pool.tensor_scalar(f1.w2[0:HALF, 2], f1.w2[0:HALF, 1], -1.0, None, ALU.mult).then_inc(weights_mixed, 1)
            pool.tensor_tensor(f3.mixw[:, :, 0], f3.w[:, :, 0], f3.w[:, :, 1], ALU.add).then_inc(weights_mixed, 1)
            pool.tensor_tensor(f3.mixw[:, :, 1], f3.w[:, :, 0], f3.w[:, :, 1], ALU.subtract).then_inc(weights_mixed, 1)
            pool.wait_ge(weights_mixed, 4)
            pool.tensor_scalar(f3.mixw[:], f3.mixw[:], 0.5, None, ALU.mult).then_inc(weights_mixed, 1)
            attention(1, lambda eng, b: eng.wait_ge(S1.inv.dve, b + 1))

        @block.tensor
        def _(pe):
            mm = nc.tensor.matmul

            def turn_norm(s, ln, bank0):
                for g in range(2):
                    for half in range(2):
                        pe.wait_ge(ln.done, 4 * g + 4)
                        for i in range(4):
                            last = nc.tensor.transpose(m.bank[bank0 + 2 * g + half][0:HALF, 128 * i:128 * (i + 1)],
                                                       m.xn[:, 4 * g + i, HALF * half:HALF * (half + 1)], c["ident"][:])
                        last.then_inc(ln.pe, 1)

            def attention(l):
                s, wl = A[l], w[l]
                if l == 0:
                    pe.wait_ge(ident_loaded, 16)
                turn_norm(s, s.ln[0], 0)
                pe.wait_ge(s.loaded["qkv"], 16)
                pe.wait_ge(s.loaded["rel"], 16)
                for j, (kind, g, part, _) in enumerate(PROJ):
                    if j >= 4:
                        wait_for(pe, s.proj_in, *taken_out(j - 4))
                    elif j < 2:
                        pe.wait_ge(s.ln[0].act, j + 1)
                        pe.wait_ge(s.ln[0].dve, j + 1)
                    bank = m.bank[4 + j % 4]
                    if kind in "qk":
                        col = (0 if kind == "q" else CH) + HALF * g
                        for half in range(2):
                            last = mm(bank[0:HALF, :], wl["qkv"][:, half, col:col + HALF], m.yT[:, half, 512 * part:512 * (part + 1)],
                                      start=half == 0, stop=half == 1)
                    elif kind in ("rel_h", "rel_w"):
                        wait_for(pe, s.proj_in, *taken_out(job("q", g, 1)))
                        q = raster(m.qT[:, g])[:, :, 8 * part:8 * (part + 1), :] if kind == "rel_w" else raster(m.qT[:, g])
                        for n in range(8 if kind == "rel_h" else SIDE):
                            place = (8 * part + n if kind == "rel_h" else n) % WIN
                            table = wl["rel"][:, 0 if kind == "rel_h" else 1, GROUP * (WIN - 1 - place):GROUP * (2 * WIN - 1 - place)]
                            cols = 64 if kind == "rel_h" else 32
                            last = mm(bank[0:GROUP * WIN, cols * n:cols * (n + 1)], table,
                                      q[:, :, 8 * part + n, :] if kind == "rel_h" else q[:, :, :, n], start=True, stop=True)
                    else:
                        pe.wait_ge(s.y_ordered, 2)
                        for tile in range(2):
                            n = HALF_WIN if g < IMAGES else EDGE_TOKENS[tile]
                            at = HALF_WIN * (2 * g + tile) if g < IMAGES else EDGE_AT[tile]
                            for half in range(2):
                                last = mm(bank[0:n, CH * tile:CH * (tile + 1)], m.yW[:, half, at:at + n], wl["qkv"][:, half, 2 * CH:3 * CH],
                                          start=half == 0, stop=half == 1)
                    last.then_inc(s.proj_in.pe, 1)

                if l == 0:
                    pe.wait_ge(aug_rows_loaded, 16 * 4)
                for step in range(N_UNITS + 6):
                    if step < N_UNITS:
                        b, h = UNITS[step]
                        if step >= RING:
                            pe.wait_ge(s.probs, step - RING + 1)
                        if step < HEADS and h % 2 == 0:
                            pe.wait_ge(s.aug[h // 2], AUG_LANDED)
                        r = slice(64 * (h % 2), 64 * (h % 2) + AUG)
                        q, k = m.qaug[r, h // 2, 0:TOKENS], m.kaug[r, h // 2, 0:TOKENS]
                        bank = m.bank[step % RING]
                        if b < IMAGES:
                            keys = raster(k)[:, b, 0:WIN, 0:WIN]
                            for part in range(2):
                                at = HALF_WIN * (2 * b + part)
                                last = mm(bank[0:HALF_WIN, 2 * HALF_WIN * part:2 * HALF_WIN * (part + 1)], q[:, at:at + HALF_WIN], keys,
                                          start=True, stop=True)
                        else:
                            e = b - IMAGES
                            n, (pad_at, pads) = EDGE_TOKENS[e], EDGE_PADS[e]
                            asking = q[:, EDGE_AT[e]:EDGE_AT[e] + n]
                            mm(bank[0:n, 0:n], asking, window(k, e), start=True, stop=True)
                            last = mm(bank[0:n, n:n + pads], asking, m.kaug[r, h // 2, pad_at:pad_at + pads], start=True, stop=True)
                        last.then_inc(s.scores, 1)
                    if 2 <= step < N_UNITS + 2:
                        u = step - 2
                        b, h = UNITS[u]
                        if u == 0:
                            pe.wait_ge(s.proj_in.act, taken_out(job("v", 2, 0))[1])
                            pe.wait_ge(s.proj_in.dve, taken_out(job("v", 4, 0))[1])
                            if l == 0:
                                pe.wait_ge(ones_set, 1)
                        pe.wait_ge(s.probs, u + 1)
                        if u >= RING:
                            pe.wait_ge(s.turned_out, u - RING + 1)
                        bank = m.bank[RING + u % RING]
                        if b < IMAGES:
                            for key in range(2):
                                for part in range(2):
                                    at = HALF_WIN * (2 * key + part)
                                    src = m.probs[0:HALF_WIN, u % RING, HALF_WIN * (2 * part + key):HALF_WIN * (2 * part + key + 1)]
                                    last = nc.tensor.transpose(bank[0:HALF_WIN, at:at + HALF_WIN], src, c["ident"][0:HALF_WIN, 0:HALF_WIN])
                        else:
                            n = EDGE_TOKENS[b - IMAGES]
                            last = nc.tensor.transpose(bank[0:n, 0:n], m.probs[0:n, u % RING, 0:n], c["ident"][0:n, 0:n])
                        last.then_inc(s.turned, 1)
                    if 3 <= step < N_UNITS + 3:
                        u = step - 3
                        b, h = UNITS[u]
                        pe.wait_ge(s.turned_out, u + 1)
                        group = o_set(u)
                        if group >= 2 and (u == 0 or o_set(u - 1) != group):
                            pe.wait_ge(s.oT_out, group - 1)
                        o = m.bank[6 + group % 2]
                        if b < IMAGES:
                            for part in range(2):
                                col = (HD + 1) * (HEADS * part + h)
                                for key in range(2):
                                    at = HALF_WIN * (2 * key + part)
                                    last = mm(o[0:HALF_WIN, col:col + HD + 1], m.probsT[0:HALF_WIN, u % RING, at:at + HALF_WIN],
                                              m.v[0:HALF_WIN, 2 * b + key, h], start=key == 0, stop=key == 1)
                        else:
                            e = b - IMAGES
                            n, col = EDGE_TOKENS[e], (HD + 1) * (HEADS * e + h)
                            last = mm(o[0:n, col:col + HD + 1], m.probsT[0:n, u % RING, 0:n], m.v[0:n, 2 * IMAGES + e, h],
                                      start=True, stop=True)
                        last.then_inc(s.pv, 1)
                    for group, u in enumerate(LAST):
                        if step == u + 5:
                            pe.wait_ge(s.o_norm, 2 * (group + 1))
                            bank = m.bank[6 + group % 2]
                            for half in range(2):
                                for part in range(2):
                                    n = HALF_WIN if group < IMAGES else EDGE_TOKENS[part]
                                    at = 256 * half + (HALF_WIN if group < IMAGES else RIGHT) * part
                                    last = nc.tensor.transpose(bank[0:HALF, at:at + n], m.o[0:n, group, part, HALF * half:HALF * (half + 1)],
                                                               c["ident"][0:n, 0:n])
                            last.then_inc(s.o_turned, 1)

                pe.wait_ge(s.oT_out, IMAGES + 1)
                pe.wait_ge(s.loaded["late"], 16 * 5)
                for b in range(IMAGES):
                    for tile in range(2):
                        for half in range(2):
                            at = PLACES * b + 128 * tile
                            last = mm(m.bank[b][:, CH * tile:CH * (tile + 1)], m.oT[:, half, at:at + 128], wl["proj"][:, half],
                                      start=half == 0, stop=half == 1)
                    last.then_inc(s.out_proj.pe, 1)
                turn_norm(s, s.ln[1], 4)
                for j in range(2 * HID_TILES):
                    g, hid = divmod(j, HID_TILES)
                    if hid == 0:
                        pe.wait_ge(s.ln[1].act, g + 1)
                        pe.wait_ge(s.ln[1].dve, g + 1)
                    if j < 4:
                        pe.wait_ge(s.out_proj.dve, j + 1)
                    else:
                        pe.wait_ge(s.fc1.act, j - 3)
                    for half in range(2):
                        last = mm(m.bank[j % 4][:, :], wl["fc1"][:, half, 128 * hid:128 * (hid + 1)], m.yT[:, half, 512 * g:512 * (g + 1)],
                                  start=half == 0, stop=half == 1)
                    last.then_inc(s.fc1.pe, 1)
                for b in range(IMAGES):
                    pe.wait_ge(s.fc1.act, HID_TILES * (b // 2 + 1))
                    for tile in range(2):
                        at = PLACES * b + 128 * tile
                        for hid in range(HID_TILES):
                            last = mm(m.bank[4 + b][:, CH * tile:CH * (tile + 1)], m.hidT[:, hid, at:at + 128], wl["fc2"][:, hid],
                                      start=hid == 0, stop=hid == HID_TILES - 1)
                    last.then_inc(s.fc2.pe, 1)

            def spectral1():
                pe.wait_ge(spectral_loaded, 16 * 11)
                for j in range(8):
                    b, half = divmod(j, 2)
                    pe.wait_ge(A[0].fc2.dve, b + 1)
                    if j >= 4:
                        wait_for(pe, S1.fwd, ("act", "dve")[j % 2], (j - 4) // 2 + 1)
                    for tile in range(2):
                        last = mm(m.bank[j % 4][0:HALF, 0:2 * MODES], m.x[:, b, tile, HALF * half:HALF * (half + 1)], c["space_fwd"][:, tile],
                                  start=tile == 0, stop=tile == 1)
                    last.then_inc(S1.fwd.pe, 1)
                pe.wait_ge(weights_mixed, 5)
                pe.wait_ge(o1_ones_set, 1)
                for j in range(8):
                    g, half, part = j // 4, j // 2 % 2, j % 2
                    pe.wait_ge(S1.fwd.act, 2 * g + 2)
                    pe.wait_ge(S1.fwd.dve, 2 * g + 2)
                    if j >= 4:
                        wait_for(pe, S1.mlp1, ("act", "dve")[j % 2], (j - 4) // 2 + 1)
                    cols = slice(2 * MODES * g, 2 * MODES * (g + 1))
                    o = m.bank[4 + j % 4][0:HALF, 0:2 * MODES]
                    mm(o, f1.w1[:, 0, half], m.xf[:, half, part, cols], start=True, stop=False)
                    last = mm(o, f1.w1[:, 1 if part else 2, half], m.xf[:, half, 1 - part, cols], start=False, stop=True)
                    last.then_inc(S1.mlp1.pe, 1)
                for j in range(8):
                    b, part = divmod(j, 2)
                    pe.wait_ge(S1.mlp1.act, 2 * (b // 2) + 2)
                    pe.wait_ge(S1.mlp1.dve, 2 * (b // 2) + 2)
                    if j >= 4:
                        pe.wait_ge(S1.mlp2.dve, j - 3)
                    for chunk in range(2):
                        at = MODES * b + MCHUNK * chunk
                        for half in range(2):
                            o = m.bank[j % 4][0:MCHUNK, CH * chunk + HALF * half:CH * chunk + HALF * (half + 1)]
                            mm(o, m.o1[:, half, 0, at:at + MCHUNK], f1.w2[:, part, half], start=True, stop=False)
                            last = mm(o, m.o1[0:HALF, half, 1, at:at + MCHUNK], f1.w2[0:HALF, 0 if part else 2, half], start=False, stop=True)
                    last.then_inc(S1.mlp2.pe, 1)
                for b in range(IMAGES):
                    pe.wait_ge(S1.mlp2.dve, 2 * (b + 1))
                    for tile in range(2):
                        for n in range(4):
                            last = mm(m.bank[4 + b][:, CH * tile:CH * (tile + 1)], c["inverse"][:, n // 2, n % 2, 128 * tile:128 * (tile + 1)],
                                      m.o2[:, n // 2, n % 2, b], start=n == 0, stop=n == 3)
                    last.then_inc(S1.inv.pe, 1)

            def spectral3():
                for b in range(IMAGES):
                    pe.wait_ge(A[1].fc2.dve, b + 1)
                    for half in range(2):
                        for tile in range(2):
                            last = mm(m.bank[4 + b][0:HALF, MODES * half:MODES * (half + 1)], m.x[:, b, tile, HALF * half:HALF * (half + 1)],
                                      c["flip"][:, tile], start=tile == 0, stop=tile == 1)
                    last.then_inc(S3.flip.pe, 1)
                for j in range(8):
                    mix, half = (3, 2, 0, 1)[j % 4], j // 4
                    pe.wait_ge(S3.mixed, 3)
                    if j >= 4:
                        wait_for(pe, S3.fwd, ("act", "dve", "act", "act")[j % 4], (1, 1, 2, 3)[j % 4])
                    for tile in range(2):
                        last = mm(m.bank[j % 4][0:HALF, 0:2 * MODES], m.mix[:, mix, tile, HALF * half:HALF * (half + 1)], c["space_fwd"][:, tile],
                                  start=tile == 0, stop=tile == 1)
                    last.then_inc(S3.fwd.pe, 1)
                pe.wait_ge(S3.fwd.act, 6)
                pe.wait_ge(S3.fwd.dve, 2)
                for j in range(4):
                    half, g = divmod(j, 2)
                    wait_for(pe, S3.flip, ("act", "dve")[j % 2], j // 2 + 1)
                    for n in range(4):
                        last = mm(m.bank[4 + j][0:HALF, 0:2 * MODES], c["chan_fwd"][:, n // 2, n % 2, HALF * half:HALF * (half + 1)],
                                  m.z[:, n // 2, n % 2, 2 * g:2 * g + 2], start=n == 0, stop=n == 3)
                    last.then_inc(S3.chan.pe, 1)
                for j in range(8):
                    half, g, nk = j // 4, j // 2 % 2, j % 2
                    wait_for(pe, S3.chan, ("act", "dve")[g], half + 1)
                    if j >= 4:
                        wait_for(pe, S3.mlp1, ("act", "dve")[j % 2], (j - 4) // 2 + 1)
                    cols = slice(2 * MODES * g, 2 * MODES * (g + 1))
                    o = m.bank[j % 4][0:HALF, 0:2 * MODES]
                    lo = slice(HALF * half, HALF * (half + 1))
                    mm(o, f3.mixw[:, 0, nk, lo], m.ak[:, half, cols], start=True, stop=False)
                    last = mm(o, f3.mixw[:, 0, 1 - nk, lo], m.an[:, half, cols], start=False, stop=True)
                    last.then_inc(S3.mlp1.pe, 1)
                for j in range(4):
                    half, g = divmod(j, 2)
                    pe.wait_ge(S3.mlp1.act, j + 1)
                    pe.wait_ge(S3.mlp1.dve, j + 1)
                    cols = slice(2 * MODES * g, 2 * MODES * (g + 1))
                    lo = slice(HALF * half, HALF * (half + 1))
                    o = m.bank[4 + j][0:HALF, 0:2 * MODES]
                    mm(o, f3.mixw[:, 1, 0, lo], m.o1[0:HALF, half, 0, cols], start=True, stop=False)
                    last = mm(o, f3.mixw[:, 1, 1, lo], m.o1[0:HALF, half, 1, cols], start=False, stop=True)
                    last.then_inc(S3.o2k.pe, 1)
                for j in range(4):
                    half, g = divmod(j, 2)
                    cols = slice(2 * MODES * g, 2 * MODES * (g + 1))
                    lo = slice(HALF * half, HALF * (half + 1))
                    o = m.bank[j][0:HALF, 0:2 * MODES]
                    mm(o, f3.mixw[:, 1, 0, lo], m.o1[0:HALF, half, 1, cols], start=True, stop=False)
                    pe.wait_ge(S3.o2k.act, j + 1)
                    last = mm(o, f3.mixw[:, 1, 1, lo], m.o2k[:, half, cols], start=False, stop=True)
                    last.then_inc(S3.o2nk.pe, 1)
                for j in range(8):
                    chunk, mix = j // 4, (3, 2, 0, 1)[j % 4]
                    pe.wait_ge(S3.hs, 3)
                    if j >= 4:
                        wait_for(pe, S3.back, ("act", "dve", "act", "act")[j % 4], (1, 1, 2, 3)[j % 4])
                    for half in range(2):
                        last = mm(m.bank[4 + j % 4][0:MCHUNK, 0:2 * CH], m.hs[:, half, mix, MCHUNK * chunk:MCHUNK * (chunk + 1)],
                                  c["chan_back"][:, half], start=half == 0, stop=half == 1)
                    last.then_inc(S3.back.pe, 1)
                pe.wait_ge(S3.back.act, 6)
                pe.wait_ge(S3.back.dve, 2)
                for b in range(IMAGES):
                    for tile in range(2):
                        for n in range(4):
                            last = mm(m.bank[b][:, CH * tile:CH * (tile + 1)], c["space_back"][:, n // 2, n % 2, 128 * tile:128 * (tile + 1)],
                                      m.gb[:, n % 2, n // 2, b], start=n == 0, stop=n == 3)
                    last.then_inc(S3.inv.pe, 1)

            attention(0)
            spectral1()
            attention(1)
            spectral3()

        @block.scalar
        def _(act):
            run = nc.scalar.activation

            def take_norm(wl, ln, bank0, col):
                for g in range(2):
                    act.wait_ge(ln.var, g + 1)
                    run(m.std[:, 4 * g:4 * g + 4], m.var[:, 4 * g:4 * g + 4], ACT.Sqrt).then_inc(ln.std, 1)
                for g in range(2):
                    act.wait_ge(ln.pe, 2 * g + 1)
                    run(m.yT[:, 0, 512 * g:512 * (g + 1)], m.bank[bank0 + 2 * g][0:HALF, :], ACT.Identity,
                        scale=wl["vecs"][:, col:col + 1], bias=wl["vecs"][:, col + 2:col + 3]).then_inc(ln.act, 1)

            def attention(l):
                s, wl = A[l], w[l]
                act.wait_ge(s.loaded["vecs"], 16)
                take_norm(wl, s.ln[0], 0, 0)
                act.wait_ge(s.qb_scaled, 1)
                for j, (kind, g, part, who) in enumerate(PROJ):
                    if who != "act":
                        continue
                    act.wait_ge(s.proj_in.pe, j + 1)
                    bank = m.bank[4 + j % 4]
                    if kind == "q":
                        ins = run(m.qT[:, g, 512 * part:512 * (part + 1)], bank[0:HALF, :], ACT.Identity, scale=HD ** -0.5,
                                  bias=m.qb4[:, l, g:g + 1])
                    elif kind == "rel_h":
                        ins = to_window_order(lambda dst, src: run(dst, src, ACT.Copy), m.relhT[:, g],
                                              bank[0:GROUP * WIN, :].rearrange("k (r b w) -> k b r w", r=8, b=IMAGES), 8 * part, 8 * part + 8)
                    else:
                        if l == 0 and g == 0:
                            act.wait_ge(ones_set, 1)
                        ins = run(m.v[0:HALF_WIN, 2 * g:2 * g + 2, :, 0:HD],
                                  bank[0:HALF_WIN, 0:2 * CH].rearrange("k (t h c) -> k t h c", t=2, c=HD), ACT.Copy)
                    ins.then_inc(s.proj_in.act, 1)
                for step in range(N_UNITS + 7):
                    if step < N_UNITS:
                        b, h = UNITS[step]
                        act.wait_ge(s.max, step + 1)
                        if step >= RING:
                            act.wait_ge(s.turned, step - RING + 1)
                        bank, slot = m.bank[step % RING], step % RING
                        if b < IMAGES:
                            for part in range(2):
                                cols = slice(2 * HALF_WIN * part, 2 * HALF_WIN * (part + 1))
                                ins = run(m.probs[0:HALF_WIN, slot, cols], bank[0:HALF_WIN, cols], ACT.Exp,
                                          bias=m.negmax[0:HALF_WIN, slot, part:part + 1])
                        else:
                            e = b - IMAGES
                            n, keys = EDGE_TOKENS[e], EDGE_TOKENS[e] + EDGE_PADS[e][1]
                            ins = run(m.probs[0:n, slot, 0:keys], bank[0:n, 0:keys], ACT.Exp, bias=m.negmax[0:n, slot, 0:1],
                                      accum_out=m.edge_sum[0:n, e, h:h + 1])
                        ins.then_inc(s.probs, 1)
                    for group, u in enumerate(LAST):
                        if step == u + 6:
                            act.wait_ge(s.o_turned, group + 1)
                            bank = m.bank[6 + group % 2]
                            for half in range(2):
                                bias = wl["vecs"][:, 8 + half:9 + half]
                                o = m.oT[:, half]
                                if group < IMAGES:
                                    ins = run(raster(o)[:, group, 0:WIN, 0:WIN],
                                              bank[0:HALF, 256 * half:256 * half + 2 * HALF_WIN].rearrange("k (r w) -> k r w", r=WIN),
                                              ACT.Identity, bias=bias)
                                else:
                                    run(window(o, 0), bank[0:HALF, 256 * half:256 * half + RIGHT].rearrange("k (b r w) -> k b r w", b=IMAGES, r=WIN),
                                        ACT.Identity, bias=bias)
                                    ins = run(window(o, 1), bank[0:HALF, 256 * half + RIGHT:256 * half + RIGHT + LOW]
                                              .rearrange("k (b r w) -> k b r w", b=IMAGES, r=EDGE), ACT.Identity, bias=bias)
                            ins.then_inc(s.oT_out, 1)
                take_norm(wl, s.ln[1], 4, 10)
                for j in range(2 * HID_TILES):
                    g, hid = divmod(j, HID_TILES)
                    act.wait_ge(s.fc1.pe, j + 1)
                    run(m.hidT[:, hid, 512 * g:512 * (g + 1)], m.bank[j % 4][:, :], ACT.Gelu, bias=wl["fc1b"][:, hid:hid + 1])\
                        .then_inc(s.fc1.act, 1)

            def spectral1():
                for j in range(0, 8, 2):
                    b, half = divmod(j, 2)
                    act.wait_ge(S1.fwd.pe, j + 1)
                    run(m.xf[:, half, :, MODES * b:MODES * (b + 1)], m.bank[j % 4][0:HALF, 0:2 * MODES].rearrange("k (a n) -> k a n", a=2),
                        ACT.Copy, scale=1.0 / SIDE).then_inc(S1.fwd.act, 1)
                for j in range(0, 8, 2):
                    g, half = j // 4, j // 2 % 2
                    act.wait_ge(S1.mlp1.pe, j + 1)
                    run(m.o1[0:HALF, half, 0, 2 * MODES * g:2 * MODES * (g + 1)], m.bank[4 + j % 4][0:HALF, 0:2 * MODES], ACT.Relu,
                        bias=f1.b1[:, 0, half:half + 1]).then_inc(S1.mlp1.act, 1)

            def spectral3():
                for b in range(0, IMAGES, 2):
                    act.wait_ge(S3.flip.pe, b + 1)
                    run(m.an[:, :, MODES * b:MODES * (b + 1)], m.bank[4 + b][0:HALF, 0:2 * MODES].rearrange("k (a n) -> k a n", a=2), ACT.Copy)\
                        .then_inc(S3.flip.act, 1)
                for j in range(8):
                    mix, half = (3, 2, 0, 1)[j % 4], j // 4
                    if mix == 2:
                        continue
                    act.wait_ge(S3.fwd.pe, j + 1)
                    if mix == 3:
                        dst = m.hpart[0:HALF, half, 0:2 * MODES]
                        run(dst, m.bank[j % 4][0:HALF, 0:2 * MODES], ACT.Copy).then_inc(S3.fwd.act, 1)
                    else:
                        run(m.z[:, half, :, 2 * mix], m.bank[j % 4][0:HALF, 0:2 * MODES].rearrange("k (a n) -> k a n", a=2), ACT.Copy)\
                            .then_inc(S3.fwd.act, 1)
                for j in (0, 2):
                    act.wait_ge(S3.chan.pe, j + 1)
                    run(m.ak[:, j // 2, 0:2 * MODES], m.bank[4 + j][0:HALF, 0:2 * MODES], ACT.Copy).then_inc(S3.chan.act, 1)
                for j in range(0, 8, 2):
                    half, g = j // 4, j // 2 % 2
                    act.wait_ge(S3.mlp1.pe, j + 1)
                    run(m.o1[0:HALF, half, 0, 2 * MODES * g:2 * MODES * (g + 1)], m.bank[j % 4][0:HALF, 0:2 * MODES], ACT.Relu,
                        bias=f3.b[:, 0, 0, half:half + 1]).then_inc(S3.mlp1.act, 1)
                for j in range(4):
                    half, g = divmod(j, 2)
                    act.wait_ge(S3.o2k.pe, j + 1)
                    run(m.o2k[:, half, 2 * MODES * g:2 * MODES * (g + 1)], m.bank[4 + j][0:HALF, 0:2 * MODES], ACT.Identity,
                        bias=f3.b[:, 1, 0, half:half + 1]).then_inc(S3.o2k.act, 1)
                for j in range(8):
                    chunk, mix = j // 4, (3, 2, 0, 1)[j % 4]
                    if mix == 2:
                        continue
                    act.wait_ge(S3.back.pe, j + 1)
                    bank = m.bank[4 + j % 4][0:MCHUNK, 0:2 * CH]
                    if mix == 3:
                        run(m.hpart[0:MCHUNK, chunk, :], bank, ACT.Copy).then_inc(S3.back.act, 1)
                    else:
                        run(m.gb[:, :, chunk, 2 * mix], bank.rearrange("k (a n) -> k a n", a=2), ACT.Copy).then_inc(S3.back.act, 1)

            attention(0)
            spectral1()
            attention(1)
            spectral3()

        @block.vector
        def _(dve):
            def normalise(ln, x_ready, eps):
                for g in range(2):
                    for b in (2 * g, 2 * g + 1):
                        x_ready(b)
                        for tile in range(2):
                            dve.bn_stats(m.stats[:, 2 * b + tile], m.x[:, b, tile]).then_inc(ln.stats, 1)
                    dve.wait_ge(ln.stats, 4 * g + 4)
                    for i in range(4 * g, 4 * g + 4):
                        dve.bn_aggr(m.meanvar[:, i], m.stats[:, i]).then_inc(ln.mean, 1)
                    dve.wait_ge(ln.mean, 4 * g + 4)
                    dve.tensor_scalar(m.var[:, 4 * g:4 * g + 4], m.meanvar[:, 4 * g:4 * g + 4, 1], eps, None, ALU.add).then_inc(ln.var, 1)
                    dve.wait_ge(ln.std, g + 1)
                    dve.reciprocal(m.rstd[:, 4 * g:4 * g + 4], m.std[:, 4 * g:4 * g + 4]).then_inc(ln.rstd, 1)
                    dve.wait_ge(ln.rstd, g + 1)
                    for i in range(4 * g, 4 * g + 4):
                        dve.tensor_scalar(m.xn[:, i], m.x[:, i // 2, i % 2], m.meanvar[:, i, 0:1], m.rstd[:, i:i + 1],
                                          ALU.subtract, ALU.mult).then_inc(ln.done, 1)

            def take_norm(wl, ln, bank0, col):
                for g in range(2):
                    dve.wait_ge(ln.pe, 2 * g + 2)
                    dve.tensor_scalar(m.yT[:, 1, 512 * g:512 * (g + 1)], m.bank[bank0 + 2 * g + 1][0:HALF, :],
                                      wl["vecs"][:, col + 1:col + 2], wl["vecs"][:, col + 3:col + 4], ALU.mult, ALU.add).then_inc(ln.dve, 1)

            def attention(l, x_ready):
                s, wl = A[l], w[l]
                normalise(s.ln[0], x_ready, EPS[l])
                dve.wait_ge(s.loaded["vecs"], 16)
                dve.tensor_scalar(m.qb4[:, l], wl["vecs"][:, 4:6], HD ** -0.5, None, ALU.mult).then_inc(s.qb_scaled, 1)
                take_norm(wl, s.ln[0], 0, 0)
                for j, (kind, g, part, who) in enumerate(PROJ):
                    if who != "dve":
                        continue
                    dve.wait_ge(s.proj_in.pe, j + 1)
                    bank = m.bank[4 + j % 4]
                    if kind == "k":
                        ins = dve.tensor_scalar(m.kT[:, g, 512 * part:512 * (part + 1)], bank[0:HALF, :], wl["vecs"][:, 6 + g:7 + g], None, ALU.add)
                    elif kind == "rel_w":
                        ins = to_window_order(dve.tensor_copy, m.relwT[:, g],
                                              bank[0:GROUP * WIN, :].rearrange("k (w b r) -> k b r w", w=SIDE, b=IMAGES), 8 * part, 8 * part + 8)
                    elif g < IMAGES:
                        if l == 0 and g == 1:
                            dve.wait_ge(ones_set, 1)
                        ins = dve.tensor_copy(m.v[0:HALF_WIN, 2 * g:2 * g + 2, :, 0:HD],
                                              bank[0:HALF_WIN, 0:2 * CH].rearrange("k (t h c) -> k t h c", t=2, c=HD))
                    else:
                        for e in range(2):
                            n = EDGE_TOKENS[e]
                            ins = dve.tensor_copy(m.v[0:n, 2 * IMAGES + e, :, 0:HD],
                                                  bank[0:n, CH * e:CH * (e + 1)].rearrange("k (h c) -> k h c", c=HD))
                    ins.then_inc(s.proj_in.dve, 1)
                for step in range(N_UNITS + 5):
                    if step < N_UNITS:
                        b, h = UNITS[step]
                        dve.wait_ge(s.scores, step + 1)
                        bank, slot = m.bank[step % RING], step % RING
                        if b < IMAGES:
                            ins = dve.tensor_reduce(m.negmax[0:HALF_WIN, slot], bank[0:HALF_WIN, 0:4 * HALF_WIN].rearrange("k (a n) -> k a n", a=2),
                                                    AX, ALU.max, negate=True)
                        else:
                            n, keys = EDGE_TOKENS[b - IMAGES], EDGE_TOKENS[b - IMAGES] + EDGE_PADS[b - IMAGES][1]
                            ins = dve.tensor_reduce(m.negmax[0:n, slot, 0:1], bank[0:n, 0:keys], AX, ALU.max, negate=True)
                        ins.then_inc(s.max, 1)
                    if 2 <= step < N_UNITS + 2:
                        u = step - 2
                        b, h = UNITS[u]
                        dve.wait_ge(s.turned, u + 1)
                        if u >= RING:
                            dve.wait_ge(s.pv, u - RING + 1)
                        n, cols = (HALF_WIN, 4 * HALF_WIN) if b < IMAGES else (EDGE_TOKENS[b - IMAGES],) * 2
                        dve.tensor_copy(m.probsT[0:n, u % RING, 0:cols], m.bank[RING + u % RING][0:n, 0:cols]).then_inc(s.turned_out, 1)
                    for group, u in enumerate(LAST):
                        if step == u + 4:
                            dve.wait_ge(s.pv, u + 1)
                            bank = m.bank[6 + group % 2][:, 0:2 * HEADS * (HD + 1)].rearrange("k (t h c) -> k t h c", t=2, c=HD + 1)
                            if group < IMAGES:
                                dve.reciprocal(m.recip[0:HALF_WIN], bank[0:HALF_WIN, :, :, HD]).then_inc(s.recip, 1)
                            else:
                                for e in range(2):
                                    ins = dve.reciprocal(m.recip[0:EDGE_TOKENS[e], e], m.edge_sum[0:EDGE_TOKENS[e], e])
                                ins.then_inc(s.recip, 1)
                            dve.wait_ge(s.recip, group + 1)
                            for part in range(2):
                                n = HALF_WIN if group < IMAGES else EDGE_TOKENS[part]
                                dve.tensor_tensor(m.o[0:n, group, part].rearrange("k (h c) -> k h c", c=HD), bank[0:n, part, :, 0:HD],
                                                  m.recip[0:n, part].unsqueeze(2).broadcast_to([n, HEADS, HD]), ALU.mult)\
                                   .then_inc(s.o_norm, 1)
                for b in range(IMAGES):
                    dve.wait_ge(s.out_proj.pe, b + 1)
                    dve.wait_ge(s.bias_added, b + 1)
                    dve.tensor_tensor(m.x[:, b], m.bank[b][:, 0:2 * CH].rearrange("k (t c) -> k t c", t=2), m.xb[:, b], ALU.add)\
                       .then_inc(s.out_proj.dve, 1)
                normalise(s.ln[1], lambda b: dve.wait_ge(s.out_proj.dve, b + 1), EPS[l])
                take_norm(wl, s.ln[1], 4, 10)
                for b in range(IMAGES):
                    dve.wait_ge(s.fc2.pe, b + 1)
                    dve.wait_ge(s.bias_added, IMAGES + b + 1)
                    dve.tensor_tensor(m.x[:, b], m.bank[4 + b][:, 0:2 * CH].rearrange("k (t c) -> k t c", t=2), m.xb[:, b], ALU.add)\
                       .then_inc(s.fc2.dve, 1)

            def spectral1():
                for j in range(1, 8, 2):
                    b, half = divmod(j, 2)
                    dve.wait_ge(S1.fwd.pe, j + 1)
                    dve.tensor_scalar(m.xf[:, half, :, MODES * b:MODES * (b + 1)],
                                      m.bank[j % 4][0:HALF, 0:2 * MODES].rearrange("k (a n) -> k a n", a=2),
                                      1.0 / SIDE, None, ALU.mult).then_inc(S1.fwd.dve, 1)
                for j in range(1, 8, 2):
                    g, half = j // 4, j // 2 % 2
                    dve.wait_ge(S1.mlp1.pe, j + 1)
                    dve.tensor_scalar(m.o1[0:HALF, half, 1, 2 * MODES * g:2 * MODES * (g + 1)], m.bank[4 + j % 4][0:HALF, 0:2 * MODES],
                                      f1.b1[:, 1, half:half + 1], 0.0, ALU.add, ALU.max).then_inc(S1.mlp1.dve, 1)
                for j in range(8):
                    b, part = divmod(j, 2)
                    dve.wait_ge(S1.mlp2.pe, j + 1)
                    bank = m.bank[j % 4][0:MCHUNK, 0:2 * CH]
                    dve.tensor_scalar(m.clip1[:, j % 2], bank, -LAMBDA, LAMBDA, ALU.max, ALU.min).then_inc(S1.clipped, 1)
                    dve.wait_ge(S1.clipped, j + 1)
                    dve.tensor_tensor(m.o2[:, part, :, b], bank.rearrange("k (a n) -> k a n", a=2),
                                      m.clip1[:, j % 2].rearrange("k (a n) -> k a n", a=2), ALU.subtract).then_inc(S1.mlp2.dve, 1)
                for b in range(IMAGES):
                    dve.wait_ge(S1.inv.pe, b + 1)
                    dve.tensor_tensor(m.x[:, b], m.bank[4 + b][:, 0:2 * CH].rearrange("k (t c) -> k t c", t=2), m.x[:, b], ALU.add)\
                       .then_inc(S1.inv.dve, 1)

            def unmix(dst, g, h, stage_sem):
                dve.tensor_tensor(dst(0, 1), g[0], h[1], ALU.add)
                dve.tensor_tensor(dst(1, 1), g[1], h[0], ALU.subtract)
                dve.tensor_tensor(dst(0, 3), g[0], h[1], ALU.subtract)
                dve.tensor_tensor(dst(1, 3), g[1], h[0], ALU.add).then_inc(stage_sem, 1)

            def spectral3():
                dve.wait_ge(A[1].fc2.dve, IMAGES)
                dve.tensor_tensor(m.mix[:, 2:4], m.x[:, 0:2], m.x[:, 2:4], ALU.subtract).then_inc(S3.mixed, 1)
                dve.tensor_tensor(m.ef[:], m.x[:, 0:2], m.x[:, 2:4], ALU.add).then_inc(S3.ef, 1)
                dve.wait_ge(S3.ef, 1)
                dve.tensor_tensor(m.mix[:, 0], m.ef[:, 0], m.ef[:, 1], ALU.add).then_inc(S3.mixed, 1)
                dve.tensor_tensor(m.mix[:, 1], m.ef[:, 0], m.ef[:, 1], ALU.subtract).then_inc(S3.mixed, 1)
                for b in range(1, IMAGES, 2):
                    dve.wait_ge(S3.flip.pe, b + 1)
                    dve.tensor_copy(m.an[:, :, MODES * b:MODES * (b + 1)], m.bank[4 + b][0:HALF, 0:2 * MODES].rearrange("k (a n) -> k a n", a=2))\
                       .then_inc(S3.flip.dve, 1)
                for half in range(2):
                    dve.wait_ge(S3.fwd.pe, 4 * half + 2)
                    dve.wait_ge(S3.fwd.act, 3 * half + 1)
                    g = m.bank[1][0:HALF, 0:2 * MODES].rearrange("k (a n) -> k a n", a=2)
                    h = m.hpart[0:HALF, half, 0:2 * MODES].rearrange("k (a n) -> k a n", a=2)
                    unmix(lambda part, b: m.z[:, half, part, b], (g[:, 0], g[:, 1]), (h[:, 0], h[:, 1]), S3.fwd.dve)
                for j in (1, 3):
                    dve.wait_ge(S3.chan.pe, j + 1)
                    dve.tensor_copy(m.ak[:, j // 2, 2 * MODES:4 * MODES], m.bank[4 + j][0:HALF, 0:2 * MODES]).then_inc(S3.chan.dve, 1)
                for j in range(1, 8, 2):
                    half, g = j // 4, j // 2 % 2
                    dve.wait_ge(S3.mlp1.pe, j + 1)
                    dve.tensor_scalar(m.o1[0:HALF, half, 1, 2 * MODES * g:2 * MODES * (g + 1)], m.bank[j % 4][0:HALF, 0:2 * MODES],
                                      f3.b[:, 0, 1, half:half + 1], 0.0, ALU.add, ALU.max).then_inc(S3.mlp1.dve, 1)
                for j in range(4):
                    half, g = divmod(j, 2)
                    cols = slice(2 * MODES * g, 2 * MODES * (g + 1))
                    dve.wait_ge(S3.o2nk.pe, j + 1)
                    dve.scalar_tensor_tensor(m.s[:, half, cols], m.bank[j][0:HALF, 0:2 * MODES], f3.b[:, 1, 1, half:half + 1],
                                             m.o2k[:, half, cols], ALU.add, ALU.add).then_inc(S3.s, 1)
                dve.wait_ge(S3.s, 4)
                dve.tensor_scalar(m.clip3[:], m.s[:], -LAMBDA, LAMBDA, ALU.max, ALU.min).then_inc(S3.clipped, 1)
                dve.wait_ge(S3.clipped, 1)
                dve.tensor_tensor(m.s[:], m.s[:], m.clip3[:], ALU.subtract).then_inc(S3.shrunk, 1)
                dve.wait_ge(S3.shrunk, 1)
                sv = m.s.rearrange("k d (b n) -> k d b n", b=IMAGES)
                dve.tensor_tensor(m.hs[:, :, 2:4], sv[:, :, 0:2], sv[:, :, 2:4], ALU.subtract).then_inc(S3.hs, 1)
                dve.tensor_tensor(m.hef[:], sv[:, :, 0:2], sv[:, :, 2:4], ALU.add).then_inc(S3.hef, 1)
                dve.wait_ge(S3.hef, 1)
                dve.tensor_tensor(m.hs[:, :, 0], m.hef[:, :, 0], m.hef[:, :, 1], ALU.add).then_inc(S3.hs, 1)
                dve.tensor_tensor(m.hs[:, :, 1], m.hef[:, :, 0], m.hef[:, :, 1], ALU.subtract).then_inc(S3.hs, 1)
                for chunk in range(2):
                    dve.wait_ge(S3.back.pe, 4 * chunk + 2)
                    dve.wait_ge(S3.back.act, 3 * chunk + 1)
                    g, h = m.bank[5][0:MCHUNK, :], m.hpart[0:MCHUNK, chunk]
                    unmix(lambda part, b: m.gb[:, part, chunk, b], (g[:, 0:CH], g[:, CH:2 * CH]), (h[:, 0:CH], h[:, CH:2 * CH]), S3.back.dve)
                for b in range(IMAGES):
                    dve.wait_ge(S3.inv.pe, b + 1)
                    dve.scalar_tensor_tensor(m.xb[:, b], m.bank[b][:, 0:2 * CH].rearrange("k (t c) -> k t c", t=2),
                                             1.0 / (TOKENS * CH), m.x[:, b], ALU.mult, ALU.add).then_inc(S3.inv.dve, 1)

            dve.memset(m.o1[HALF:HALF + 1], 1.0).then_inc(o1_ones_set, 1)
            attention(0, lambda b: dve.wait_ge(x_loaded[b], 16))
            spectral1()
            attention(1, lambda b: dve.wait_ge(S1.inv.dve, b + 1))
            spectral3()


def _halves(v):
    return v.reshape(2, HALF).T


def _block_diagonal(blocks):
    n = blocks.shape[-1]
    out = np.zeros((HALF, 2, HALF), blocks.dtype)
    for i in range(8):
        lo = n * (i % 4)
        out[lo:lo + n, i // 4, lo:lo + n] = blocks[i]
    return out


def _laid_out(a):
    out = {"x": a["x"]}
    names = [("norm1_scale", "norm1_bias", "norm2_scale", "norm2_bias"), ("ln1_w", "ln1_b", "ln2_w", "ln2_b")]
    for l, (layer, (s1, b1, s2, b2)) in enumerate(zip(("L0_conv_", "L2_conv_"), names)):
        g = lambda n: a[layer + n]
        qb, kb, vb = g("qkv_b").reshape(3, CH)
        out[f"vecs{l}"] = np.concatenate([_halves(v) for v in (g(s1), g(b1), qb, kb, vb, g(s2), g(b2))], 1)
        out[f"qkv{l}"] = g("qkv_w").reshape(2, HALF, 3 * CH).transpose(1, 0, 2)
        rel = np.zeros((HALF, 2, 2 * WIN - 1, GROUP), np.float32)
        for n, table in enumerate((g("rel_pos_h"), g("rel_pos_w"))):
            for h in range(GROUP):
                rel[HD * h:HD * (h + 1), n, :, h] = table[::-1].T
        out[f"rel{l}"] = rel.reshape(HALF, 2, -1)
        out[f"fc1b{l}"] = g("fc1_b").reshape(HID_TILES, 128).T
        out[f"rows{l}"] = np.broadcast_to(np.stack([g("proj_b"), g("fc2_b")]), (128, 2, CH))
        out[f"proj{l}"] = g("proj_w").reshape(2, HALF, CH).transpose(1, 0, 2)
        out[f"fc1{l}"] = g("fc1_w").reshape(2, HALF, HID).transpose(1, 0, 2)
        out[f"fc2{l}"] = g("fc2_w").reshape(HID_TILES, 128, CH).transpose(1, 0, 2)
    w1, w2 = a["L1_conv_w1"], a["L1_conv_w2"]
    out["f1_w1"] = np.stack([_block_diagonal(w1[..., i]) for i in range(2)], 1)
    out["f1_b1"] = np.stack([_halves(a["L1_conv_b1"][..., i].reshape(-1)) for i in range(2)], 1)
    f1_w2 = np.zeros((HALF + 1, 2, 2, HALF), np.float32)
    for i in range(2):
        f1_w2[:HALF, i] = _block_diagonal(w2[..., i])
        f1_w2[HALF, i] = a["L1_conv_b2"][..., i].reshape(2, HALF)
    out["f1_w2"] = f1_w2
    out["f3_w"] = np.stack([np.stack([_block_diagonal(a[f"L3_conv_{n}"][i]).reshape(HALF, 2 * HALF) for i in range(2)], 1)
                            for n in ("w1", "w2")], 1)
    out["f3_b"] = np.stack([np.stack([_halves(a[f"L3_conv_{n}"][i].reshape(-1)) for i in range(2)], 1)
                            for n in ("b1", "b2")], 1)
    return out


def kernel(**inputs):
    import concourse.bacc as bacc
    from concourse.bass_utils import run_bass_kernel_spmd

    nc = bacc.Bacc("TRN2", target_bir_lowering=False, num_devices=1)
    laid = _laid_out({k: np.asarray(v) for k, v in inputs.items()})
    laid.update(constants())
    arrays, args = {}, {}
    for name, a in laid.items():
        a = np.ascontiguousarray(a)
        arrays[f"in_{name}"] = a
        args[name] = nc.dram_tensor(f"in_{name}", a.shape, mybir.dt.from_np(a.dtype), kind="ExternalInput").ap()
    out = nc.dram_tensor("out", (IMAGES, SIDE, SIDE, CH), F32, kind="ExternalOutput").ap()
    build(nc, args, out)
    result = run_bass_kernel_spmd(nc, [arrays], core_ids=[0])
    return result.results[0]["out"]
```

```python
from contextlib import ExitStack

import numpy as np
import concourse.bass as bass
from concourse import mybir

F32 = mybir.dt.float32
ALU = mybir.AluOpType
ACT = mybir.ActivationFunctionType
AX = mybir.AxisListType.X

IMAGES, SIDE, CH = 4, 16, 192
WIN = 14
EDGE = SIDE - WIN
PLACES = SIDE * SIDE
TOKENS = IMAGES * PLACES
TILES = TOKENS // 128
HALF = CH // 2
HEADS, HD = 12, 16
QUADS = HEADS // 4
GROUP = HALF // HD
HID = 4 * CH
HID_TILES = HID // 128
CODES = 2 * IMAGES
BIAS_ROW = 4 * HD
CODE_ROW = BIAS_ROW + 2 * WIN
AUG = CODE_ROW + CODES
PAD_RIGHT = WIN * (WIN - EDGE)
PAD_LOW = PAD_RIGHT + EDGE * (WIN - EDGE)
KEYS = TOKENS + PAD_RIGHT + PAD_LOW
HW_ROWS = WIN // 2
HALF_WIN = HW_ROWS * WIN
MAIN = IMAGES * WIN * WIN
RIGHT = IMAGES * WIN * EDGE
LOW = IMAGES * EDGE * SIDE
BIG = 1e30
HALF_COLS = SIDE // 2 + 1
MODES = SIDE * HALF_COLS
MCHUNK = MODES // 2
LAMBDA = 0.01
EPS = (1e-6, 1e-5)


def _places():
    h, w = np.divmod(np.arange(PLACES), SIDE)
    return h, w


def _key_rows():
    out = np.zeros((2 * WIN + CODES, KEYS), np.float32)
    h, w = _places()
    for b in range(IMAGES):
        at = b * PLACES + np.arange(PLACES)
        out[h % WIN, at] = 4.0
        out[WIN + w % WIN, at] = 4.0
        for code in range(CODES):
            right = (h < WIN) & (w >= WIN)
            low = (h >= WIN) & (w < WIN)
            corner = (h >= WIN) & (w >= WIN)
            other = (right & (code != b) & (code < IMAGES)) | (low & (code != b)) | (corner & (code != IMAGES + b))
            out[2 * WIN + code, at[other]] = -BIG
    pads = [(i, j) for i in range(WIN) for j in range(EDGE, WIN)]
    pads += [(i, j) for i in range(EDGE, WIN) for j in range(WIN)]
    pads += [(i, j) for i in range(EDGE) for j in range(EDGE, WIN)]
    for n, (i, j) in enumerate(pads):
        out[i, TOKENS + n] = 4.0
        out[WIN + j, TOKENS + n] = 4.0
    out[2 * WIN:2 * WIN + IMAGES, TOKENS + 2 * PAD_RIGHT:] = -BIG
    return out


def _query_codes():
    out = np.zeros((CODES, TOKENS), np.float32)
    for b in range(IMAGES):
        out[b, MAIN + b * WIN * EDGE:MAIN + (b + 1) * WIN * EDGE] = 1.0
        for r in range(EDGE):
            at = MAIN + RIGHT + (EDGE * b + r) * SIDE
            out[b, at:at + WIN] = 1.0
            out[IMAGES + b, at + WIN:at + SIDE] = 1.0
    return out


def constants():
    h, w = _places()
    kh, kw = np.divmod(np.arange(MODES), HALF_COLS)
    theta = 2 * np.pi * (np.outer(h, kh) + np.outer(w, kw)) / SIDE
    space = np.stack([np.cos(theta), -np.sin(theta)], 1)
    back = np.stack([np.cos(theta) - np.sin(theta), np.cos(theta) + np.sin(theta)], 1)
    flip = np.zeros((PLACES, MODES))
    flip[((-kh) % SIDE) * SIDE + (-kw) % SIDE, np.arange(MODES)] = 1.0
    spec = np.zeros((2 * MODES, SIDE, HALF_COLS), complex)
    spec[np.arange(MODES), kh, kw] = 1.0
    spec[MODES + np.arange(MODES), kh, kw] = 1j
    inverse = np.fft.irfft2(spec, s=(SIDE, SIDE), norm="ortho").reshape(2, 2, MCHUNK, PLACES)
    phi = 2 * np.pi * np.outer(np.arange(CH), np.arange(CH)) / CH
    c, s = np.cos(phi), np.sin(phi)
    chan = np.stack([c - s, c + s], 1).reshape(2, HALF, 2, CH)
    chan_back = np.concatenate([c, -s], 1).reshape(2, HALF, 2 * CH)
    made = {
        "space_fwd": space.reshape(2, 128, 2 * MODES).transpose(1, 0, 2),
        "flip": flip.reshape(2, 128, MODES).transpose(1, 0, 2),
        "inverse": inverse.transpose(2, 0, 1, 3),
        "space_back": back.transpose(2, 1, 0).reshape(2, MCHUNK, 2, PLACES).transpose(1, 0, 2, 3),
        "chan_fwd": chan.transpose(1, 0, 2, 3),
        "chan_back": chan_back.transpose(1, 0, 2),
        "ident": np.eye(128),
        "key_rows": _key_rows(),
        "query_codes": _query_codes(),
    }
    return {k: np.ascontiguousarray(v, np.float32) for k, v in made.items()}


PROJ = []
for _g in range(2):
    PROJ += [("q", _g, 0, "act"), ("q", _g, 1, "act"), ("k", _g, 0, "dve"), ("k", _g, 1, "dve"),
             ("rel_h", _g, 0, "act"), ("rel_h", _g, 1, "act"), ("rel_w", _g, 0, "dve"), ("rel_w", _g, 1, "dve")]
PROJ += [("v", 0, 0, "act"), ("v", 1, 0, "dve"), ("v", 2, 0, "act"), ("v", 3, 0, "dve"), ("v", 4, 0, "dve")]


def taken_out(j):
    who = PROJ[j][3]
    return who, sum(p[3] == who for p in PROJ[:j + 1])


def job(kind, group, part):
    return [p[:3] for p in PROJ].index((kind, group, part))


UNITS = [(b, h) for b in range(IMAGES) for h in range(HEADS)]
UNITS += [(IMAGES + s, 4 * q + n) for q in range(QUADS) for s in range(2) for n in range(4)]
N_UNITS = len(UNITS)
S_RING = 4
TURN_RING = 3
P_RING = 4
T_RING = 7
TURN_LAG = 3
PV_LAG = 6


def o_job(u):
    b, h = UNITS[u]
    return min(b, IMAGES) * QUADS + h // 4


LAST = [max(u // 4 for u in range(N_UNITS) if o_job(u) == j) for j in range((IMAGES + 1) * QUADS)]


def turned_by(u):
    return ("dve", (u + 3) // 3) if u % 3 == 0 else ("act", u - u // 3)


class Named:
    pass


def build(nc, t, out):
    ctx = ExitStack()
    with ctx:
        def sb(name, shape):
            return ctx.enter_context(nc.sbuf_tensor(name, shape, F32))

        def sem(name):
            return ctx.enter_context(nc.semaphore(name))

        m = Named()
        m.bank = [ctx.enter_context(nc.psum_tensor(f"bank{i}", [128, 512], F32)) for i in range(8)]
        m.qaug = sb("qaug", [128, HEADS, TOKENS])
        m.kaug = sb("kaug", [AUG, QUADS, KEYS])
        m.x = sb("x_tok", [128, IMAGES, 2, CH])
        m.xb = sb("x_plus_bias", [128, IMAGES, 2, CH])
        m.yT = sb("yT", [HALF, 2, TOKENS])
        m.norm_q = sb("norm_or_q", [128, 2 * TOKENS])
        m.xn = m.norm_q[:, 0:TILES * CH].rearrange("p (i c) -> p i c", c=CH)
        m.qW = m.norm_q[0:HALF, :].rearrange("p (a n) -> p a n", a=2)
        m.probs = sb("probs", [128, P_RING, 4 * HALF_WIN])
        m.probsT = sb("probsT", [128, T_RING, 4 * HALF_WIN])
        m.v = sb("v_padded", [128, 2 * IMAGES + 2, HEADS, 32])
        m.stats = sb("stats", [128, TILES, 6])
        m.meanvar = sb("meanvar", [128, TILES, 2])
        m.var, m.std, m.rstd = (sb(n, [128, TILES]) for n in ("var_eps", "std", "rstd"))
        m.negmax = sb("negmax", [128, P_RING, 2])
        m.sums = sb("sums", [128, P_RING, 2])
        m.recip = sb("recip", [128, P_RING, 2])
        m.qb4 = sb("qb4", [HALF, 2, 2])
        m.yW = m.probsT[0:HALF].rearrange("p a n -> p (a n)")[:, 0:2 * TOKENS].rearrange("p (a n) -> p a n", a=2)
        arena = sb("arena", [128, 9216])

        def carve(base, at, rows, *dims):
            n = int(np.prod(dims))
            view = base[0:rows, at:at + n]
            names = "abcde"[:len(dims)]
            if len(dims) > 1:
                view = view.rearrange(f"p ({' '.join(names)}) -> p {' '.join(names)}",
                                      **{k: d for k, d in zip(names, dims)})
            return view, at + n

        m.qT, at = carve(arena, 0, HALF, 2, TOKENS)
        m.kT, at = carve(arena, at, HALF, 2, KEYS)
        m.relhT, at = carve(arena, at, GROUP * WIN, 2, TOKENS)
        m.relwT, at = carve(arena, at, GROUP * WIN, 2, TOKENS)
        m.oT, at = carve(arena, 0, 128, QUADS, TOKENS)
        m.hidT, _ = carve(arena, at, 128, HID_TILES, TOKENS)
        m.xf, at = carve(arena, 0, HALF, 2, 2, IMAGES * MODES)
        m.o2, at = carve(arena, at, MCHUNK, 2, 2, IMAGES, CH)
        m.clip1, at = carve(arena, at, MCHUNK, 2, 2 * CH)
        m.o1, at = carve(arena, at, HALF + 1, 2, 2, IMAGES * MODES)
        m.mix, at = carve(arena, 0, 128, 4, 2, CH)
        m.ef, at = carve(arena, at, 128, 2, 2, CH)
        m.hpart, at = carve(arena, at, 128, 2, 2 * CH)
        m.z, at = carve(arena, at, HALF, 2, 2, IMAGES, MODES)
        m.an, at = carve(arena, at, HALF, 2, IMAGES * MODES)
        m.ak, at = carve(arena, at, HALF, 2, IMAGES * MODES)
        qflat = m.qaug[:, :, :].rearrange("p a b -> p (a b)")
        m.o1n, at = carve(qflat, 0, HALF, 2, 2, IMAGES * MODES)
        m.o2k, at = carve(qflat, at, HALF, 2, IMAGES * MODES)
        m.s, at = carve(qflat, at, HALF, 2, IMAGES * MODES)
        m.clip3, at = carve(qflat, at, HALF, 2, IMAGES * MODES)
        m.hs, at = carve(qflat, at, HALF, 2, 4, MODES)
        m.hef, at = carve(qflat, at, HALF, 2, 2, MODES)
        m.gb, at = carve(qflat, at, MCHUNK, 2, 2, IMAGES, CH)

        c = {name: sb(name, list(t[name].shape))
             for name in ("space_fwd", "flip", "inverse", "chan_fwd", "chan_back", "ident")}
        c["space_back"] = c["inverse"]
        w = [{}, {}]
        ATT = ("vecs", "qkv", "rel", "cols", "rows", "proj", "fc1", "fc2")
        for l in range(2):
            for name in ATT:
                shared = l == 1 and name in ("qkv", "rows", "proj", "fc1", "fc2")
                w[l][name] = w[0][name] if shared else sb(f"{name}{l}", list(t[f"{name}{l}"].shape))
        f1, f3 = Named(), Named()
        f1.w1 = sb("f1_w1", [HALF, 3, 2, HALF])
        f1.b1 = sb("f1_b1", [HALF, 2, 2])
        f1.w2 = sb("f1_w2", [HALF + 1, 3, 2, HALF])
        f3.w = sb("f3_w", [HALF, 2, 2, 2 * HALF])
        f3.mixw = sb("f3_mixw", [HALF, 2, 2, 2 * HALF])
        f3.b = sb("f3_b", [HALF, 2, 2, 2])

        x_loaded = [sem(f"x_loaded{b}") for b in range(IMAGES)]
        ident_loaded = sem("ident_loaded")
        aug_rows_loaded = sem("aug_rows_loaded")
        spectral_loaded = sem("spectral_loaded")
        v_zeroed, q_zeroed = sem("v_zeroed"), sem("q_zeroed")
        o1_ones_set = sem("o1_ones_set")
        space_back_loaded = sem("space_back_loaded")
        weights_mixed = sem("weights_mixed")
        stored = sem("stored")

        def stage(name, takers="act dve"):
            s = Named()
            s.pe = sem(f"{name}_pe")
            s.act = sem(f"{name}_act") if "act" in takers else None
            s.dve = sem(f"{name}_dve") if "dve" in takers else None
            return s

        def attention_sems(l):
            s = Named()
            s.loaded = {n: sem(f"{n}{l}_loaded") for n in ("vecs", "qkv", "rel", "late")}
            s.proj_in, s.out_proj = stage(f"proj_in{l}"), stage(f"out_proj{l}", "dve")
            s.fc1, s.fc2 = stage(f"fc1{l}", "act"), stage(f"fc2{l}", "dve")
            s.ln = []
            for k in range(2):
                n = stage(f"ln{l}_{k}")
                n.stats, n.mean, n.var, n.std, n.rstd, n.done = (sem(f"ln{l}_{k}_{q}") for q in ("stats", "mean", "var", "std", "rstd", "done"))
                s.ln.append(n)
            s.qb_scaled, s.kpad_set, s.bias_added = sem(f"qb_scaled{l}"), sem(f"kpad_set{l}"), sem(f"bias_added{l}")
            s.q_ordered, s.y_ordered = sem(f"q_ordered{l}"), sem(f"y_ordered{l}")
            s.aug = [sem(f"aug{l}_{q}") for q in range(QUADS)]
            s.scores, s.max, s.probs = sem(f"scores{l}"), sem(f"max{l}"), sem(f"probs{l}")
            s.recip, s.normed, s.pv, s.oT_out = sem(f"recip{l}"), sem(f"normed{l}"), sem(f"pv{l}"), sem(f"oT_out{l}")
            s.turn = stage(f"turn{l}")
            return s

        A = [attention_sems(0), attention_sems(1)]
        S1 = Named()
        S1.fwd, S1.mlp1 = stage("s1_fwd"), stage("s1_mlp1")
        S1.mlp2, S1.inv = stage("s1_mlp2", "dve"), stage("s1_inv", "dve")
        S1.clipped = sem("s1_clipped")
        S3 = Named()
        S3.fwd, S3.flip, S3.chan, S3.mlp1 = stage("s3_fwd"), stage("s3_flip"), stage("s3_chan"), stage("s3_mlp1")
        S3.o2k, S3.o2nk = stage("s3_o2k", "act"), stage("s3_o2nk", "dve")
        S3.back, S3.inv = stage("s3_back"), stage("s3_inv", "dve")
        S3.mixed, S3.ef, S3.s, S3.clipped = sem("s3_mixed"), sem("s3_ef"), sem("s3_s"), sem("s3_clipped")
        S3.shrunk, S3.hef, S3.hs = sem("s3_shrunk"), sem("s3_hef"), sem("s3_hs")

        def raster(ap):
            return ap.rearrange("k (b r w) -> k b r w", b=IMAGES, r=SIDE)

        def main(ap):
            return ap[:, 0:MAIN].rearrange("k (b r w) -> k b r w", b=IMAGES, r=WIN)

        def right(ap):
            return ap[:, MAIN:MAIN + RIGHT].rearrange("k (b r w) -> k b r w", b=IMAGES, r=WIN)

        def low(ap):
            return ap[:, MAIN + RIGHT:TOKENS].rearrange("k (b r w) -> k b r w", b=IMAGES, r=EDGE)

        def to_window_order(copy, dst, src, lo, hi):
            top = min(hi, WIN)
            copy(main(dst)[:, :, lo:top], src[:, :, 0:top - lo, 0:WIN])
            last = copy(right(dst)[:, :, lo:top], src[:, :, 0:top - lo, WIN:SIDE])
            return copy(low(dst), src[:, :, top - lo:hi - lo, :]) if hi > WIN else last

        def window(ap, s):
            return raster(ap)[:, :, 0:WIN, WIN:SIDE] if s == 0 else raster(ap)[:, :, WIN:SIDE, :]

        EDGE_TOKENS = (RIGHT, LOW)
        EDGE_AT = (MAIN, MAIN + RIGHT)
        EDGE_PADS = ((TOKENS, PAD_RIGHT), (TOKENS + PAD_RIGHT, PAD_LOW))

        def turned_size(u):
            b = UNITS[u][0]
            return (HALF_WIN, 4 * HALF_WIN) if b < IMAGES else (EDGE_TOKENS[b - IMAGES], EDGE_TOKENS[b - IMAGES])

        def wait_for(eng, st, who, n):
            eng.wait_ge(st.act if who == "act" else st.dve, n)

        KEY_PIECES = (((0, 0, 3), (1, 4, 5)), ((1, 6, 7), (2, 8, 11)))
        AUG_LANDED = [16 * (3 * 4 + sum(p[0] == quad for g in KEY_PIECES for p in g)) for quad in range(QUADS)]

        block = ctx.enter_context(nc.Block())

        @block.sync
        def _(sp):
            x_dram = t["x"].rearrange("b h w c -> b (h w) c").rearrange("b (t p) c -> b p t c", p=128)
            for b in range(IMAGES):
                sp.dma_start(m.x[:, b], x_dram[b]).then_inc(x_loaded[b], 16)
            sp.dma_start(c["ident"][:, :], t["ident"]).then_inc(ident_loaded, 16)

            def load(l, name, s):
                sp.dma_start(w[l][name][:], t[f"{name}{l}"]).then_inc(s, 16)

            for name in ("vecs", "qkv", "rel"):
                load(0, name, A[0].loaded[name])
            sp.dma_start(m.kaug[BIAS_ROW:AUG], t["key_rows"].unsqueeze(1).broadcast_to([AUG - BIAS_ROW, QUADS, KEYS]))\
              .then_inc(aug_rows_loaded, 16)
            sp.dma_start(m.qaug[CODE_ROW:AUG], t["query_codes"].unsqueeze(1).broadcast_to([CODES, HEADS, TOKENS]))\
              .then_inc(aug_rows_loaded, 16)
            sp.wait_ge(q_zeroed, 1)
            for name in ("rows", "cols", "proj", "fc1", "fc2"):
                load(0, name, A[0].loaded["late"])
            sp.dma_start(f1.w1[:, 0:2], t["f1_w1"]).then_inc(spectral_loaded, 16)
            sp.dma_start(f1.w2[:, 0:2], t["f1_w2"]).then_inc(spectral_loaded, 16)
            sp.dma_start(f1.b1[:], t["f1_b1"]).then_inc(spectral_loaded, 16)
            sp.dma_start(f3.w[:], t["f3_w"]).then_inc(spectral_loaded, 16)
            sp.dma_start(f3.b[:], t["f3_b"]).then_inc(spectral_loaded, 16)
            for name in ("space_fwd", "flip", "inverse", "chan_fwd", "chan_back"):
                sp.dma_start(c[name][:], t[name]).then_inc(spectral_loaded, 16)
            load(1, "vecs", A[1].loaded["vecs"])
            load(1, "rel", A[1].loaded["rel"])
            load(1, "cols", A[1].loaded["late"])

            for l in range(2):
                s = A[l]
                if l == 1:
                    sp.wait_ge(A[0].proj_in.pe, len(PROJ))
                    load(1, "qkv", s.loaded["qkv"])
                    sp.wait_ge(A[0].out_proj.pe, IMAGES)
                    load(1, "proj", s.loaded["late"])
                    sp.wait_ge(A[0].bias_added, 2 * IMAGES)
                    load(1, "rows", s.loaded["late"])
                    sp.wait_ge(A[0].fc1.pe, 2 * HID_TILES)
                    load(1, "fc1", s.loaded["late"])
                    sp.wait_ge(A[0].fc2.pe, IMAGES)
                    load(1, "fc2", s.loaded["late"])
                for g in range(2):
                    for kind in ("q", "k", "rel_h", "rel_w"):
                        if kind == "q":
                            sp.wait_ge(s.q_ordered, g + 1)
                        else:
                            wait_for(sp, s.proj_in, *taken_out(job(kind, g, 1)))
                        if kind == "k":
                            sp.wait_ge(s.kpad_set, g + 1)
                            for quad, first, last in KEY_PIECES[g]:
                                sp.dma_start(m.kaug[HD * (first % 4):HD * (last % 4 + 1), quad, :],
                                             m.kT[HD * (first % GROUP):HD * (last % GROUP + 1), g]).then_inc(s.aug[quad], 16)
                            continue
                        for n in range(GROUP):
                            head = GROUP * g + n
                            if kind == "q":
                                lo = HD * (head % 4)
                                sp.dma_start(m.qaug[lo:lo + HD, head, :], m.qW[HD * n:HD * (n + 1), g]).then_inc(s.aug[head // 4], 16)
                            else:
                                lo, src = (BIAS_ROW, m.relhT) if kind == "rel_h" else (BIAS_ROW + WIN, m.relwT)
                                sp.dma_start(m.qaug[lo:lo + WIN, head, :], src[n:GROUP * WIN:GROUP, g]).then_inc(s.aug[head // 4], 16)
                if l == 1:
                    sp.wait_ge(S1.inv.pe, IMAGES)
                    sp.dma_start(c["space_back"][:], t["space_back"]).then_inc(space_back_loaded, 16)
            out_dram = out.rearrange("b h w c -> b (h w) c").rearrange("b (t p) c -> b p t c", p=128)
            for b in range(IMAGES):
                sp.wait_ge(S3.inv.dve, b + 1)
                sp.dma_start(out_dram[b], m.xb[:, b]).then_inc(stored, 16)
            sp.wait_ge(stored, 16 * IMAGES)

        @block.gpsimd
        def _(pool):
            pool.memset(m.qaug[0:BIAS_ROW], 0.0).then_inc(q_zeroed, 1)
            pool.memset(m.v[:], 0.0).then_inc(v_zeroed, 1)

            def attention(l, x_ready):
                s = A[l]
                pool.wait_ge(s.loaded["vecs"], 16)
                for g in range(2):
                    if l == 1 and g == 0:
                        pool.wait_ge(S1.inv.pe, IMAGES)
                        pool.wait_ge(S1.inv.dve, IMAGES)
                    pool.tensor_copy(m.kT[:, g, TOKENS:KEYS], w[l]["vecs"][:, 6 + g:7 + g].broadcast_to([HALF, KEYS - TOKENS]))\
                        .then_inc(s.kpad_set, 1)
                pool.wait_ge(s.ln[0].act, 2)
                pool.wait_ge(s.ln[0].dve, 2)
                for half in range(2):
                    to_window_order(pool.tensor_copy, m.yW[:, half], raster(m.yT[:, half]), 0, SIDE).then_inc(s.y_ordered, 1)
                for g in range(2):
                    wait_for(pool, s.proj_in, *taken_out(job("q", g, 1)))
                    to_window_order(pool.tensor_copy, m.qW[:, g], raster(m.qT[:, g]), 0, SIDE).then_inc(s.q_ordered, 1)
                for u in range(N_UNITS):
                    n, cols = turned_size(u)
                    pool.wait_ge(s.recip, u + 1)
                    p, by = m.probs[0:n, u % P_RING, 0:cols], m.recip[0:n, u % P_RING]
                    if UNITS[u][0] < IMAGES:
                        p = p.rearrange("k (a n) -> k a n", a=2)
                        pool.tensor_tensor(p, p, by.unsqueeze(2).broadcast_to([n, 2, cols // 2]), ALU.mult).then_inc(s.normed, 1)
                    else:
                        pool.tensor_scalar(p, p, by[:, 0:1], None, ALU.mult).then_inc(s.normed, 1)
                pool.wait_ge(s.loaded["late"], 16 * 5)
                for b in range(IMAGES):
                    x_ready(pool, b)
                    pool.tensor_tensor(m.xb[:, b], m.x[:, b], w[l]["rows"][:, 0:1].broadcast_to([128, 2, CH]), ALU.add)\
                        .then_inc(s.bias_added, 1)
                for b in range(IMAGES):
                    pool.wait_ge(s.out_proj.dve, b + 1)
                    pool.tensor_tensor(m.xb[:, b], m.x[:, b], w[l]["rows"][:, 1:2].broadcast_to([128, 2, CH]), ALU.add)\
                        .then_inc(s.bias_added, 1)

            attention(0, lambda eng, b: eng.wait_ge(x_loaded[b], 16))
            pool.wait_ge(spectral_loaded, 16 * 10)
            pool.tensor_scalar(f1.w1[:, 2], f1.w1[:, 1], -1.0, None, ALU.mult).then_inc(weights_mixed, 1)
            pool.tensor_scalar(f1.w2[0:HALF, 2], f1.w2[0:HALF, 1], -1.0, None, ALU.mult).then_inc(weights_mixed, 1)
            pool.tensor_tensor(f3.mixw[:, :, 0], f3.w[:, :, 0], f3.w[:, :, 1], ALU.add).then_inc(weights_mixed, 1)
            pool.tensor_tensor(f3.mixw[:, :, 1], f3.w[:, :, 0], f3.w[:, :, 1], ALU.subtract).then_inc(weights_mixed, 1)
            pool.wait_ge(weights_mixed, 4)
            pool.tensor_scalar(f3.mixw[:], f3.mixw[:], 0.5, None, ALU.mult).then_inc(weights_mixed, 1)
            attention(1, lambda eng, b: eng.wait_ge(S1.inv.dve, b + 1))

        @block.tensor
        def _(pe):
            mm = nc.tensor.matmul

            def turn_norm(s, ln, bank0):
                for g in range(2):
                    for half in range(2):
                        pe.wait_ge(ln.done, 4 * g + 4)
                        for i in range(4):
                            last = nc.tensor.transpose(m.bank[bank0 + 2 * g + half][0:HALF, 128 * i:128 * (i + 1)],
                                                       m.xn[:, 4 * g + i, HALF * half:HALF * (half + 1)], c["ident"][:])
                        last.then_inc(ln.pe, 1)

            def attention(l):
                s, wl = A[l], w[l]
                if l == 0:
                    pe.wait_ge(ident_loaded, 16)
                turn_norm(s, s.ln[0], 0)
                pe.wait_ge(s.loaded["qkv"], 16)
                pe.wait_ge(s.loaded["rel"], 16)
                for j, (kind, g, part, _) in enumerate(PROJ):
                    if j >= 4:
                        wait_for(pe, s.proj_in, *taken_out(j - 4))
                    elif j < 2:
                        pe.wait_ge(s.ln[0].act, j + 1)
                        pe.wait_ge(s.ln[0].dve, j + 1)
                    bank = m.bank[4 + j % 4]
                    if kind in "qk":
                        col = (0 if kind == "q" else CH) + HALF * g
                        for half in range(2):
                            last = mm(bank[0:HALF, :], wl["qkv"][:, half, col:col + HALF], m.yT[:, half, 512 * part:512 * (part + 1)],
                                      start=half == 0, stop=half == 1)
                    elif kind in ("rel_h", "rel_w"):
                        wait_for(pe, s.proj_in, *taken_out(job("q", g, 1)))
                        q = raster(m.qT[:, g])[:, :, 8 * part:8 * (part + 1), :] if kind == "rel_w" else raster(m.qT[:, g])
                        for n in range(8 if kind == "rel_h" else SIDE):
                            place = (8 * part + n if kind == "rel_h" else n) % WIN
                            table = wl["rel"][:, 0 if kind == "rel_h" else 1, GROUP * (WIN - 1 - place):GROUP * (2 * WIN - 1 - place)]
                            cols = 64 if kind == "rel_h" else 32
                            last = mm(bank[0:GROUP * WIN, cols * n:cols * (n + 1)], table,
                                      q[:, :, 8 * part + n, :] if kind == "rel_h" else q[:, :, :, n], start=True, stop=True)
                    else:
                        pe.wait_ge(s.y_ordered, 2)
                        for tile in range(2):
                            n = HALF_WIN if g < IMAGES else EDGE_TOKENS[tile]
                            at = HALF_WIN * (2 * g + tile) if g < IMAGES else EDGE_AT[tile]
                            for half in range(2):
                                last = mm(bank[0:n, CH * tile:CH * (tile + 1)], m.yW[:, half, at:at + n], wl["qkv"][:, half, 2 * CH:3 * CH],
                                          start=half == 0, stop=half == 1)
                    last.then_inc(s.proj_in.pe, 1)

                if l == 0:
                    pe.wait_ge(aug_rows_loaded, 16 * 2)
                for step in range(N_UNITS + PV_LAG):
                    if step < N_UNITS:
                        b, h = UNITS[step]
                        if step >= S_RING:
                            pe.wait_ge(s.probs, step - S_RING + 1)
                        if step < HEADS and h % 4 == 0:
                            pe.wait_ge(s.aug[h // 4], AUG_LANDED[h // 4])
                        q, k = m.qaug[0:AUG, h], m.kaug[:, h // 4, 0:TOKENS]
                        bank = m.bank[step % S_RING]
                        if b < IMAGES:
                            keys = raster(k)[:, b, 0:WIN, 0:WIN]
                            for part in range(2):
                                at = HALF_WIN * (2 * b + part)
                                last = mm(bank[0:HALF_WIN, 2 * HALF_WIN * part:2 * HALF_WIN * (part + 1)], q[:, at:at + HALF_WIN], keys,
                                          start=True, stop=True)
                        else:
                            e = b - IMAGES
                            n, (pad_at, pads) = EDGE_TOKENS[e], EDGE_PADS[e]
                            asking = q[:, EDGE_AT[e]:EDGE_AT[e] + n]
                            mm(bank[0:n, 0:n], asking, window(k, e), start=True, stop=True)
                            last = mm(bank[0:n, n:n + pads], asking, m.kaug[:, h // 4, pad_at:pad_at + pads], start=True, stop=True)
                        last.then_inc(s.scores, 1)
                    if TURN_LAG <= step < N_UNITS + TURN_LAG:
                        u = step - TURN_LAG
                        b, h = UNITS[u]
                        if u == 0:
                            pe.wait_ge(s.proj_in.act, taken_out(job("v", 2, 0))[1])
                            pe.wait_ge(s.proj_in.dve, taken_out(job("v", 4, 0))[1])
                        pe.wait_ge(s.normed, u + 1)
                        if u >= TURN_RING:
                            wait_for(pe, s.turn, *turned_by(u - TURN_RING))
                        bank = m.bank[S_RING + u % TURN_RING]
                        if b < IMAGES:
                            for key in range(2):
                                for part in range(2):
                                    at = HALF_WIN * (2 * key + part)
                                    src = m.probs[0:HALF_WIN, u % P_RING, HALF_WIN * (2 * part + key):HALF_WIN * (2 * part + key + 1)]
                                    last = nc.tensor.transpose(bank[0:HALF_WIN, at:at + HALF_WIN], src, c["ident"][0:HALF_WIN, 0:HALF_WIN])
                        else:
                            n = EDGE_TOKENS[b - IMAGES]
                            last = nc.tensor.transpose(bank[0:n, 0:n], m.probs[0:n, u % P_RING, 0:n], c["ident"][0:n, 0:n])
                        last.then_inc(s.turn.pe, 1)
                    if step >= PV_LAG and (step - PV_LAG) % 4 == 3:
                        burst = (step - PV_LAG) // 4
                        units = range(4 * burst, 4 * burst + 4)
                        j = o_job(4 * burst)
                        for who in ("act", "dve"):
                            wait_for(pe, s.turn, who, max(turned_by(u)[1] for u in units if turned_by(u)[0] == who))
                        if j >= 1 and o_job(4 * burst - 1) != j:
                            pe.wait_ge(s.oT_out, j)
                        e = UNITS[4 * burst][0] - IMAGES
                        for key in range(2 if e < 0 else 1):
                            for u in units:
                                b, h = UNITS[u]
                                n, keys, at, cols = ((HALF_WIN, 2 * b + key, 0, 2 * HALF_WIN) if e < 0 else
                                                     (EDGE_TOKENS[e], 2 * IMAGES + e, EDGE_AT[e] - MAIN, EDGE_TOKENS[e]))
                                last = mm(m.bank[7][32 * (h % 4):32 * (h % 4) + 32, at:at + cols], m.v[0:n, keys, h],
                                          m.probsT[0:n, u % T_RING, cols * key:cols * (key + 1)], start=key == 0, stop=key == 1 or e >= 0)
                        last.then_inc(s.pv, 1)

                pe.wait_ge(s.oT_out, len(LAST))
                pe.wait_ge(s.loaded["late"], 16 * 5)
                for b in range(IMAGES):
                    for tile in range(2):
                        for quad in range(QUADS):
                            at = PLACES * b + 128 * tile
                            last = mm(m.bank[b][:, CH * tile:CH * (tile + 1)], m.oT[:, quad, at:at + 128], wl["proj"][:, quad],
                                      start=quad == 0, stop=quad == QUADS - 1)
                    last.then_inc(s.out_proj.pe, 1)
                turn_norm(s, s.ln[1], 4)
                for j in range(2 * HID_TILES):
                    g, hid = divmod(j, HID_TILES)
                    if hid == 0:
                        pe.wait_ge(s.ln[1].act, g + 1)
                        pe.wait_ge(s.ln[1].dve, g + 1)
                    if j < 4:
                        pe.wait_ge(s.out_proj.dve, j + 1)
                    else:
                        pe.wait_ge(s.fc1.act, j - 3)
                    for half in range(2):
                        last = mm(m.bank[j % 4][:, :], wl["fc1"][:, half, 128 * hid:128 * (hid + 1)], m.yT[:, half, 512 * g:512 * (g + 1)],
                                  start=half == 0, stop=half == 1)
                    last.then_inc(s.fc1.pe, 1)
                for b in range(IMAGES):
                    pe.wait_ge(s.fc1.act, HID_TILES * (b // 2 + 1))
                    for tile in range(2):
                        at = PLACES * b + 128 * tile
                        for hid in range(HID_TILES):
                            last = mm(m.bank[4 + b][:, CH * tile:CH * (tile + 1)], m.hidT[:, hid, at:at + 128], wl["fc2"][:, hid],
                                      start=hid == 0, stop=hid == HID_TILES - 1)
                    last.then_inc(s.fc2.pe, 1)

            def spectral1():
                pe.wait_ge(spectral_loaded, 16 * 10)
                for j in range(8):
                    b, half = divmod(j, 2)
                    pe.wait_ge(A[0].fc2.dve, b + 1)
                    if j >= 4:
                        wait_for(pe, S1.fwd, ("act", "dve")[j % 2], (j - 4) // 2 + 1)
                    for tile in range(2):
                        last = mm(m.bank[j % 4][0:HALF, 0:2 * MODES], m.x[:, b, tile, HALF * half:HALF * (half + 1)], c["space_fwd"][:, tile],
                                  start=tile == 0, stop=tile == 1)
                    last.then_inc(S1.fwd.pe, 1)
                pe.wait_ge(weights_mixed, 5)
                pe.wait_ge(o1_ones_set, 1)
                for j in range(8):
                    g, half, part = j // 4, j // 2 % 2, j % 2
                    pe.wait_ge(S1.fwd.act, 2 * g + 2)
                    pe.wait_ge(S1.fwd.dve, 2 * g + 2)
                    if j >= 4:
                        wait_for(pe, S1.mlp1, ("act", "dve")[j % 2], (j - 4) // 2 + 1)
                    cols = slice(2 * MODES * g, 2 * MODES * (g + 1))
                    o = m.bank[4 + j % 4][0:HALF, 0:2 * MODES]
                    mm(o, f1.w1[:, 0, half], m.xf[:, half, part, cols], start=True, stop=False)
                    last = mm(o, f1.w1[:, 1 if part else 2, half], m.xf[:, half, 1 - part, cols], start=False, stop=True)
                    last.then_inc(S1.mlp1.pe, 1)
                for j in range(8):
                    b, part = divmod(j, 2)
                    pe.wait_ge(S1.mlp1.act, 2 * (b // 2) + 2)
                    pe.wait_ge(S1.mlp1.dve, 2 * (b // 2) + 2)
                    if j >= 4:
                        pe.wait_ge(S1.mlp2.dve, j - 3)
                    for chunk in range(2):
                        at = MODES * b + MCHUNK * chunk
                        for half in range(2):
                            o = m.bank[j % 4][0:MCHUNK, CH * chunk + HALF * half:CH * chunk + HALF * (half + 1)]
                            mm(o, m.o1[:, half, 0, at:at + MCHUNK], f1.w2[:, part, half], start=True, stop=False)
                            last = mm(o, m.o1[0:HALF, half, 1, at:at + MCHUNK], f1.w2[0:HALF, 0 if part else 2, half], start=False, stop=True)
                    last.then_inc(S1.mlp2.pe, 1)
                for b in range(IMAGES):
                    pe.wait_ge(S1.mlp2.dve, 2 * (b + 1))
                    for tile in range(2):
                        for n in range(4):
                            last = mm(m.bank[4 + b][:, CH * tile:CH * (tile + 1)], c["inverse"][:, n // 2, n % 2, 128 * tile:128 * (tile + 1)],
                                      m.o2[:, n // 2, n % 2, b], start=n == 0, stop=n == 3)
                    last.then_inc(S1.inv.pe, 1)

            def spectral3():
                for b in range(IMAGES):
                    pe.wait_ge(A[1].fc2.dve, b + 1)
                    for half in range(2):
                        for tile in range(2):
                            last = mm(m.bank[4 + b][0:HALF, MODES * half:MODES * (half + 1)], m.x[:, b, tile, HALF * half:HALF * (half + 1)],
                                      c["flip"][:, tile], start=tile == 0, stop=tile == 1)
                    last.then_inc(S3.flip.pe, 1)
                for j in range(8):
                    mix, half = (3, 2, 0, 1)[j % 4], j // 4
                    pe.wait_ge(S3.mixed, 3)
                    if j >= 4:
                        wait_for(pe, S3.fwd, ("act", "dve", "act", "act")[j % 4], (1, 1, 2, 3)[j % 4])
                    for tile in range(2):
                        last = mm(m.bank[j % 4][0:HALF, 0:2 * MODES], m.mix[:, mix, tile, HALF * half:HALF * (half + 1)], c["space_fwd"][:, tile],
                                  start=tile == 0, stop=tile == 1)
                    last.then_inc(S3.fwd.pe, 1)
                pe.wait_ge(S3.fwd.act, 6)
                pe.wait_ge(S3.fwd.dve, 2)
                for j in range(4):
                    half, g = divmod(j, 2)
                    wait_for(pe, S3.flip, ("act", "dve")[j % 2], j // 2 + 1)
                    for n in range(4):
                        last = mm(m.bank[4 + j][0:HALF, 0:2 * MODES], c["chan_fwd"][:, n // 2, n % 2, HALF * half:HALF * (half + 1)],
                                  m.z[:, n // 2, n % 2, 2 * g:2 * g + 2], start=n == 0, stop=n == 3)
                    last.then_inc(S3.chan.pe, 1)
                for j in range(8):
                    half, g, nk = j // 4, j // 2 % 2, j % 2
                    wait_for(pe, S3.chan, ("act", "dve")[g], half + 1)
                    if j >= 4:
                        wait_for(pe, S3.mlp1, ("act", "dve")[j % 2], (j - 4) // 2 + 1)
                    cols = slice(2 * MODES * g, 2 * MODES * (g + 1))
                    o = m.bank[j % 4][0:HALF, 0:2 * MODES]
                    lo = slice(HALF * half, HALF * (half + 1))
                    mm(o, f3.mixw[:, 0, nk, lo], m.ak[:, half, cols], start=True, stop=False)
                    last = mm(o, f3.mixw[:, 0, 1 - nk, lo], m.an[:, half, cols], start=False, stop=True)
                    last.then_inc(S3.mlp1.pe, 1)
                for j in range(4):
                    half, g = divmod(j, 2)
                    pe.wait_ge(S3.mlp1.act, j + 1)
                    pe.wait_ge(S3.mlp1.dve, j + 1)
                    cols = slice(2 * MODES * g, 2 * MODES * (g + 1))
                    lo = slice(HALF * half, HALF * (half + 1))
                    o = m.bank[4 + j][0:HALF, 0:2 * MODES]
                    mm(o, f3.mixw[:, 1, 0, lo], m.o1n[0:HALF, half, 0, cols], start=True, stop=False)
                    last = mm(o, f3.mixw[:, 1, 1, lo], m.o1n[0:HALF, half, 1, cols], start=False, stop=True)
                    last.then_inc(S3.o2k.pe, 1)
                for j in range(4):
                    half, g = divmod(j, 2)
                    cols = slice(2 * MODES * g, 2 * MODES * (g + 1))
                    lo = slice(HALF * half, HALF * (half + 1))
                    o = m.bank[j][0:HALF, 0:2 * MODES]
                    mm(o, f3.mixw[:, 1, 0, lo], m.o1n[0:HALF, half, 1, cols], start=True, stop=False)
                    pe.wait_ge(S3.o2k.act, j + 1)
                    last = mm(o, f3.mixw[:, 1, 1, lo], m.o2k[:, half, cols], start=False, stop=True)
                    last.then_inc(S3.o2nk.pe, 1)
                for j in range(8):
                    chunk, mix = j // 4, (3, 2, 0, 1)[j % 4]
                    pe.wait_ge(S3.hs, 3)
                    if j >= 4:
                        wait_for(pe, S3.back, ("act", "dve", "act", "act")[j % 4], (1, 1, 2, 3)[j % 4])
                    for half in range(2):
                        last = mm(m.bank[4 + j % 4][0:MCHUNK, 0:2 * CH], m.hs[:, half, mix, MCHUNK * chunk:MCHUNK * (chunk + 1)],
                                  c["chan_back"][:, half], start=half == 0, stop=half == 1)
                    last.then_inc(S3.back.pe, 1)
                pe.wait_ge(S3.back.act, 6)
                pe.wait_ge(S3.back.dve, 2)
                pe.wait_ge(space_back_loaded, 16)
                for b in range(IMAGES):
                    for tile in range(2):
                        for n in range(4):
                            last = mm(m.bank[b][:, CH * tile:CH * (tile + 1)], c["space_back"][:, n // 2, n % 2, 128 * tile:128 * (tile + 1)],
                                      m.gb[:, n % 2, n // 2, b], start=n == 0, stop=n == 3)
                    last.then_inc(S3.inv.pe, 1)

            attention(0)
            spectral1()
            attention(1)
            spectral3()

        @block.scalar
        def _(act):
            run = nc.scalar.activation

            def take_norm(wl, ln, bank0, col):
                for g in range(2):
                    act.wait_ge(ln.var, g + 1)
                    run(m.std[:, 4 * g:4 * g + 4], m.var[:, 4 * g:4 * g + 4], ACT.Sqrt).then_inc(ln.std, 1)
                for g in range(2):
                    act.wait_ge(ln.pe, 2 * g + 1)
                    run(m.yT[:, 0, 512 * g:512 * (g + 1)], m.bank[bank0 + 2 * g][0:HALF, :], ACT.Identity,
                        scale=wl["vecs"][:, col:col + 1], bias=wl["vecs"][:, col + 2:col + 3]).then_inc(ln.act, 1)

            def attention(l):
                s, wl = A[l], w[l]
                act.wait_ge(s.loaded["vecs"], 16)
                take_norm(wl, s.ln[0], 0, 0)
                act.wait_ge(s.qb_scaled, 1)
                act.wait_ge(s.loaded["late"], 16 * 5)
                for j, (kind, g, part, who) in enumerate(PROJ):
                    if who != "act":
                        continue
                    act.wait_ge(s.proj_in.pe, j + 1)
                    bank = m.bank[4 + j % 4]
                    if kind == "q":
                        ins = run(m.qT[:, g, 512 * part:512 * (part + 1)], bank[0:HALF, :], ACT.Identity, scale=HD ** -0.5,
                                  bias=m.qb4[:, l, g:g + 1])
                    elif kind == "rel_h":
                        ins = to_window_order(lambda dst, src: run(dst, src, ACT.Copy), m.relhT[:, g],
                                              bank[0:GROUP * WIN, :].rearrange("k (r b w) -> k b r w", r=8, b=IMAGES), 8 * part, 8 * part + 8)
                    else:
                        if l == 0 and g == 0:
                            act.wait_ge(v_zeroed, 1)
                        ins = run(m.v[0:HALF_WIN, 2 * g:2 * g + 2, :, 0:HD],
                                  bank[0:HALF_WIN, 0:2 * CH].rearrange("k (t h c) -> k t h c", t=2, c=HD), ACT.Copy)
                    ins.then_inc(s.proj_in.act, 1)
                for step in range(N_UNITS + PV_LAG + 1):
                    if step < N_UNITS:
                        b, h = UNITS[step]
                        act.wait_ge(s.max, step + 1)
                        if step >= P_RING:
                            act.wait_ge(s.turn.pe, step - P_RING + 1)
                        bank, slot = m.bank[step % S_RING], step % P_RING
                        if b < IMAGES:
                            for part in range(2):
                                cols = slice(2 * HALF_WIN * part, 2 * HALF_WIN * (part + 1))
                                ins = run(m.probs[0:HALF_WIN, slot, cols], bank[0:HALF_WIN, cols], ACT.Exp,
                                          bias=m.negmax[0:HALF_WIN, slot, part:part + 1], accum_out=m.sums[0:HALF_WIN, slot, part:part + 1])
                        else:
                            e = b - IMAGES
                            n, keys = EDGE_TOKENS[e], EDGE_TOKENS[e] + EDGE_PADS[e][1]
                            ins = run(m.probs[0:n, slot, 0:keys], bank[0:n, 0:keys], ACT.Exp, bias=m.negmax[0:n, slot, 0:1],
                                      accum_out=m.sums[0:n, slot, 0:1])
                        ins.then_inc(s.probs, 1)
                    if TURN_LAG <= step < N_UNITS + TURN_LAG and turned_by(step - TURN_LAG)[0] == "act":
                        u = step - TURN_LAG
                        act.wait_ge(s.turn.pe, u + 1)
                        if u >= T_RING:
                            act.wait_ge(s.pv, (u - T_RING) // 4 + 1)
                        n, cols = turned_size(u)
                        run(m.probsT[0:n, u % T_RING, 0:cols], m.bank[S_RING + u % TURN_RING][0:n, 0:cols], ACT.Copy).then_inc(s.turn.act, 1)
                    for j, burst in enumerate(LAST):
                        if step == 4 * burst + 3 + PV_LAG + 1:
                            act.wait_ge(s.pv, burst + 1)
                            bank, o = m.bank[7], m.oT[:, j % QUADS]
                            bias = wl["cols"][:, HID_TILES + j % QUADS:HID_TILES + j % QUADS + 1]
                            if j < IMAGES * QUADS:
                                ins = run(raster(o)[:, j // QUADS, 0:WIN, 0:WIN], bank[:, 0:2 * HALF_WIN].rearrange("k (r w) -> k r w", r=WIN),
                                          ACT.Identity, bias=bias)
                            else:
                                run(window(o, 0), bank[:, 0:RIGHT].rearrange("k (b r w) -> k b r w", b=IMAGES, r=WIN), ACT.Identity, bias=bias)
                                ins = run(window(o, 1), bank[:, RIGHT:RIGHT + LOW].rearrange("k (b r w) -> k b r w", b=IMAGES, r=EDGE),
                                          ACT.Identity, bias=bias)
                            ins.then_inc(s.oT_out, 1)
                take_norm(wl, s.ln[1], 4, 10)
                for j in range(2 * HID_TILES):
                    g, hid = divmod(j, HID_TILES)
                    act.wait_ge(s.fc1.pe, j + 1)
                    run(m.hidT[:, hid, 512 * g:512 * (g + 1)], m.bank[j % 4][:, :], ACT.Gelu, bias=wl["cols"][:, hid:hid + 1])\
                        .then_inc(s.fc1.act, 1)

            def spectral1():
                for j in range(0, 8, 2):
                    b, half = divmod(j, 2)
                    act.wait_ge(S1.fwd.pe, j + 1)
                    run(m.xf[:, half, :, MODES * b:MODES * (b + 1)], m.bank[j % 4][0:HALF, 0:2 * MODES].rearrange("k (a n) -> k a n", a=2),
                        ACT.Copy, scale=1.0 / SIDE).then_inc(S1.fwd.act, 1)
                for j in range(0, 8, 2):
                    g, half = j // 4, j // 2 % 2
                    act.wait_ge(S1.mlp1.pe, j + 1)
                    run(m.o1[0:HALF, half, 0, 2 * MODES * g:2 * MODES * (g + 1)], m.bank[4 + j % 4][0:HALF, 0:2 * MODES], ACT.Relu,
                        bias=f1.b1[:, 0, half:half + 1]).then_inc(S1.mlp1.act, 1)

            def spectral3():
                for b in range(0, IMAGES, 2):
                    act.wait_ge(S3.flip.pe, b + 1)
                    run(m.an[:, :, MODES * b:MODES * (b + 1)], m.bank[4 + b][0:HALF, 0:2 * MODES].rearrange("k (a n) -> k a n", a=2), ACT.Copy)\
                        .then_inc(S3.flip.act, 1)
                for j in range(8):
                    mix, half = (3, 2, 0, 1)[j % 4], j // 4
                    if mix == 2:
                        continue
                    act.wait_ge(S3.fwd.pe, j + 1)
                    if mix == 3:
                        dst = m.hpart[0:HALF, half, 0:2 * MODES]
                        run(dst, m.bank[j % 4][0:HALF, 0:2 * MODES], ACT.Copy).then_inc(S3.fwd.act, 1)
                    else:
                        run(m.z[:, half, :, 2 * mix], m.bank[j % 4][0:HALF, 0:2 * MODES].rearrange("k (a n) -> k a n", a=2), ACT.Copy)\
                            .then_inc(S3.fwd.act, 1)
                for j in (0, 2):
                    act.wait_ge(S3.chan.pe, j + 1)
                    run(m.ak[:, j // 2, 0:2 * MODES], m.bank[4 + j][0:HALF, 0:2 * MODES], ACT.Copy).then_inc(S3.chan.act, 1)
                for j in range(0, 8, 2):
                    half, g = j // 4, j // 2 % 2
                    act.wait_ge(S3.mlp1.pe, j + 1)
                    run(m.o1n[0:HALF, half, 0, 2 * MODES * g:2 * MODES * (g + 1)], m.bank[j % 4][0:HALF, 0:2 * MODES], ACT.Relu,
                        bias=f3.b[:, 0, 0, half:half + 1]).then_inc(S3.mlp1.act, 1)
                for j in range(4):
                    half, g = divmod(j, 2)
                    act.wait_ge(S3.o2k.pe, j + 1)
                    run(m.o2k[:, half, 2 * MODES * g:2 * MODES * (g + 1)], m.bank[4 + j][0:HALF, 0:2 * MODES], ACT.Identity,
                        bias=f3.b[:, 1, 0, half:half + 1]).then_inc(S3.o2k.act, 1)
                for j in range(8):
                    chunk, mix = j // 4, (3, 2, 0, 1)[j % 4]
                    if mix == 2:
                        continue
                    act.wait_ge(S3.back.pe, j + 1)
                    bank = m.bank[4 + j % 4][0:MCHUNK, 0:2 * CH]
                    if mix == 3:
                        run(m.hpart[0:MCHUNK, chunk, :], bank, ACT.Copy).then_inc(S3.back.act, 1)
                    else:
                        run(m.gb[:, :, chunk, 2 * mix], bank.rearrange("k (a n) -> k a n", a=2), ACT.Copy).then_inc(S3.back.act, 1)

            attention(0)
            spectral1()
            attention(1)
            spectral3()

        @block.vector
        def _(dve):
            def normalise(ln, x_ready, eps):
                for g in range(2):
                    for b in (2 * g, 2 * g + 1):
                        x_ready(b)
                        for tile in range(2):
                            dve.bn_stats(m.stats[:, 2 * b + tile], m.x[:, b, tile]).then_inc(ln.stats, 1)
                    dve.wait_ge(ln.stats, 4 * g + 4)
                    for i in range(4 * g, 4 * g + 4):
                        dve.bn_aggr(m.meanvar[:, i], m.stats[:, i]).then_inc(ln.mean, 1)
                    dve.wait_ge(ln.mean, 4 * g + 4)
                    dve.tensor_scalar(m.var[:, 4 * g:4 * g + 4], m.meanvar[:, 4 * g:4 * g + 4, 1], eps, None, ALU.add).then_inc(ln.var, 1)
                    dve.wait_ge(ln.std, g + 1)
                    dve.reciprocal(m.rstd[:, 4 * g:4 * g + 4], m.std[:, 4 * g:4 * g + 4]).then_inc(ln.rstd, 1)
                    dve.wait_ge(ln.rstd, g + 1)
                    for i in range(4 * g, 4 * g + 4):
                        dve.tensor_scalar(m.xn[:, i], m.x[:, i // 2, i % 2], m.meanvar[:, i, 0:1], m.rstd[:, i:i + 1],
                                          ALU.subtract, ALU.mult).then_inc(ln.done, 1)

            def take_norm(wl, ln, bank0, col):
                for g in range(2):
                    dve.wait_ge(ln.pe, 2 * g + 2)
                    dve.tensor_scalar(m.yT[:, 1, 512 * g:512 * (g + 1)], m.bank[bank0 + 2 * g + 1][0:HALF, :],
                                      wl["vecs"][:, col + 1:col + 2], wl["vecs"][:, col + 3:col + 4], ALU.mult, ALU.add).then_inc(ln.dve, 1)

            def attention(l, x_ready):
                s, wl = A[l], w[l]
                normalise(s.ln[0], x_ready, EPS[l])
                dve.wait_ge(s.loaded["vecs"], 16)
                dve.tensor_scalar(m.qb4[:, l], wl["vecs"][:, 4:6], HD ** -0.5, None, ALU.mult).then_inc(s.qb_scaled, 1)
                take_norm(wl, s.ln[0], 0, 0)
                for j, (kind, g, part, who) in enumerate(PROJ):
                    if who != "dve":
                        continue
                    dve.wait_ge(s.proj_in.pe, j + 1)
                    bank = m.bank[4 + j % 4]
                    if kind == "k":
                        ins = dve.tensor_scalar(m.kT[:, g, 512 * part:512 * (part + 1)], bank[0:HALF, :], wl["vecs"][:, 6 + g:7 + g], None, ALU.add)
                    elif kind == "rel_w":
                        ins = to_window_order(dve.tensor_copy, m.relwT[:, g],
                                              bank[0:GROUP * WIN, :].rearrange("k (w b r) -> k b r w", w=SIDE, b=IMAGES), 8 * part, 8 * part + 8)
                    elif g < IMAGES:
                        if l == 0 and g == 1:
                            dve.wait_ge(v_zeroed, 1)
                        ins = dve.tensor_copy(m.v[0:HALF_WIN, 2 * g:2 * g + 2, :, 0:HD],
                                              bank[0:HALF_WIN, 0:2 * CH].rearrange("k (t h c) -> k t h c", t=2, c=HD))
                    else:
                        for e in range(2):
                            n = EDGE_TOKENS[e]
                            ins = dve.tensor_copy(m.v[0:n, 2 * IMAGES + e, :, 0:HD],
                                                  bank[0:n, CH * e:CH * (e + 1)].rearrange("k (h c) -> k h c", c=HD))
                    ins.then_inc(s.proj_in.dve, 1)
                for step in range(N_UNITS + TURN_LAG):
                    if step < N_UNITS:
                        b, h = UNITS[step]
                        dve.wait_ge(s.scores, step + 1)
                        bank, slot = m.bank[step % S_RING], step % P_RING
                        if b < IMAGES:
                            ins = dve.tensor_reduce(m.negmax[0:HALF_WIN, slot], bank[0:HALF_WIN, 0:4 * HALF_WIN].rearrange("k (a n) -> k a n", a=2),
                                                    AX, ALU.max, negate=True)
                        else:
                            n, keys = EDGE_TOKENS[b - IMAGES], EDGE_TOKENS[b - IMAGES] + EDGE_PADS[b - IMAGES][1]
                            ins = dve.tensor_reduce(m.negmax[0:n, slot, 0:1], bank[0:n, 0:keys], AX, ALU.max, negate=True)
                        ins.then_inc(s.max, 1)
                    if 1 <= step < N_UNITS + 1:
                        u = step - 1
                        n, parts = turned_size(u)[0], 2 if UNITS[u][0] < IMAGES else 1
                        dve.wait_ge(s.probs, u + 1)
                        dve.reciprocal(m.recip[0:n, u % P_RING, 0:parts], m.sums[0:n, u % P_RING, 0:parts]).then_inc(s.recip, 1)
                    if step >= TURN_LAG and turned_by(step - TURN_LAG)[0] == "dve":
                        u = step - TURN_LAG
                        dve.wait_ge(s.turn.pe, u + 1)
                        if u >= T_RING:
                            dve.wait_ge(s.pv, (u - T_RING) // 4 + 1)
                        n, cols = turned_size(u)
                        dve.tensor_copy(m.probsT[0:n, u % T_RING, 0:cols], m.bank[S_RING + u % TURN_RING][0:n, 0:cols]).then_inc(s.turn.dve, 1)
                for b in range(IMAGES):
                    dve.wait_ge(s.out_proj.pe, b + 1)
                    dve.wait_ge(s.bias_added, b + 1)
                    dve.tensor_tensor(m.x[:, b], m.bank[b][:, 0:2 * CH].rearrange("k (t c) -> k t c", t=2), m.xb[:, b], ALU.add)\
                       .then_inc(s.out_proj.dve, 1)
                normalise(s.ln[1], lambda b: dve.wait_ge(s.out_proj.dve, b + 1), EPS[l])
                take_norm(wl, s.ln[1], 4, 10)
                for b in range(IMAGES):
                    dve.wait_ge(s.fc2.pe, b + 1)
                    dve.wait_ge(s.bias_added, IMAGES + b + 1)
                    dve.tensor_tensor(m.x[:, b], m.bank[4 + b][:, 0:2 * CH].rearrange("k (t c) -> k t c", t=2), m.xb[:, b], ALU.add)\
                       .then_inc(s.fc2.dve, 1)

            def spectral1():
                dve.memset(m.o1[HALF:HALF + 1, :, 0], 1.0).then_inc(o1_ones_set, 1)
                for j in range(1, 8, 2):
                    b, half = divmod(j, 2)
                    dve.wait_ge(S1.fwd.pe, j + 1)
                    dve.tensor_scalar(m.xf[:, half, :, MODES * b:MODES * (b + 1)],
                                      m.bank[j % 4][0:HALF, 0:2 * MODES].rearrange("k (a n) -> k a n", a=2),
                                      1.0 / SIDE, None, ALU.mult).then_inc(S1.fwd.dve, 1)
                for j in range(1, 8, 2):
                    g, half = j // 4, j // 2 % 2
                    dve.wait_ge(S1.mlp1.pe, j + 1)
                    dve.tensor_scalar(m.o1[0:HALF, half, 1, 2 * MODES * g:2 * MODES * (g + 1)], m.bank[4 + j % 4][0:HALF, 0:2 * MODES],
                                      f1.b1[:, 1, half:half + 1], 0.0, ALU.add, ALU.max).then_inc(S1.mlp1.dve, 1)
                for j in range(8):
                    b, part = divmod(j, 2)
                    dve.wait_ge(S1.mlp2.pe, j + 1)
                    bank = m.bank[j % 4][0:MCHUNK, 0:2 * CH]
                    dve.tensor_scalar(m.clip1[:, j % 2], bank, -LAMBDA, LAMBDA, ALU.max, ALU.min).then_inc(S1.clipped, 1)
                    dve.wait_ge(S1.clipped, j + 1)
                    dve.tensor_tensor(m.o2[:, part, :, b], bank.rearrange("k (a n) -> k a n", a=2),
                                      m.clip1[:, j % 2].rearrange("k (a n) -> k a n", a=2), ALU.subtract).then_inc(S1.mlp2.dve, 1)
                for b in range(IMAGES):
                    dve.wait_ge(S1.inv.pe, b + 1)
                    dve.tensor_tensor(m.x[:, b], m.bank[4 + b][:, 0:2 * CH].rearrange("k (t c) -> k t c", t=2), m.x[:, b], ALU.add)\
                       .then_inc(S1.inv.dve, 1)

            def unmix(dst, g, h, stage_sem):
                dve.tensor_tensor(dst(0, 1), g[0], h[1], ALU.add)
                dve.tensor_tensor(dst(1, 1), g[1], h[0], ALU.subtract)
                dve.tensor_tensor(dst(0, 3), g[0], h[1], ALU.subtract)
                dve.tensor_tensor(dst(1, 3), g[1], h[0], ALU.add).then_inc(stage_sem, 1)

            def spectral3():
                dve.wait_ge(A[1].fc2.dve, IMAGES)
                dve.tensor_tensor(m.mix[:, 2:4], m.x[:, 0:2], m.x[:, 2:4], ALU.subtract).then_inc(S3.mixed, 1)
                dve.tensor_tensor(m.ef[:], m.x[:, 0:2], m.x[:, 2:4], ALU.add).then_inc(S3.ef, 1)
                dve.wait_ge(S3.ef, 1)
                dve.tensor_tensor(m.mix[:, 0], m.ef[:, 0], m.ef[:, 1], ALU.add).then_inc(S3.mixed, 1)
                dve.tensor_tensor(m.mix[:, 1], m.ef[:, 0], m.ef[:, 1], ALU.subtract).then_inc(S3.mixed, 1)
                for b in range(1, IMAGES, 2):
                    dve.wait_ge(S3.flip.pe, b + 1)
                    dve.tensor_copy(m.an[:, :, MODES * b:MODES * (b + 1)], m.bank[4 + b][0:HALF, 0:2 * MODES].rearrange("k (a n) -> k a n", a=2))\
                       .then_inc(S3.flip.dve, 1)
                for half in range(2):
                    dve.wait_ge(S3.fwd.pe, 4 * half + 2)
                    dve.wait_ge(S3.fwd.act, 3 * half + 1)
                    g = m.bank[1][0:HALF, 0:2 * MODES].rearrange("k (a n) -> k a n", a=2)
                    h = m.hpart[0:HALF, half, 0:2 * MODES].rearrange("k (a n) -> k a n", a=2)
                    unmix(lambda part, b: m.z[:, half, part, b], (g[:, 0], g[:, 1]), (h[:, 0], h[:, 1]), S3.fwd.dve)
                for j in (1, 3):
                    dve.wait_ge(S3.chan.pe, j + 1)
                    dve.tensor_copy(m.ak[:, j // 2, 2 * MODES:4 * MODES], m.bank[4 + j][0:HALF, 0:2 * MODES]).then_inc(S3.chan.dve, 1)
                for j in range(1, 8, 2):
                    half, g = j // 4, j // 2 % 2
                    dve.wait_ge(S3.mlp1.pe, j + 1)
                    dve.tensor_scalar(m.o1n[0:HALF, half, 1, 2 * MODES * g:2 * MODES * (g + 1)], m.bank[j % 4][0:HALF, 0:2 * MODES],
                                      f3.b[:, 0, 1, half:half + 1], 0.0, ALU.add, ALU.max).then_inc(S3.mlp1.dve, 1)
                for j in range(4):
                    half, g = divmod(j, 2)
                    cols = slice(2 * MODES * g, 2 * MODES * (g + 1))
                    dve.wait_ge(S3.o2nk.pe, j + 1)
                    dve.scalar_tensor_tensor(m.s[:, half, cols], m.bank[j][0:HALF, 0:2 * MODES], f3.b[:, 1, 1, half:half + 1],
                                             m.o2k[:, half, cols], ALU.add, ALU.add).then_inc(S3.s, 1)
                dve.wait_ge(S3.s, 4)
                dve.tensor_scalar(m.clip3[:], m.s[:], -LAMBDA, LAMBDA, ALU.max, ALU.min).then_inc(S3.clipped, 1)
                dve.wait_ge(S3.clipped, 1)
                dve.tensor_tensor(m.s[:], m.s[:], m.clip3[:], ALU.subtract).then_inc(S3.shrunk, 1)
                dve.wait_ge(S3.shrunk, 1)
                sv = m.s.rearrange("k d (b n) -> k d b n", b=IMAGES)
                dve.tensor_tensor(m.hs[:, :, 2:4], sv[:, :, 0:2], sv[:, :, 2:4], ALU.subtract).then_inc(S3.hs, 1)
                dve.tensor_tensor(m.hef[:], sv[:, :, 0:2], sv[:, :, 2:4], ALU.add).then_inc(S3.hef, 1)
                dve.wait_ge(S3.hef, 1)
                dve.tensor_tensor(m.hs[:, :, 0], m.hef[:, :, 0], m.hef[:, :, 1], ALU.add).then_inc(S3.hs, 1)
                dve.tensor_tensor(m.hs[:, :, 1], m.hef[:, :, 0], m.hef[:, :, 1], ALU.subtract).then_inc(S3.hs, 1)
                for chunk in range(2):
                    dve.wait_ge(S3.back.pe, 4 * chunk + 2)
                    dve.wait_ge(S3.back.act, 3 * chunk + 1)
                    g, h = m.bank[5][0:MCHUNK, :], m.hpart[0:MCHUNK, chunk]
                    unmix(lambda part, b: m.gb[:, part, chunk, b], (g[:, 0:CH], g[:, CH:2 * CH]), (h[:, 0:CH], h[:, CH:2 * CH]), S3.back.dve)
                for b in range(IMAGES):
                    dve.wait_ge(S3.inv.pe, b + 1)
                    dve.scalar_tensor_tensor(m.xb[:, b], m.bank[b][:, 0:2 * CH].rearrange("k (t c) -> k t c", t=2),
                                             1.0 / (TOKENS * CH), m.x[:, b], ALU.mult, ALU.add).then_inc(S3.inv.dve, 1)

            attention(0, lambda b: dve.wait_ge(x_loaded[b], 16))
            spectral1()
            attention(1, lambda b: dve.wait_ge(S1.inv.dve, b + 1))
            spectral3()


def _halves(v):
    return v.reshape(2, HALF).T


def _block_diagonal(blocks):
    n = blocks.shape[-1]
    out = np.zeros((HALF, 2, HALF), blocks.dtype)
    for i in range(8):
        lo = n * (i % 4)
        out[lo:lo + n, i // 4, lo:lo + n] = blocks[i]
    return out


def _laid_out(a):
    out = {"x": a["x"]}
    names = [("norm1_scale", "norm1_bias", "norm2_scale", "norm2_bias"), ("ln1_w", "ln1_b", "ln2_w", "ln2_b")]
    for l, (layer, (s1, b1, s2, b2)) in enumerate(zip(("L0_conv_", "L2_conv_"), names)):
        g = lambda n: a[layer + n]
        qb, kb, vb = g("qkv_b").reshape(3, CH)
        out[f"vecs{l}"] = np.concatenate([_halves(v) for v in (g(s1), g(b1), qb, kb, vb, g(s2), g(b2))], 1)
        out[f"qkv{l}"] = g("qkv_w").reshape(2, HALF, 3 * CH).transpose(1, 0, 2)
        rel = np.zeros((HALF, 2, 2 * WIN - 1, GROUP), np.float32)
        for n, table in enumerate((g("rel_pos_h"), g("rel_pos_w"))):
            for h in range(GROUP):
                rel[HD * h:HD * (h + 1), n, :, h] = table[::-1].T
        out[f"rel{l}"] = rel.reshape(HALF, 2, -1)
        cols = np.zeros((128, HID_TILES + QUADS), np.float32)
        cols[:, :HID_TILES] = g("fc1_b").reshape(HID_TILES, 128).T
        proj = np.zeros((128, QUADS, CH), np.float32)
        for h in range(HEADS):
            at, c = 32 * (h % 4), slice(HD * h, HD * (h + 1))
            cols[at:at + HD, HID_TILES + h // 4] = vb[c]
            proj[at:at + HD, h // 4] = g("proj_w")[c]
        out[f"cols{l}"] = cols
        out[f"rows{l}"] = np.broadcast_to(np.stack([g("proj_b"), g("fc2_b")]), (128, 2, CH))
        out[f"proj{l}"] = proj
        out[f"fc1{l}"] = g("fc1_w").reshape(2, HALF, HID).transpose(1, 0, 2)
        out[f"fc2{l}"] = g("fc2_w").reshape(HID_TILES, 128, CH).transpose(1, 0, 2)
    w1, w2 = a["L1_conv_w1"], a["L1_conv_w2"]
    out["f1_w1"] = np.stack([_block_diagonal(w1[..., i]) for i in range(2)], 1)
    out["f1_b1"] = np.stack([_halves(a["L1_conv_b1"][..., i].reshape(-1)) for i in range(2)], 1)
    f1_w2 = np.zeros((HALF + 1, 2, 2, HALF), np.float32)
    for i in range(2):
        f1_w2[:HALF, i] = _block_diagonal(w2[..., i])
        f1_w2[HALF, i] = a["L1_conv_b2"][..., i].reshape(2, HALF)
    out["f1_w2"] = f1_w2
    out["f3_w"] = np.stack([np.stack([_block_diagonal(a[f"L3_conv_{n}"][i]).reshape(HALF, 2 * HALF) for i in range(2)], 1)
                            for n in ("w1", "w2")], 1)
    out["f3_b"] = np.stack([np.stack([_halves(a[f"L3_conv_{n}"][i].reshape(-1)) for i in range(2)], 1)
                            for n in ("b1", "b2")], 1)
    return out


def kernel(**inputs):
    import concourse.bacc as bacc
    from concourse.bass_utils import run_bass_kernel_spmd

    nc = bacc.Bacc("TRN2", target_bir_lowering=False, num_devices=1)
    laid = _laid_out({k: np.asarray(v) for k, v in inputs.items()})
    laid.update(constants())
    arrays, args = {}, {}
    for name, a in laid.items():
        a = np.ascontiguousarray(a)
        arrays[f"in_{name}"] = a
        args[name] = nc.dram_tensor(f"in_{name}", a.shape, mybir.dt.from_np(a.dtype), kind="ExternalInput").ap()
    out = nc.dram_tensor("out", (IMAGES, SIDE, SIDE, CH), F32, kind="ExternalOutput").ap()
    build(nc, args, out)
    result = run_bass_kernel_spmd(nc, [arrays], core_ids=[0])
    return result.results[0]["out"]
```

```python
from contextlib import ExitStack

import numpy as np
import concourse.bass as bass
from concourse import mybir

F32 = mybir.dt.float32
ALU = mybir.AluOpType
ACT = mybir.ActivationFunctionType
AX = mybir.AxisListType.X

IMAGES, SIDE, CH = 4, 16, 192
WIN = 14
EDGE = SIDE - WIN
PLACES = SIDE * SIDE
TOKENS = IMAGES * PLACES
TILES = TOKENS // 128
HALF = CH // 2
HEADS, HD = 12, 16
QUADS = HEADS // 4
O_TILES = (QUADS + 1) // 2
QK_CHUNKS = 2 * CH // 128
REL_HEADS = (8, 4)
HID = 4 * CH
HID_TILES = HID // 128
CODES = 2 * IMAGES
BIAS_ROW = 4 * HD
CODE_ROW = BIAS_ROW + 2 * WIN
AUG = CODE_ROW + CODES
PAD_RIGHT = WIN * (WIN - EDGE)
PAD_LOW = PAD_RIGHT + EDGE * (WIN - EDGE)
KEYS = TOKENS + PAD_RIGHT + PAD_LOW
HW_ROWS = WIN // 2
HALF_WIN = HW_ROWS * WIN
MAIN = IMAGES * WIN * WIN
RIGHT = IMAGES * WIN * EDGE
LOW = IMAGES * EDGE * SIDE
BIG = 1e30
HALF_COLS = SIDE // 2 + 1
MODES = SIDE * HALF_COLS
MCHUNK = MODES // 2
FULL = 128
LEFT = MODES - FULL
LEFT_AT = IMAGES * FULL
OUT_ORDER = (1, 3, 0, 2)
LAMBDA = 0.01
EPS = (1e-6, 1e-5)
WARM_UPS = 3


def _places():
    h, w = np.divmod(np.arange(PLACES), SIDE)
    return h, w


def _key_rows():
    out = np.zeros((2 * WIN + CODES, KEYS), np.float32)
    h, w = _places()
    for b in range(IMAGES):
        at = b * PLACES + np.arange(PLACES)
        out[h % WIN, at] = 4.0
        out[WIN + w % WIN, at] = 4.0
        for code in range(CODES):
            right = (h < WIN) & (w >= WIN)
            low = (h >= WIN) & (w < WIN)
            corner = (h >= WIN) & (w >= WIN)
            other = (right & (code != b) & (code < IMAGES)) | (low & (code != b)) | (corner & (code != IMAGES + b))
            out[2 * WIN + code, at[other]] = -BIG
    pads = [(i, j) for i in range(WIN) for j in range(EDGE, WIN)]
    pads += [(i, j) for i in range(EDGE, WIN) for j in range(WIN)]
    pads += [(i, j) for i in range(EDGE) for j in range(EDGE, WIN)]
    for n, (i, j) in enumerate(pads):
        out[i, TOKENS + n] = 4.0
        out[WIN + j, TOKENS + n] = 4.0
    out[2 * WIN:2 * WIN + IMAGES, TOKENS + 2 * PAD_RIGHT:] = -BIG
    return out


def _query_codes():
    out = np.zeros((CODES, TOKENS), np.float32)
    for b in range(IMAGES):
        out[b, MAIN + b * WIN * EDGE:MAIN + (b + 1) * WIN * EDGE] = 1.0
        for r in range(EDGE):
            at = MAIN + RIGHT + (EDGE * b + r) * SIDE
            out[b, at:at + WIN] = 1.0
            out[IMAGES + b, at + WIN:at + SIDE] = 1.0
    return out


def _by_modes(table, left):
    out = np.zeros((128, 2 + IMAGES, PLACES))
    out[:, 0:2] = table[:, :FULL].transpose(1, 0, 2)
    for b, rows in enumerate(left):
        for (part, k), (sign, src) in rows.items():
            at = LEFT * (IMAGES * part + k)
            out[at:at + LEFT, 2 + b] = sign * table[src, FULL:]
    return out


def constants():
    h, w = _places()
    kh, kw = np.divmod(np.arange(MODES), HALF_COLS)
    kh = np.r_[0, SIDE // 2 + 1:SIDE, 1:SIDE // 2 + 1][kh]
    theta = 2 * np.pi * (np.outer(h, kh) + np.outer(w, kw)) / SIDE
    space = np.stack([np.cos(theta), -np.sin(theta)], 1)
    back = np.stack([np.cos(theta) - np.sin(theta), np.cos(theta) + np.sin(theta)], 1)
    flip = np.zeros((PLACES, MODES))
    flip[((-kh) % SIDE) * SIDE + (-kw) % SIDE, np.arange(MODES)] = 1.0
    spec = np.zeros((2 * MODES, SIDE, HALF_COLS), complex)
    spec[np.arange(MODES), kh, kw] = 1.0
    spec[MODES + np.arange(MODES), kh, kw] = 1j
    inverse = _by_modes(np.fft.irfft2(spec, s=(SIDE, SIDE), norm="ortho").reshape(2, MODES, PLACES),
                        [{(part, b): (1, part) for part in range(2)} for b in range(IMAGES)])
    back = _by_modes(back.transpose(1, 2, 0),
                     [{(0, 0): (1, 0), (1, 0): (1, 1)},
                      {(0, 2): (1, 0), (1, 2): (1, 1), (1, 3): (1, 0), (0, 3): (-1, 1)},
                      {(0, 1): (1, 0), (1, 1): (1, 1)},
                      {(0, 2): (1, 0), (1, 2): (1, 1), (1, 3): (-1, 0), (0, 3): (1, 1)}])
    phi = 2 * np.pi * np.outer(np.arange(CH), np.arange(CH)) / CH
    c, s = np.cos(phi), np.sin(phi)
    chan = np.stack([c - s, c + s], 1).reshape(2, HALF, 2, CH)
    chan_back = np.concatenate([c, -s], 1).reshape(2, HALF, 2 * CH)
    made = {
        "space_fwd": space.reshape(2, 128, 2 * MODES).transpose(1, 0, 2),
        "flip": np.stack([flip.reshape(2, 128, 2, MCHUNK)[tile, :, tile] for tile in range(2)], 1),
        "inverse": inverse,
        "space_back": back,
        "chan_fwd": chan.transpose(1, 0, 2, 3),
        "chan_back": chan_back.transpose(1, 0, 2),
        "ident": np.eye(128),
        "key_rows": _key_rows(),
        "query_codes": _query_codes(),
    }
    return {k: np.ascontiguousarray(v, np.float32) for k, v in made.items()}


PROJ = [("qk", 0, 0, "act"), ("qk", 1, 0, "dve"), ("qk", 2, 0, "dve"), ("qk", 0, 1, "act"), ("qk", 1, 1, "dve"), ("qk", 2, 1, "act")]
PROJ += [("rel_h", 0, 0, "act"), ("rel_h", 0, 1, "act"), ("rel_w", 0, 0, "dve"), ("rel_w", 0, 1, "dve")]
PROJ += [("rel_h", 1, 0, "act"), ("rel_w", 1, 0, "dve"), ("rel_h", 1, 1, "act"), ("rel_w", 1, 1, "dve")]
PROJ += [("v", 0, 0, "act"), ("v", 1, 0, "dve"), ("v", 2, 0, "act"), ("v", 3, 0, "dve"), ("v", 4, 0, "dve")]


def taken_out(j):
    who = PROJ[j][3]
    return who, sum(p[3] == who for p in PROJ[:j + 1])


def job(kind, group, part):
    return [p[:3] for p in PROJ].index((kind, group, part))


UNITS = [(IMAGES + s, 4 * q + n) for q in range(QUADS) for s in range(2) for n in range(4)]
UNITS += [(b, h) for b in range(IMAGES) for h in range(HEADS)]
N_UNITS = len(UNITS)
S_RING = 4
TURN_RING = 3
P_RING = 5
T_RING = 8
TURN_LAG = 4
PV_LAG = 8


def o_job(u):
    b, h = UNITS[u]
    return (0 if b >= IMAGES else b + 1) * O_TILES + h // 8


LAST = [max(u // 4 for u in range(N_UNITS) if o_job(u) == j) for j in range((IMAGES + 1) * O_TILES)]


def turned_by(u):
    return "dve" if u % 2 == 0 else "act", u // 2 + 1


class Named:
    pass


def build(nc, t, out):
    ctx = ExitStack()
    with ctx:
        def sb(name, shape):
            return ctx.enter_context(nc.sbuf_tensor(name, shape, F32))

        def sem(name):
            return ctx.enter_context(nc.semaphore(name))

        m = Named()
        m.bank = [ctx.enter_context(nc.psum_tensor(f"bank{i}", [128, 512], F32)) for i in range(8)]
        m.qaug = sb("qaug", [128, HEADS, TOKENS])
        m.kaug = sb("kaug", [AUG, QUADS, KEYS])
        m.x = sb("x_tok", [128, IMAGES, 2, CH])
        m.xb = sb("x_plus_bias", [128, IMAGES, 2, CH])
        m.yT = sb("yT", [HALF, 2, TOKENS])
        m.norm_q = sb("norm_or_q", [128, 2 * TOKENS])
        m.xn = m.norm_q[:, 0:TILES * CH].rearrange("p (i c) -> p i c", c=CH)
        m.qW = m.norm_q[:, :].rearrange("p (a n) -> p a n", a=2)
        m.probs = sb("probs", [128, P_RING, 4 * HALF_WIN])
        m.probsT = sb("probsT", [128, T_RING, 4 * HALF_WIN])
        m.v = sb("v_padded", [128, 2 * IMAGES + 2, HEADS, 32])
        m.v_cols = m.v[:, :, :, :].rearrange("p k h c -> p k (h c)")
        m.stats = sb("stats", [128, TILES, 6])
        m.meanvar = sb("meanvar", [128, TILES, 2])
        m.var, m.std, m.rstd = (sb(n, [128, TILES]) for n in ("var_eps", "std", "rstd"))
        m.negmax = sb("negmax", [128, P_RING, 2])
        m.sums = sb("sums", [128, P_RING, 2])
        m.recip = sb("recip", [128, P_RING, 2])
        m.qk_scale = sb("qk_scale", [128, QK_CHUNKS])
        m.qk_bias = sb("qk_bias", [128, 2, QK_CHUNKS])
        m.spare = sb("spare", [128, 2])
        m.yW = m.probsT[0:HALF].rearrange("p a n -> p (a n)")[:, 0:2 * TOKENS].rearrange("p (a n) -> p a n", a=2)
        arena = sb("arena", [128, QK_CHUNKS * KEYS + 4 * TOKENS])

        def carve(base, at, rows, *dims):
            n = int(np.prod(dims))
            view = base[0:rows, at:at + n]
            names = "abcde"[:len(dims)]
            if len(dims) > 1:
                view = view.rearrange(f"p ({' '.join(names)}) -> p {' '.join(names)}",
                                      **{k: d for k, d in zip(names, dims)})
            return view, at + n

        m.qkT, at = carve(arena, 0, 128, QK_CHUNKS, KEYS)
        m.relhT, at = carve(arena, at, REL_HEADS[0] * WIN, 2, TOKENS)
        m.relwT, at = carve(arena, at, 128, 2, TOKENS)
        m.oT, at = carve(arena, 0, 128, O_TILES, TOKENS)
        m.hidT, _ = carve(arena, at, 128, HID_TILES, TOKENS)
        m.xf, at = carve(arena, 0, HALF, 2, 2, IMAGES * MODES)
        m.o2, at = carve(arena, at, 128, 2, IMAGES, CH)
        m.o2_left, at = carve(arena, at, 128, CH)
        m.clip1, at = carve(arena, at, 128, 2, 2 * CH)
        m.o1, at = carve(arena, at, HALF + 1, 2, 2, IMAGES * MODES)
        m.mix, at = carve(arena, 0, 128, 4, 2, CH)
        m.ef, at = carve(arena, at, 128, 2, 2, CH)
        m.hpart, at = carve(arena, at, 128, 2, 2 * CH)
        m.z, at = carve(arena, at, HALF, 2, 2, IMAGES, MODES)
        m.an, at = carve(arena, at, HALF, 2, IMAGES * MODES)
        m.ak, at = carve(arena, at, HALF, 2, IMAGES * MODES)
        qflat = m.qaug[:, :, :].rearrange("p a b -> p (a b)")
        m.o1n, at = carve(qflat, 0, HALF, 2, 2, IMAGES * MODES)
        m.o2k, at = carve(qflat, at, HALF, 2, IMAGES * MODES)
        m.s, at = carve(qflat, at, HALF, 2, IMAGES * MODES)
        m.clip3, at = carve(qflat, at, HALF, 2, IMAGES * MODES)
        m.hs, at = carve(qflat, at, HALF, 2, IMAGES * MODES)
        m.hef, at = carve(qflat, at, HALF, 2, 2, MODES)
        m.gb, at = carve(qflat, at, 128, 2, IMAGES, CH)
        m.gb_left, at = carve(qflat, at, 128, CH)

        c = {name: sb(name, list(t[name].shape))
             for name in ("space_fwd", "flip", "inverse", "chan_fwd", "chan_back", "ident")}
        c["space_back"] = c["inverse"]
        w = [{}, {}]
        ATT = ("vecs", "qkv", "rel8", "rel4", "cols", "rows", "proj", "fc1", "fc2")
        for l in range(2):
            for name in ATT:
                shared = l == 1 and name in ("qkv", "rel8", "rel4", "rows", "proj", "fc1", "fc2")
                w[l][name] = w[0][name] if shared else sb(f"{name}{l}", list(t[f"{name}{l}"].shape))
        f1, f3 = Named(), Named()
        f1.w1 = sb("f1_w1", [HALF, 3, 2, HALF])
        f1.b1 = sb("f1_b1", [HALF, 2, 2])
        f1.w2 = sb("f1_w2", [HALF + 1, 4, 2, HALF])
        f3.w = sb("f3_w", [HALF, 2, 2, 2 * HALF])
        f3.mixw = sb("f3_mixw", [HALF, 2, 2, 2 * HALF])
        f3.b = sb("f3_b", [HALF, 2, 2, 2])

        x_loaded = [sem(f"x_loaded{b}") for b in range(IMAGES)]
        ident_loaded = sem("ident_loaded")
        aug_rows_loaded = sem("aug_rows_loaded")
        spectral_loaded = sem("spectral_loaded")
        spare_set, ones_set, scale_set = sem("spare_set"), sem("ones_set"), sem("scale_set")
        v_zeroed, q_zeroed = sem("v_zeroed"), sem("q_zeroed")
        o1_ones_set = sem("o1_ones_set")
        space_back_loaded = sem("space_back_loaded")
        weights_mixed = sem("weights_mixed")
        stored = sem("stored")

        def stage(name, takers="act dve"):
            s = Named()
            s.pe = sem(f"{name}_pe")
            s.act = sem(f"{name}_act") if "act" in takers else None
            s.dve = sem(f"{name}_dve") if "dve" in takers else None
            return s

        def attention_sems(l):
            s = Named()
            s.loaded = {n: sem(f"{n}{l}_loaded") for n in ("vecs", "qkv", "rel", "late")}
            s.proj_in, s.out_proj = stage(f"proj_in{l}"), stage(f"out_proj{l}", "dve")
            s.fc1, s.fc2 = stage(f"fc1{l}", "act"), stage(f"fc2{l}", "dve")
            s.ln = []
            for k in range(2):
                n = stage(f"ln{l}_{k}")
                n.stats, n.mean, n.var, n.std, n.rstd, n.done = (sem(f"ln{l}_{k}_{q}") for q in ("stats", "mean", "var", "std", "rstd", "done"))
                s.ln.append(n)
            s.bias_scaled, s.kpad_set, s.bias_added = sem(f"bias_scaled{l}"), sem(f"kpad_set{l}"), sem(f"bias_added{l}")
            s.y_ordered = sem(f"y_ordered{l}")
            s.aug_bias = [sem(f"aug_bias{l}_{g}") for g in range(2)]
            s.aug = [sem(f"aug{l}_{q}") for q in range(QUADS)]
            s.scores, s.max, s.probs = sem(f"scores{l}"), sem(f"max{l}"), sem(f"probs{l}")
            s.recip, s.normed, s.pv, s.oT_out = sem(f"recip{l}"), sem(f"normed{l}"), sem(f"pv{l}"), sem(f"oT_out{l}")
            s.turn = stage(f"turn{l}")
            return s

        A = [attention_sems(0), attention_sems(1)]
        S1 = Named()
        S1.fwd, S1.mlp1 = stage("s1_fwd"), stage("s1_mlp1")
        S1.mlp2, S1.inv = stage("s1_mlp2", "dve"), stage("s1_inv", "dve")
        S1.clipped = sem("s1_clipped")
        S3 = Named()
        S3.fwd, S3.flip, S3.chan, S3.mlp1 = stage("s3_fwd"), stage("s3_flip"), stage("s3_chan"), stage("s3_mlp1")
        S3.o2k, S3.o2nk = stage("s3_o2k", "act"), stage("s3_o2nk", "dve")
        S3.back, S3.inv = stage("s3_back"), stage("s3_inv", "dve")
        S3.mixed, S3.ef, S3.s, S3.clipped = sem("s3_mixed"), sem("s3_ef"), sem("s3_s"), sem("s3_clipped")
        S3.shrunk, S3.hef, S3.hs = sem("s3_shrunk"), sem("s3_hef"), sem("s3_hs")

        def raster(ap):
            return ap.rearrange("k (b r w) -> k b r w", b=IMAGES, r=SIDE)

        def main(ap):
            return ap[:, 0:MAIN].rearrange("k (b r w) -> k b r w", b=IMAGES, r=WIN)

        def right(ap):
            return ap[:, MAIN:MAIN + RIGHT].rearrange("k (b r w) -> k b r w", b=IMAGES, r=WIN)

        def low(ap):
            return ap[:, MAIN + RIGHT:TOKENS].rearrange("k (b r w) -> k b r w", b=IMAGES, r=EDGE)

        def to_window_order(copy, dst, src, lo, hi):
            top = min(hi, WIN)
            copy(main(dst)[:, :, lo:top], src[:, :, 0:top - lo, 0:WIN])
            last = copy(right(dst)[:, :, lo:top], src[:, :, 0:top - lo, WIN:SIDE])
            return copy(low(dst), src[:, :, top - lo:hi - lo, :]) if hi > WIN else last

        def to_window_columns(copy, dst, src, lo, hi):
            left = min(hi, WIN)
            copy(main(dst)[:, :, :, lo:left], src[:, :, 0:WIN, 0:left - lo])
            if hi > WIN:
                copy(right(dst), src[:, :, 0:WIN, left - lo:hi - lo])
            return copy(low(dst)[:, :, :, lo:hi], src[:, :, WIN:SIDE, :])

        def window(ap, s):
            return raster(ap)[:, :, 0:WIN, WIN:SIDE] if s == 0 else raster(ap)[:, :, WIN:SIDE, :]

        EDGE_TOKENS = (RIGHT, LOW)
        EDGE_AT = (MAIN, MAIN + RIGHT)
        EDGE_PADS = ((TOKENS, PAD_RIGHT), (TOKENS + PAD_RIGHT, PAD_LOW))

        def turned_size(u):
            b = UNITS[u][0]
            return (HALF_WIN, 4 * HALF_WIN) if b < IMAGES else (EDGE_TOKENS[b - IMAGES], EDGE_TOKENS[b - IMAGES])

        def wait_for(eng, st, who, n):
            eng.wait_ge(st.act if who == "act" else st.dve, n)

        S1_COLS = (slice(0, 2 * FULL), slice(2 * FULL, IMAGES * MODES))
        S1_MLP2 = (0, 1, IMAGES, 2, 3)
        S1_MLP2_BANK = (0, 1, 2, 3, 2)

        def split(ap, b):
            return ap[..., FULL * b:FULL * (b + 1)], ap[..., LEFT_AT + LEFT * b:LEFT_AT + LEFT * (b + 1)]

        AUG_LANDED = 16 * 5

        REL_ROWS = {"rel_h": (slice(0, 8 * WIN), slice(0, 4 * WIN)), "rel_w": (slice(0, 8 * WIN), slice(64, 64 + 4 * WIN))}

        def take_qk(scaled, c, part, bank):
            last = scaled(m.qkT[:, c, 512 * part:512 * (part + 1)], bank[:, :], slice(0, 128))
            if c < 2:
                rows, two = slice(0, HD * REL_HEADS[c]), slice(2 * part, 2 * part + 2)
                src, qW = bank[rows, :].rearrange("k (b r w) -> k b r w", b=2, r=SIDE), m.qW[rows, c]
                scaled(main(qW)[:, two], src[:, :, 0:WIN, 0:WIN], rows)
                scaled(right(qW)[:, two], src[:, :, 0:WIN, WIN:SIDE], rows)
                last = scaled(low(qW)[:, two], src[:, :, WIN:SIDE, :], rows)
            return last

        block = ctx.enter_context(nc.Block())

        @block.sync
        def _(sp):
            x_dram = t["x"].rearrange("b h w c -> b (h w) c").rearrange("b (t p) c -> b p t c", p=128)
            for b in range(IMAGES):
                sp.dma_start(m.x[:, b], x_dram[b]).then_inc(x_loaded[b], 16)
            sp.dma_start(c["ident"][:, :], t["ident"]).then_inc(ident_loaded, 16)

            def load(l, name, s):
                sp.dma_start(w[l][name][:], t[f"{name}{l}"]).then_inc(s, 16)

            for name in ("vecs", "qkv", "rel8", "rel4"):
                load(0, name, A[0].loaded["rel" if name in ("rel8", "rel4") else name])
            sp.dma_start(m.kaug[BIAS_ROW:AUG], t["key_rows"].unsqueeze(1).broadcast_to([AUG - BIAS_ROW, QUADS, KEYS]))\
              .then_inc(aug_rows_loaded, 16)
            sp.dma_start(m.qaug[CODE_ROW:AUG], t["query_codes"].unsqueeze(1).broadcast_to([CODES, HEADS, TOKENS]))\
              .then_inc(aug_rows_loaded, 16)
            sp.wait_ge(q_zeroed, 1)
            for name in ("rows", "cols", "proj", "fc1", "fc2"):
                load(0, name, A[0].loaded["late"])
            sp.dma_start(f1.w1[:, 0:2], t["f1_w1"]).then_inc(spectral_loaded, 16)
            sp.dma_start(f1.w2[:, 0:2], t["f1_w2"]).then_inc(spectral_loaded, 16)
            sp.dma_start(f1.b1[:], t["f1_b1"]).then_inc(spectral_loaded, 16)
            sp.dma_start(f3.w[:], t["f3_w"]).then_inc(spectral_loaded, 16)
            sp.dma_start(f3.b[:], t["f3_b"]).then_inc(spectral_loaded, 16)
            for name in ("space_fwd", "flip", "inverse", "chan_fwd", "chan_back"):
                sp.dma_start(c[name][:], t[name]).then_inc(spectral_loaded, 16)
            load(1, "vecs", A[1].loaded["vecs"])
            load(1, "cols", A[1].loaded["late"])

            for l in range(2):
                s = A[l]
                if l == 1:
                    sp.wait_ge(A[0].proj_in.pe, len(PROJ))
                    load(1, "qkv", s.loaded["qkv"])
                    load(1, "rel8", s.loaded["rel"])
                    load(1, "rel4", s.loaded["rel"])
                    sp.wait_ge(A[0].out_proj.pe, IMAGES)
                    load(1, "proj", s.loaded["late"])
                    sp.wait_ge(A[0].bias_added, 2 * IMAGES)
                    load(1, "rows", s.loaded["late"])
                    sp.wait_ge(A[0].fc1.pe, 2 * HID_TILES)
                    load(1, "fc1", s.loaded["late"])
                    sp.wait_ge(A[0].fc2.pe, IMAGES)
                    load(1, "fc2", s.loaded["late"])
                for chunk in range(QK_CHUNKS):
                    wait_for(sp, s.proj_in, *taken_out(job("qk", chunk, 1)))
                    if chunk > 0:
                        sp.wait_ge(s.kpad_set, 1)
                        for quad in ((0,), (1, 2))[chunk - 1]:
                            rows = slice(0, 64) if quad == 1 else slice(64, 128)
                            sp.dma_start(m.kaug[0:BIAS_ROW, quad, :], m.qkT[rows, chunk]).then_inc(s.aug[quad], 16)
                    for n in range(REL_HEADS[chunk] if chunk < 2 else 0):
                        head = REL_HEADS[0] * chunk + n
                        lo = HD * (head % 4)
                        sp.dma_start(m.qaug[lo:lo + HD, head, :], m.qW[HD * n:HD * (n + 1), chunk]).then_inc(s.aug[head // 4], 16)
                for g in range(2):
                    for kind, lo, src in (("rel_h", BIAS_ROW, m.relhT), ("rel_w", BIAS_ROW + WIN, m.relwT)):
                        wait_for(sp, s.proj_in, *taken_out(job(kind, g, 1)))
                        heads = slice(REL_HEADS[0] * g, REL_HEADS[0] * g + REL_HEADS[g])
                        sp.dma_start(m.qaug[lo:lo + WIN, heads, :], src[REL_ROWS[kind][g], g]).then_inc(s.aug_bias[g], 16)
                if l == 1:
                    sp.wait_ge(S1.inv.pe, IMAGES)
                    sp.dma_start(c["space_back"][:], t["space_back"]).then_inc(space_back_loaded, 16)
            out_dram = out.rearrange("b h w c -> b (h w) c").rearrange("b (t p) c -> b p t c", p=128)
            for n, b in enumerate(OUT_ORDER):
                sp.wait_ge(S3.inv.dve, n + 1)
                sp.dma_start(out_dram[b], m.xb[:, b]).then_inc(stored, 16)
            sp.wait_ge(stored, 16 * IMAGES)

        @block.gpsimd
        def _(pool):
            pool.memset(m.qaug[0:BIAS_ROW], 0.0).then_inc(q_zeroed, 1)
            pool.memset(m.v[:], 0.0).then_inc(v_zeroed, 1)

            def attention(l, x_ready):
                s = A[l]
                pool.wait_ge(s.loaded["vecs"], 16)
                if l == 1:
                    pool.wait_ge(S1.inv.pe, IMAGES)
                    pool.wait_ge(S1.inv.dve, IMAGES)
                pool.tensor_copy(m.qkT[:, 1:3, TOKENS:KEYS], w[l]["vecs"][:, 5:7].unsqueeze(2).broadcast_to([128, 2, KEYS - TOKENS]))\
                    .then_inc(s.kpad_set, 1)
                pool.wait_ge(s.ln[0].act, 2)
                pool.wait_ge(s.ln[0].dve, 2)
                for half in range(2):
                    to_window_order(pool.tensor_copy, m.yW[:, half], raster(m.yT[:, half]), 0, SIDE).then_inc(s.y_ordered, 1)
                pool.wait_ge(s.loaded["late"], 16 * 5)
                for b in range(IMAGES):
                    x_ready(pool, b)
                    pool.tensor_tensor(m.xb[:, b], m.x[:, b], w[l]["rows"][:, 0:1].broadcast_to([128, 2, CH]), ALU.add)\
                        .then_inc(s.bias_added, 1)
                for u in range(N_UNITS):
                    n, cols = turned_size(u)
                    pool.wait_ge(s.recip, u + 1)
                    p, by = m.probs[0:n, u % P_RING, 0:cols], m.recip[0:n, u % P_RING]
                    if UNITS[u][0] < IMAGES:
                        p = p.rearrange("k (a n) -> k a n", a=2)
                        pool.tensor_tensor(p, p, by.unsqueeze(2).broadcast_to([n, 2, cols // 2]), ALU.mult).then_inc(s.normed, 1)
                    else:
                        pool.tensor_scalar(p, p, by[:, 0:1], None, ALU.mult).then_inc(s.normed, 1)
                for b in range(IMAGES):
                    pool.wait_ge(s.out_proj.dve, b + 1)
                    pool.tensor_tensor(m.xb[:, b], m.x[:, b], w[l]["rows"][:, 1:2].broadcast_to([128, 2, CH]), ALU.add)\
                        .then_inc(s.bias_added, 1)

            attention(0, lambda eng, b: eng.wait_ge(x_loaded[b], 16))
            pool.wait_ge(spectral_loaded, 16 * 10)
            pool.tensor_scalar(f1.w1[:, 2], f1.w1[:, 1], -1.0, None, ALU.mult).then_inc(weights_mixed, 1)
            pool.tensor_scalar(f1.w2[0:HALF, 2], f1.w2[0:HALF, 1], -1.0, None, ALU.mult).then_inc(weights_mixed, 1)
            pool.tensor_copy(f1.w2[0:HALF, 3], f1.w2[0:HALF, 0]).then_inc(weights_mixed, 1)
            pool.tensor_tensor(f3.mixw[:, :, 0], f3.w[:, :, 0], f3.w[:, :, 1], ALU.add).then_inc(weights_mixed, 1)
            pool.tensor_tensor(f3.mixw[:, :, 1], f3.w[:, :, 0], f3.w[:, :, 1], ALU.subtract).then_inc(weights_mixed, 1)
            pool.wait_ge(weights_mixed, 5)
            pool.tensor_scalar(f3.mixw[:], f3.mixw[:], 0.5, None, ALU.mult).then_inc(weights_mixed, 1)
            attention(1, lambda eng, b: eng.wait_ge(S1.inv.dve, b + 1))

        @block.tensor
        def _(pe):
            mm = nc.tensor.matmul

            def turn_norm(ln, bank0, g):
                for i in range(4):
                    pe.wait_ge(ln.done, 4 * g + i + 1)
                    for half in range(2):
                        last = nc.tensor.transpose(m.bank[bank0 + 2 * g + half][0:HALF, 128 * i:128 * (i + 1)],
                                                   m.xn[:, 4 * g + i, HALF * half:HALF * (half + 1)], c["ident"][:])
                        if i == 3:
                            last.then_inc(ln.pe, 1)

            def out_project(s, wl, b):
                pe.wait_ge(s.oT_out, O_TILES * (b + 2))
                for tile in range(2):
                    for heads in range(O_TILES):
                        at = PLACES * b + 128 * tile
                        last = mm(m.bank[b][:, CH * tile:CH * (tile + 1)], m.oT[:, heads, at:at + 128], wl["proj"][:, heads],
                                  start=heads == 0, stop=heads == O_TILES - 1)
                last.then_inc(s.out_proj.pe, 1)

            def attention(l):
                s, wl = A[l], w[l]
                if l == 0:
                    pe.wait_ge(ones_set, 1)
                    for _ in range(WARM_UPS):
                        mm(m.bank[7][:, 0:4 * HALF_WIN], m.probs[:, 0, 0:128], m.probs[:, 0, :], start=True, stop=True)
                    pe.wait_ge(ident_loaded, 16)
                    turn_norm(s.ln[0], 0, 0)
                pe.wait_ge(s.loaded["qkv"], 16)
                pe.wait_ge(s.loaded["rel"], 16 * 2)
                for j, (kind, g, part, _) in enumerate(PROJ):
                    if j >= 4:
                        wait_for(pe, s.proj_in, *taken_out(j - 4))
                    if j == 2:
                        turn_norm(s.ln[0], 0, 1)
                    if j == job("qk", 0, part):
                        pe.wait_ge(s.ln[0].act, part + 1)
                        pe.wait_ge(s.ln[0].dve, part + 1)
                    bank = m.bank[4 + j % 4]
                    if kind == "qk":
                        for half in range(2):
                            last = mm(bank[:, :], wl["qkv"][:, half, 128 * g:128 * (g + 1)], m.yT[:, half, 512 * part:512 * (part + 1)],
                                      start=half == 0, stop=half == 1)
                    elif kind in ("rel_h", "rel_w"):
                        wait_for(pe, s.proj_in, *taken_out(job("qk", g, 1)))
                        if g == 1 and kind == "rel_h":
                            continue
                        q, heads = raster(m.qkT[:, g, 0:TOKENS]), REL_HEADS[g]
                        for n in range(SIDE // 2):
                            at = SIDE // 2 * part + n
                            columns = slice(heads * (WIN - 1 - at % WIN), heads * (2 * WIN - 1 - at % WIN))
                            for one in ("rel_h", "rel_w") if g == 1 else (kind,):
                                o = m.bank[4 + (j - (one != kind)) % 4][REL_ROWS[one][g], 64 * n:64 * (n + 1)]
                                last = mm(o, wl[f"rel{heads}"][:, 0 if one == "rel_h" else 1, columns],
                                          q[:, :, at, :] if one == "rel_h" else q[:, :, :, at], start=True, stop=True)
                        if g == 1:
                            last.then_inc(s.proj_in.pe, 2)
                            continue
                    else:
                        pe.wait_ge(s.y_ordered, 2)
                        for tile in range(2):
                            n = HALF_WIN if g < IMAGES else EDGE_TOKENS[tile]
                            at = HALF_WIN * (2 * g + tile) if g < IMAGES else EDGE_AT[tile]
                            for half in range(2):
                                last = mm(bank[0:n, CH * tile:CH * (tile + 1)], m.yW[:, half, at:at + n], wl["qkv"][:, half, 2 * CH:3 * CH],
                                          start=half == 0, stop=half == 1)
                    last.then_inc(s.proj_in.pe, 1)

                if l == 0:
                    pe.wait_ge(aug_rows_loaded, 16 * 2)
                for step in range(N_UNITS + PV_LAG):
                    if step < N_UNITS:
                        b, h = UNITS[step]
                        if step >= S_RING:
                            pe.wait_ge(s.probs, step - S_RING + 1)
                        if b == IMAGES and h % 4 == 0:
                            pe.wait_ge(s.aug[h // 4], AUG_LANDED)
                            pe.wait_ge(s.aug_bias[h // REL_HEADS[0]], 16 * 2)
                        q, k = m.qaug[0:AUG, h], m.kaug[:, h // 4, 0:TOKENS]
                        bank = m.bank[step % S_RING]
                        if b < IMAGES:
                            keys = raster(k)[:, b, 0:WIN, 0:WIN]
                            for part in range(2):
                                at = HALF_WIN * (2 * b + part)
                                last = mm(bank[0:HALF_WIN, 2 * HALF_WIN * part:2 * HALF_WIN * (part + 1)], q[:, at:at + HALF_WIN], keys,
                                          start=True, stop=True)
                        else:
                            e = b - IMAGES
                            n, (pad_at, pads) = EDGE_TOKENS[e], EDGE_PADS[e]
                            asking = q[:, EDGE_AT[e]:EDGE_AT[e] + n]
                            mm(bank[0:n, 0:n], asking, window(k, e), start=True, stop=True)
                            last = mm(bank[0:n, n:n + pads], asking, m.kaug[:, h // 4, pad_at:pad_at + pads], start=True, stop=True)
                        last.then_inc(s.scores, 1)
                    if step == N_UNITS:
                        pe.wait_ge(s.loaded["late"], 16 * 5)
                        pe.wait_ge(s.probs, N_UNITS - S_RING + 1)
                        out_project(s, wl, 0)
                    if TURN_LAG <= step < N_UNITS + TURN_LAG:
                        u = step - TURN_LAG
                        b, h = UNITS[u]
                        if u == 0:
                            pe.wait_ge(s.proj_in.act, taken_out(job("v", 2, 0))[1])
                            pe.wait_ge(s.proj_in.dve, taken_out(job("v", 4, 0))[1])
                        pe.wait_ge(s.normed, u + 1)
                        if u >= TURN_RING:
                            wait_for(pe, s.turn, *turned_by(u - TURN_RING))
                        bank = m.bank[S_RING + u % TURN_RING]
                        if b < IMAGES:
                            for key in range(2):
                                for part in range(2):
                                    at = HALF_WIN * (2 * key + part)
                                    src = m.probs[0:HALF_WIN, u % P_RING, HALF_WIN * (2 * part + key):HALF_WIN * (2 * part + key + 1)]
                                    last = nc.tensor.transpose(bank[0:HALF_WIN, at:at + HALF_WIN], src, c["ident"][0:HALF_WIN, 0:HALF_WIN])
                        else:
                            n = EDGE_TOKENS[b - IMAGES]
                            last = nc.tensor.transpose(bank[0:n, 0:n], m.probs[0:n, u % P_RING, 0:n], c["ident"][0:n, 0:n])
                        last.then_inc(s.turn.pe, 1)
                    if step == N_UNITS + TURN_LAG - 1:
                        out_project(s, wl, 1)
                    if step >= PV_LAG and (step - PV_LAG) % 4 == 3:
                        burst = (step - PV_LAG) // 4
                        units = range(4 * burst, 4 * burst + 4)
                        j = o_job(4 * burst)
                        for who in ("act", "dve"):
                            wait_for(pe, s.turn, who, max(turned_by(u)[1] for u in units if turned_by(u)[0] == who))
                        if j >= 1 and o_job(4 * burst - 1) != j:
                            pe.wait_ge(s.oT_out, j)
                        e = UNITS[4 * burst][0] - IMAGES
                        first, last_burst = burst == 0 or o_job(4 * burst - 1) != j, burst == LAST[j]
                        for key in range(2 if e < 0 else 1):
                            for u in units:
                                b, h = UNITS[u]
                                n, keys, at, cols = ((HALF_WIN, 2 * b + key, 0, 2 * HALF_WIN) if e < 0 else
                                                     (EDGE_TOKENS[e], 2 * IMAGES + e, EDGE_AT[e] - MAIN, EDGE_TOKENS[e]))
                                v_at = 32 * h - HD * (h // 4 % 2)
                                last = mm(m.bank[7][32 * (h % 4):32 * (h % 4) + 32, at:at + cols], m.v_cols[0:n, keys, v_at:v_at + 32],
                                          m.probsT[0:n, u % T_RING, cols * key:cols * (key + 1)],
                                          start=first and key == 0, stop=last_burst and (key == 1 or e >= 0))
                        last.then_inc(s.pv, 1)
                        if burst == N_UNITS // 4 - 2:
                            out_project(s, wl, 2)

                turn_norm(s.ln[1], 4, 0)
                out_project(s, wl, IMAGES - 1)
                for j in range(2 * HID_TILES):
                    g, hid = divmod(j, HID_TILES)
                    if j == 2:
                        turn_norm(s.ln[1], 4, 1)
                    if hid == 0:
                        pe.wait_ge(s.ln[1].act, g + 1)
                        pe.wait_ge(s.ln[1].dve, g + 1)
                    if j < 4:
                        pe.wait_ge(s.out_proj.dve, j + 1)
                    else:
                        pe.wait_ge(s.fc1.act, j - 3)
                    for half in range(2):
                        last = mm(m.bank[j % 4][:, :], wl["fc1"][:, half, 128 * hid:128 * (hid + 1)], m.yT[:, half, 512 * g:512 * (g + 1)],
                                  start=half == 0, stop=half == 1)
                    last.then_inc(s.fc1.pe, 1)
                for b in range(IMAGES):
                    pe.wait_ge(s.fc1.act, HID_TILES * (b // 2 + 1))
                    for tile in range(2):
                        at = PLACES * b + 128 * tile
                        for hid in range(HID_TILES):
                            last = mm(m.bank[4 + b][:, CH * tile:CH * (tile + 1)], m.hidT[:, hid, at:at + 128], wl["fc2"][:, hid],
                                      start=hid == 0, stop=hid == HID_TILES - 1)
                    last.then_inc(s.fc2.pe, 1)

            def spectral1():
                pe.wait_ge(spectral_loaded, 16 * 10)
                for j in range(8):
                    b, half = divmod(j, 2)
                    pe.wait_ge(A[0].fc2.dve, b + 1)
                    if j >= 4:
                        wait_for(pe, S1.fwd, ("act", "dve")[j % 2], (j - 4) // 2 + 1)
                    for tile in range(2):
                        last = mm(m.bank[j % 4][0:HALF, 0:2 * MODES], m.x[:, b, tile, HALF * half:HALF * (half + 1)], c["space_fwd"][:, tile],
                                  start=tile == 0, stop=tile == 1)
                    last.then_inc(S1.fwd.pe, 1)
                pe.wait_ge(weights_mixed, 6)
                pe.wait_ge(o1_ones_set, 1)
                for j in range(8):
                    g, half, part = j // 4, j // 2 % 2, j % 2
                    pe.wait_ge(S1.fwd.act, 2 * g + 2)
                    pe.wait_ge(S1.fwd.dve, 2 * g + 2)
                    if j >= 4:
                        wait_for(pe, S1.mlp1, ("act", "dve")[j % 2], (j - 4) // 2 + 1)
                    cols = S1_COLS[g]
                    o = m.bank[4 + j % 4][0:HALF, 0:cols.stop - cols.start]
                    mm(o, f1.w1[:, 0, half], m.xf[:, half, part, cols], start=True, stop=False)
                    last = mm(o, f1.w1[:, 1 if part else 2, half], m.xf[:, half, 1 - part, cols], start=False, stop=True)
                    last.then_inc(S1.mlp1.pe, 1)
                def second_layer(j):
                    b = S1_MLP2[j]
                    n = 2 if b < 2 else 4
                    pe.wait_ge(S1.mlp1.act, n)
                    pe.wait_ge(S1.mlp1.dve, n)
                    if j == 4:
                        pe.wait_ge(S1.mlp2.dve, 3)
                    for half in range(2):
                        if b < IMAGES:
                            o = m.bank[S1_MLP2_BANK[j]][:, 0:2 * CH].rearrange("k (p h c) -> k p h c", p=2, h=2)[:, :, half]
                            at = slice(FULL * b, FULL * (b + 1))
                            mm(o, m.o1[:, half, 0, at], f1.w2[:, 0:2, half], start=True, stop=False)
                            last = mm(o, m.o1[0:HALF, half, 1, at], f1.w2[0:HALF, 2:4, half], start=False, stop=True)
                            continue
                        for part in range(2):
                            o = m.bank[S1_MLP2_BANK[j]][64 * part:64 * (part + 1), HALF * half:HALF * (half + 1)]
                            mm(o, m.o1[:, half, 0, LEFT_AT:], f1.w2[:, part, half], start=True, stop=False)
                            last = mm(o, m.o1[0:HALF, half, 1, LEFT_AT:], f1.w2[0:HALF, 2 + part, half], start=False, stop=True)
                    last.then_inc(S1.mlp2.pe, 1)

                def inverse(b):
                    pe.wait_ge(S1.mlp2.dve, 1 + max(S1_MLP2.index(b), S1_MLP2.index(IMAGES)))
                    for tile in range(2):
                        for n, (row, o2) in enumerate(((0, m.o2[:, 0, b]), (1, m.o2[:, 1, b]), (2 + b, m.o2_left[:, :]))):
                            last = mm(m.bank[4 + b][:, CH * tile:CH * (tile + 1)], c["inverse"][:, row, 128 * tile:128 * (tile + 1)], o2,
                                      start=n == 0, stop=n == 2)
                    last.then_inc(S1.inv.pe, 1)

                for j in range(4):
                    second_layer(j)
                inverse(0)
                inverse(1)
                second_layer(4)
                inverse(2)
                turn_norm(A[1].ln[0], 0, 0)
                inverse(3)

            def spectral3():
                for b in range(IMAGES):
                    pe.wait_ge(A[1].fc2.dve, b + 1)
                    for half in range(2):
                        for tile in range(2):
                            at = MODES * half + MCHUNK * tile
                            last = mm(m.bank[4 + b][0:HALF, at:at + MCHUNK], m.x[:, b, tile, HALF * half:HALF * (half + 1)],
                                      c["flip"][:, tile], start=True, stop=True)
                    last.then_inc(S3.flip.pe, 1)
                for j in range(8):
                    mix, half = (3, 2, 0, 1)[j % 4], j // 4
                    pe.wait_ge(S3.mixed, {3: 1, 2: 1, 0: 2, 1: 3}[mix])
                    if j >= 4:
                        wait_for(pe, S3.fwd, ("act", "dve", "act", "act")[j % 4], (1, 1, 2, 3)[j % 4])
                    for tile in range(2):
                        last = mm(m.bank[j % 4][0:HALF, 0:2 * MODES], m.mix[:, mix, tile, HALF * half:HALF * (half + 1)], c["space_fwd"][:, tile],
                                  start=tile == 0, stop=tile == 1)
                    last.then_inc(S3.fwd.pe, 1)
                pe.wait_ge(S3.fwd.dve, 2)
                for j in range(4):
                    half, g = divmod(j, 2)
                    pe.wait_ge(S3.fwd.act, 6 if g else 5)
                    wait_for(pe, S3.flip, ("act", "dve")[j % 2], j // 2 + 1)
                    for n in range(4):
                        last = mm(m.bank[4 + j][0:HALF, 0:2 * MODES], c["chan_fwd"][:, n // 2, n % 2, HALF * half:HALF * (half + 1)],
                                  m.z[:, n // 2, n % 2, 2 * g:2 * g + 2], start=n == 0, stop=n == 3)
                    last.then_inc(S3.chan.pe, 1)
                for j in range(8):
                    half, g, nk = j // 4, j // 2 % 2, j % 2
                    wait_for(pe, S3.chan, ("act", "dve")[g], half + 1)
                    if j >= 4:
                        wait_for(pe, S3.mlp1, ("act", "dve")[j % 2], (j - 4) // 2 + 1)
                    cols = slice(2 * MODES * g, 2 * MODES * (g + 1))
                    o = m.bank[j % 4][0:HALF, 0:2 * MODES]
                    lo = slice(HALF * half, HALF * (half + 1))
                    mm(o, f3.mixw[:, 0, nk, lo], m.ak[:, half, cols], start=True, stop=False)
                    last = mm(o, f3.mixw[:, 0, 1 - nk, lo], m.an[:, half, cols], start=False, stop=True)
                    last.then_inc(S3.mlp1.pe, 1)
                for half in range(2):
                    lo = slice(HALF * half, HALF * (half + 1))
                    for g in range(2):
                        j = 2 * half + g
                        pe.wait_ge(S3.mlp1.act, j + 1)
                        pe.wait_ge(S3.mlp1.dve, j + 1)
                        cols = slice(2 * MODES * g, 2 * MODES * (g + 1))
                        o = m.bank[4 + j][0:HALF, 0:2 * MODES]
                        mm(o, f3.mixw[:, 1, 0, lo], m.o1n[0:HALF, half, 0, cols], start=True, stop=False)
                        last = mm(o, f3.mixw[:, 1, 1, lo], m.o1n[0:HALF, half, 1, cols], start=False, stop=True)
                        last.then_inc(S3.o2k.pe, 1)
                    for g in range(2):
                        j = 2 * half + g
                        if half == 0:
                            pe.wait_ge(S3.mlp1.act, 4)
                            pe.wait_ge(S3.mlp1.dve, 4)
                        cols = slice(2 * MODES * g, 2 * MODES * (g + 1))
                        o = m.bank[j][0:HALF, 0:2 * MODES]
                        mm(o, f3.mixw[:, 1, 0, lo], m.o1n[0:HALF, half, 1, cols], start=True, stop=False)
                        pe.wait_ge(S3.o2k.act, j + 1)
                        last = mm(o, f3.mixw[:, 1, 1, lo], m.o2k[:, half, cols], start=False, stop=True)
                        last.then_inc(S3.o2nk.pe, 1)
                for half in range(2):
                    for n, mix in enumerate((3, 2, 0, 1)):
                        pe.wait_ge(S3.hs, 6 * half + (1, 1, 3, 4)[n])
                        last = mm(m.bank[4 + n][:, 0:2 * CH], m.hs[:, half, FULL * mix:FULL * (mix + 1)], c["chan_back"][:, half],
                                  start=half == 0, stop=half == 1)
                        if half:
                            last.then_inc(S3.back.pe, 1)
                    pe.wait_ge(S3.hs, 6 * (half + 1))
                    for part in range(2):
                        last = mm(m.bank[0][64 * part:64 * (part + 1), 0:CH], m.hs[:, half, LEFT_AT:],
                                  c["chan_back"][:, half, CH * part:CH * (part + 1)], start=half == 0, stop=half == 1)
                    if half:
                        last.then_inc(S3.back.pe, 1)
                pe.wait_ge(space_back_loaded, 16)
                pe.wait_ge(S3.back.dve, 1)
                for n, b in enumerate(OUT_ORDER):
                    for tile in range(2):
                        for i, (row, gb) in enumerate(((0, m.gb[:, 0, b]), (1, m.gb[:, 1, b]), (2 + b, m.gb_left[:, :]))):
                            if n == tile == 0 and i == 2:
                                pe.wait_ge(S3.back.act, 4)
                            last = mm(m.bank[1 + n][:, CH * tile:CH * (tile + 1)], c["space_back"][:, row, 128 * tile:128 * (tile + 1)], gb,
                                      start=i == 0, stop=i == 2)
                    last.then_inc(S3.inv.pe, 1)

            attention(0)
            spectral1()
            attention(1)
            spectral3()

        @block.scalar
        def _(act):
            run = nc.scalar.activation

            def load_table(func):
                run(m.spare[:, 0:1], m.spare[:, 1:2], func)

            def root(ln, g):
                act.wait_ge(ln.var, g + 1)
                run(m.std[:, 4 * g:4 * g + 4], m.var[:, 4 * g:4 * g + 4], ACT.Sqrt).then_inc(ln.std, 1)

            def take_norm(wl, ln, bank0, col, g):
                act.wait_ge(ln.pe, 2 * g + 1)
                run(m.yT[:, 0, 512 * g:512 * (g + 1)], m.bank[bank0 + 2 * g][0:HALF, :], ACT.Identity,
                    scale=wl["vecs"][0:HALF, col:col + 1], bias=wl["vecs"][0:HALF, col + 2:col + 3]).then_inc(ln.act, 1)

            def attention(l):
                s, wl = A[l], w[l]
                load_table(ACT.Sqrt)
                for g in range(2):
                    root(s.ln[0], g)
                    act.wait_ge(s.loaded["vecs"], 16)
                    take_norm(wl, s.ln[0], 0, 0, g)
                act.wait_ge(s.bias_scaled, 1)
                for j, (kind, g, part, who) in enumerate(PROJ):
                    if who != "act":
                        continue
                    act.wait_ge(s.proj_in.pe, j + 1)
                    bank = m.bank[4 + j % 4]
                    if kind == "qk":
                        ins = take_qk(lambda dst, src, rows: run(dst, src, ACT.Identity, scale=m.qk_scale[rows, g:g + 1],
                                                                 bias=m.qk_bias[rows, l, g:g + 1]), g, part, bank)
                    elif kind == "rel_h":
                        rows = REL_ROWS[kind][g]
                        ins = to_window_order(lambda dst, src: run(dst, src, ACT.Copy), m.relhT[rows, g],
                                              bank[rows, :].rearrange("k (r b w) -> k b r w", r=8, b=IMAGES), 8 * part, 8 * part + 8)
                    else:
                        if l == 0 and g == 0:
                            act.wait_ge(v_zeroed, 1)
                        ins = run(m.v[0:HALF_WIN, 2 * g:2 * g + 2, :, 0:HD],
                                  bank[0:HALF_WIN, 0:2 * CH].rearrange("k (t h c) -> k t h c", t=2, c=HD), ACT.Copy)
                    ins.then_inc(s.proj_in.act, 1)
                act.wait_ge(s.loaded["late"], 16 * 5)
                load_table(ACT.Exp)
                for step in range(N_UNITS + PV_LAG + 1):
                    if step < N_UNITS:
                        b, h = UNITS[step]
                        act.wait_ge(s.max, step + 1)
                        if step >= P_RING:
                            act.wait_ge(s.turn.pe, step - P_RING + 1)
                        bank, slot = m.bank[step % S_RING], step % P_RING
                        if b < IMAGES:
                            for part in range(2):
                                cols = slice(2 * HALF_WIN * part, 2 * HALF_WIN * (part + 1))
                                ins = run(m.probs[0:HALF_WIN, slot, cols], bank[0:HALF_WIN, cols], ACT.Exp,
                                          bias=m.negmax[0:HALF_WIN, slot, part:part + 1], accum_out=m.sums[0:HALF_WIN, slot, part:part + 1])
                        else:
                            e = b - IMAGES
                            n, keys = EDGE_TOKENS[e], EDGE_TOKENS[e] + EDGE_PADS[e][1]
                            ins = run(m.probs[0:n, slot, 0:keys], bank[0:n, 0:keys], ACT.Exp, bias=m.negmax[0:n, slot, 0:1],
                                      accum_out=m.sums[0:n, slot, 0:1])
                        ins.then_inc(s.probs, 1)
                    if TURN_LAG <= step < N_UNITS + TURN_LAG and turned_by(step - TURN_LAG)[0] == "act":
                        u = step - TURN_LAG
                        act.wait_ge(s.turn.pe, u + 1)
                        if u >= T_RING:
                            act.wait_ge(s.pv, (u - T_RING) // 4 + 1)
                        n, cols = turned_size(u)
                        run(m.probsT[0:n, u % T_RING, 0:cols], m.bank[S_RING + u % TURN_RING][0:n, 0:cols], ACT.Copy).then_inc(s.turn.act, 1)
                    if step == N_UNITS + TURN_LAG:
                        load_table(ACT.Sqrt)
                        root(s.ln[1], 0)
                    for j, burst in enumerate(LAST):
                        if step == 4 * burst + 3 + PV_LAG + 1:
                            act.wait_ge(s.pv, burst + 1)
                            bank, o = m.bank[7], m.oT[:, j % O_TILES]
                            bias = wl["cols"][:, HID_TILES + j % O_TILES:HID_TILES + j % O_TILES + 1]
                            if j == 0:
                                act.wait_ge(s.aug_bias[1], 16 * 2)
                                act.wait_ge(s.aug[QUADS - 1], AUG_LANDED)
                            if j >= O_TILES:
                                ins = run(raster(o)[:, j // O_TILES - 1, 0:WIN, 0:WIN], bank[:, 0:2 * HALF_WIN].rearrange("k (r w) -> k r w", r=WIN),
                                          ACT.Identity, bias=bias)
                            else:
                                run(window(o, 0), bank[:, 0:RIGHT].rearrange("k (b r w) -> k b r w", b=IMAGES, r=WIN), ACT.Identity, bias=bias)
                                ins = run(window(o, 1), bank[:, RIGHT:RIGHT + LOW].rearrange("k (b r w) -> k b r w", b=IMAGES, r=EDGE),
                                          ACT.Identity, bias=bias)
                            ins.then_inc(s.oT_out, 1)
                take_norm(wl, s.ln[1], 4, 7, 0)
                root(s.ln[1], 1)
                load_table(ACT.Gelu)
                for j in range(2 * HID_TILES):
                    g, hid = divmod(j, HID_TILES)
                    if j == 2:
                        take_norm(wl, s.ln[1], 4, 7, 1)
                    act.wait_ge(s.fc1.pe, j + 1)
                    run(m.hidT[:, hid, 512 * g:512 * (g + 1)], m.bank[j % 4][:, :], ACT.Gelu, bias=wl["cols"][:, hid:hid + 1])\
                        .then_inc(s.fc1.act, 1)

            def spectral1():
                for j in range(0, 8, 2):
                    b, half = divmod(j, 2)
                    act.wait_ge(S1.fwd.pe, j + 1)
                    src = m.bank[j % 4][0:HALF, 0:2 * MODES].rearrange("k (a n) -> k a n", a=2)
                    full, left = split(m.xf[:, half], b)
                    run(full, src[:, :, 0:FULL], ACT.Copy, scale=1.0 / SIDE)
                    run(left, src[:, :, FULL:MODES], ACT.Copy, scale=1.0 / SIDE).then_inc(S1.fwd.act, 1)
                for j in range(0, 8, 2):
                    g, half = j // 4, j // 2 % 2
                    act.wait_ge(S1.mlp1.pe, j + 1)
                    cols = S1_COLS[g]
                    run(m.o1[0:HALF, half, 0, cols], m.bank[4 + j % 4][0:HALF, 0:cols.stop - cols.start], ACT.Relu,
                        bias=f1.b1[:, 0, half:half + 1]).then_inc(S1.mlp1.act, 1)

            def spectral3():
                for b in range(0, IMAGES, 2):
                    act.wait_ge(S3.flip.pe, b + 1)
                    run(m.an[:, :, MODES * b:MODES * (b + 1)], m.bank[4 + b][0:HALF, 0:2 * MODES].rearrange("k (a n) -> k a n", a=2), ACT.Copy)\
                        .then_inc(S3.flip.act, 1)
                for j in range(8):
                    mix, half = (3, 2, 0, 1)[j % 4], j // 4
                    if mix == 2:
                        continue
                    act.wait_ge(S3.fwd.pe, j + 1)
                    if mix == 3:
                        dst = m.hpart[0:HALF, half, 0:2 * MODES]
                        run(dst, m.bank[j % 4][0:HALF, 0:2 * MODES], ACT.Copy).then_inc(S3.fwd.act, 1)
                    else:
                        run(m.z[:, half, :, 2 * mix], m.bank[j % 4][0:HALF, 0:2 * MODES].rearrange("k (a n) -> k a n", a=2), ACT.Copy)\
                            .then_inc(S3.fwd.act, 1)
                for j in (0, 2):
                    act.wait_ge(S3.chan.pe, j + 1)
                    run(m.ak[:, j // 2, 0:2 * MODES], m.bank[4 + j][0:HALF, 0:2 * MODES], ACT.Copy).then_inc(S3.chan.act, 1)
                for j in range(0, 8, 2):
                    half, g = j // 4, j // 2 % 2
                    act.wait_ge(S3.mlp1.pe, j + 1)
                    run(m.o1n[0:HALF, half, 0, 2 * MODES * g:2 * MODES * (g + 1)], m.bank[j % 4][0:HALF, 0:2 * MODES], ACT.Relu,
                        bias=f3.b[:, 0, 0, half:half + 1]).then_inc(S3.mlp1.act, 1)
                for j in range(4):
                    half, g = divmod(j, 2)
                    act.wait_ge(S3.o2k.pe, j + 1)
                    run(m.o2k[:, half, 2 * MODES * g:2 * MODES * (g + 1)], m.bank[4 + j][0:HALF, 0:2 * MODES], ACT.Identity,
                        bias=f3.b[:, 1, 0, half:half + 1]).then_inc(S3.o2k.act, 1)
                jobs = ((0, m.hpart[:, 0, :]), (2, m.gb[:, :, 0]), (3, m.gb[:, :, 2]), (4, m.gb_left[:, :]))
                for j, dst in jobs:
                    act.wait_ge(S3.back.pe, j + 1)
                    src = m.bank[4 + j][:, 0:2 * CH] if j < 4 else m.bank[0][:, 0:CH]
                    if j in (2, 3):
                        src = src.rearrange("k (a n) -> k a n", a=2)
                    run(dst, src, ACT.Copy).then_inc(S3.back.act, 1)

            act.wait_ge(spare_set, 1)
            attention(0)
            spectral1()
            attention(1)
            spectral3()

        @block.vector
        def _(dve):
            def normalise(wl, ln, x_ready, eps, bank0, col, meanwhile=None):
                def take_norm(g):
                    dve.wait_ge(ln.pe, 2 * g + 2)
                    dve.tensor_scalar(m.yT[:, 1, 512 * g:512 * (g + 1)], m.bank[bank0 + 2 * g + 1][0:HALF, :],
                                      wl["vecs"][0:HALF, col + 1:col + 2], wl["vecs"][0:HALF, col + 3:col + 4], ALU.mult, ALU.add).then_inc(ln.dve, 1)

                for g in range(2):
                    for b in (2 * g, 2 * g + 1):
                        if b == IMAGES - 1:
                            take_norm(0)
                        x_ready(b)
                        for tile in range(2):
                            dve.bn_stats(m.stats[:, 2 * b + tile], m.x[:, b, tile]).then_inc(ln.stats, 1)
                    dve.wait_ge(ln.stats, 4 * g + 4)
                    for i in range(4 * g, 4 * g + 4):
                        dve.bn_aggr(m.meanvar[:, i], m.stats[:, i]).then_inc(ln.mean, 1)
                    dve.wait_ge(ln.mean, 4 * g + 4)
                    dve.tensor_scalar(m.var[:, 4 * g:4 * g + 4], m.meanvar[:, 4 * g:4 * g + 4, 1], eps, None, ALU.add).then_inc(ln.var, 1)
                    if g == 0 and meanwhile:
                        meanwhile()
                    dve.wait_ge(ln.std, g + 1)
                    dve.reciprocal(m.rstd[:, 4 * g:4 * g + 4], m.std[:, 4 * g:4 * g + 4]).then_inc(ln.rstd, 1)
                    dve.wait_ge(ln.rstd, g + 1)
                    for i in range(4 * g, 4 * g + 4):
                        dve.tensor_scalar(m.xn[:, i], m.x[:, i // 2, i % 2], m.meanvar[:, i, 0:1], m.rstd[:, i:i + 1],
                                          ALU.subtract, ALU.mult).then_inc(ln.done, 1)
                take_norm(1)

            def attention(l, x_ready, meanwhile=None):
                s, wl = A[l], w[l]
                def first_input(b):
                    x_ready(b)
                    if b == 2:
                        dve.wait_ge(s.loaded["vecs"], 16)
                        dve.wait_ge(scale_set, 4)
                        dve.tensor_tensor(m.qk_bias[:, l], wl["vecs"][:, 4:7], m.qk_scale[:], ALU.mult).then_inc(s.bias_scaled, 1)
                        dve.wait_ge(s.bias_scaled, 1)

                def add_output(b):
                    dve.wait_ge(s.out_proj.pe, b + 1)
                    dve.wait_ge(s.bias_added, b + 1)
                    dve.tensor_tensor(m.x[:, b], m.bank[b][:, 0:2 * CH].rearrange("k (t c) -> k t c", t=2), m.xb[:, b], ALU.add)\
                       .then_inc(s.out_proj.dve, 1)
                    dve.wait_ge(s.out_proj.dve, b + 1)

                normalise(wl, s.ln[0], first_input, EPS[l], 0, 0, meanwhile)
                for j, (kind, g, part, who) in enumerate(PROJ):
                    if who != "dve":
                        continue
                    dve.wait_ge(s.proj_in.pe, j + 1)
                    bank = m.bank[4 + j % 4]
                    if kind == "qk":
                        ins = take_qk(lambda dst, src, rows: dve.tensor_scalar(dst, src, m.qk_scale[rows, g:g + 1], m.qk_bias[rows, l, g:g + 1],
                                                                               ALU.mult, ALU.add), g, part, bank)
                    elif kind == "rel_w":
                        rows = REL_ROWS[kind][g]
                        ins = to_window_columns(dve.tensor_copy, m.relwT[rows, g],
                                                bank[rows, :].rearrange("k (w b r) -> k b r w", w=8, b=IMAGES), 8 * part, 8 * part + 8)
                    elif g < IMAGES:
                        if l == 0 and g == 1:
                            dve.wait_ge(v_zeroed, 1)
                        ins = dve.tensor_copy(m.v[0:HALF_WIN, 2 * g:2 * g + 2, :, 0:HD],
                                              bank[0:HALF_WIN, 0:2 * CH].rearrange("k (t h c) -> k t h c", t=2, c=HD))
                    else:
                        for e in range(2):
                            n = EDGE_TOKENS[e]
                            ins = dve.tensor_copy(m.v[0:n, 2 * IMAGES + e, :, 0:HD],
                                                  bank[0:n, CH * e:CH * (e + 1)].rearrange("k (h c) -> k h c", c=HD))
                    ins.then_inc(s.proj_in.dve, 1)
                for step in range(N_UNITS + TURN_LAG):
                    if step < N_UNITS:
                        b, h = UNITS[step]
                        dve.wait_ge(s.scores, step + 1)
                        bank, slot = m.bank[step % S_RING], step % P_RING
                        if b < IMAGES:
                            ins = dve.tensor_reduce(m.negmax[0:HALF_WIN, slot], bank[0:HALF_WIN, 0:4 * HALF_WIN].rearrange("k (a n) -> k a n", a=2),
                                                    AX, ALU.max, negate=True)
                        else:
                            n, keys = EDGE_TOKENS[b - IMAGES], EDGE_TOKENS[b - IMAGES] + EDGE_PADS[b - IMAGES][1]
                            ins = dve.tensor_reduce(m.negmax[0:n, slot, 0:1], bank[0:n, 0:keys], AX, ALU.max, negate=True)
                        ins.then_inc(s.max, 1)
                    if 1 <= step < N_UNITS + 1:
                        u = step - 1
                        n, parts = turned_size(u)[0], 2 if UNITS[u][0] < IMAGES else 1
                        dve.wait_ge(s.probs, u + 1)
                        dve.reciprocal(m.recip[0:n, u % P_RING, 0:parts], m.sums[0:n, u % P_RING, 0:parts]).then_inc(s.recip, 1)
                    if step >= TURN_LAG and turned_by(step - TURN_LAG)[0] == "dve":
                        u = step - TURN_LAG
                        dve.wait_ge(s.turn.pe, u + 1)
                        if u >= T_RING:
                            dve.wait_ge(s.pv, (u - T_RING) // 4 + 1)
                        n, cols = turned_size(u)
                        dve.tensor_copy(m.probsT[0:n, u % T_RING, 0:cols], m.bank[S_RING + u % TURN_RING][0:n, 0:cols]).then_inc(s.turn.dve, 1)
                normalise(wl, s.ln[1], add_output, EPS[l], 4, 7)
                for b in range(IMAGES):
                    dve.wait_ge(s.fc2.pe, b + 1)
                    dve.wait_ge(s.bias_added, IMAGES + b + 1)
                    dve.tensor_tensor(m.x[:, b], m.bank[4 + b][:, 0:2 * CH].rearrange("k (t c) -> k t c", t=2), m.xb[:, b], ALU.add)\
                       .then_inc(s.fc2.dve, 1)

            def spectral1():
                dve.memset(m.o1[HALF:HALF + 1, :, 0], 1.0).then_inc(o1_ones_set, 1)
                for j in range(1, 8, 2):
                    b, half = divmod(j, 2)
                    dve.wait_ge(S1.fwd.pe, j + 1)
                    src = m.bank[j % 4][0:HALF, 0:2 * MODES].rearrange("k (a n) -> k a n", a=2)
                    full, left = split(m.xf[:, half], b)
                    dve.tensor_scalar(full, src[:, :, 0:FULL], 1.0 / SIDE, None, ALU.mult)
                    dve.tensor_scalar(left, src[:, :, FULL:MODES], 1.0 / SIDE, None, ALU.mult).then_inc(S1.fwd.dve, 1)
                for j in range(1, 8, 2):
                    g, half = j // 4, j // 2 % 2
                    dve.wait_ge(S1.mlp1.pe, j + 1)
                    cols = S1_COLS[g]
                    dve.tensor_scalar(m.o1[0:HALF, half, 1, cols], m.bank[4 + j % 4][0:HALF, 0:cols.stop - cols.start],
                                      f1.b1[:, 1, half:half + 1], 0.0, ALU.add, ALU.max).then_inc(S1.mlp1.dve, 1)
                for j in range(4):
                    shrink(j)

            def shrink(j):
                b = S1_MLP2[j]
                dve.wait_ge(S1.mlp2.pe, j + 1)
                cols = 2 * CH if b < IMAGES else CH
                bank, clip = m.bank[S1_MLP2_BANK[j]][:, 0:cols], m.clip1[:, j % 2, 0:cols]
                dve.tensor_scalar(clip, bank, -LAMBDA, LAMBDA, ALU.max, ALU.min).then_inc(S1.clipped, 1)
                dve.wait_ge(S1.clipped, j + 1)
                if b < IMAGES:
                    dve.tensor_tensor(m.o2[:, :, b], bank.rearrange("k (a n) -> k a n", a=2), clip.rearrange("k (a n) -> k a n", a=2),
                                      ALU.subtract).then_inc(S1.mlp2.dve, 1)
                else:
                    dve.tensor_tensor(m.o2_left[:, :], bank, clip, ALU.subtract).then_inc(S1.mlp2.dve, 1)

            def add_inverse(b):
                dve.wait_ge(S1.inv.pe, b + 1)
                dve.tensor_tensor(m.x[:, b], m.bank[4 + b][:, 0:2 * CH].rearrange("k (t c) -> k t c", t=2), m.x[:, b], ALU.add)\
                   .then_inc(S1.inv.dve, 1)
                dve.wait_ge(S1.inv.dve, b + 1)

            def unmix(dst, g, h, stage_sem):
                dve.tensor_tensor(dst(0, 1), g[0], h[1], ALU.add)
                dve.tensor_tensor(dst(1, 1), g[1], h[0], ALU.subtract)
                dve.tensor_tensor(dst(0, 3), g[0], h[1], ALU.subtract)
                dve.tensor_tensor(dst(1, 3), g[1], h[0], ALU.add).then_inc(stage_sem, 1)

            def spectral3():
                dve.wait_ge(A[1].fc2.dve, IMAGES)
                dve.tensor_tensor(m.mix[:, 2:4], m.x[:, 0:2], m.x[:, 2:4], ALU.subtract).then_inc(S3.mixed, 1)
                dve.tensor_tensor(m.ef[:], m.x[:, 0:2], m.x[:, 2:4], ALU.add).then_inc(S3.ef, 1)
                dve.wait_ge(S3.ef, 1)
                dve.tensor_tensor(m.mix[:, 0], m.ef[:, 0], m.ef[:, 1], ALU.add).then_inc(S3.mixed, 1)
                dve.tensor_tensor(m.mix[:, 1], m.ef[:, 0], m.ef[:, 1], ALU.subtract).then_inc(S3.mixed, 1)
                for b in range(1, IMAGES, 2):
                    dve.wait_ge(S3.flip.pe, b + 1)
                    dve.tensor_copy(m.an[:, :, MODES * b:MODES * (b + 1)], m.bank[4 + b][0:HALF, 0:2 * MODES].rearrange("k (a n) -> k a n", a=2))\
                       .then_inc(S3.flip.dve, 1)
                for half in range(2):
                    dve.wait_ge(S3.fwd.pe, 4 * half + 2)
                    dve.wait_ge(S3.fwd.act, 3 * half + 1)
                    g = m.bank[1][0:HALF, 0:2 * MODES].rearrange("k (a n) -> k a n", a=2)
                    h = m.hpart[0:HALF, half, 0:2 * MODES].rearrange("k (a n) -> k a n", a=2)
                    unmix(lambda part, b: m.z[:, half, part, b], (g[:, 0], g[:, 1]), (h[:, 0], h[:, 1]), S3.fwd.dve)
                for j in (1, 3):
                    dve.wait_ge(S3.chan.pe, j + 1)
                    dve.tensor_copy(m.ak[:, j // 2, 2 * MODES:4 * MODES], m.bank[4 + j][0:HALF, 0:2 * MODES]).then_inc(S3.chan.dve, 1)
                for j in range(1, 8, 2):
                    half, g = j // 4, j // 2 % 2
                    dve.wait_ge(S3.mlp1.pe, j + 1)
                    dve.tensor_scalar(m.o1n[0:HALF, half, 1, 2 * MODES * g:2 * MODES * (g + 1)], m.bank[j % 4][0:HALF, 0:2 * MODES],
                                      f3.b[:, 0, 1, half:half + 1], 0.0, ALU.add, ALU.max).then_inc(S3.mlp1.dve, 1)
                sv = m.s.rearrange("k d (b n) -> k d b n", b=IMAGES)
                for half in range(2):
                    for g in range(2):
                        cols = slice(2 * MODES * g, 2 * MODES * (g + 1))
                        dve.wait_ge(S3.o2nk.pe, 2 * half + g + 1)
                        dve.scalar_tensor_tensor(m.s[:, half, cols], m.bank[2 * half + g][0:HALF, 0:2 * MODES], f3.b[:, 1, 1, half:half + 1],
                                                 m.o2k[:, half, cols], ALU.add, ALU.add).then_inc(S3.s, 1)
                        dve.wait_ge(S3.s, 2 * half + g + 1)
                        dve.tensor_scalar(m.clip3[:, half, cols], m.s[:, half, cols], -LAMBDA, LAMBDA, ALU.max, ALU.min).then_inc(S3.clipped, 1)
                        dve.wait_ge(S3.clipped, 2 * half + g + 1)
                        dve.tensor_tensor(m.s[:, half, cols], m.s[:, half, cols], m.clip3[:, half, cols], ALU.subtract).then_inc(S3.shrunk, 1)
                    dve.wait_ge(S3.shrunk, 2 * (half + 1))
                    full = m.hs[:, half, 0:LEFT_AT].rearrange("k (b n) -> k b n", b=4)
                    left = m.hs[:, half, LEFT_AT:].rearrange("k (b n) -> k b n", b=4)
                    for dst, n in ((full, slice(0, FULL)), (left, slice(FULL, MODES))):
                        dve.tensor_tensor(dst[:, 2:4], sv[:, half, 0:2, n], sv[:, half, 2:4, n], ALU.subtract).then_inc(S3.hs, 1)
                    dve.tensor_tensor(m.hef[:, half], sv[:, half, 0:2], sv[:, half, 2:4], ALU.add).then_inc(S3.hef, 1)
                    dve.wait_ge(S3.hef, half + 1)
                    for dst, n in ((full, slice(0, FULL)), (left, slice(FULL, MODES))):
                        dve.tensor_tensor(dst[:, 0], m.hef[:, half, 0, n], m.hef[:, half, 1, n], ALU.add).then_inc(S3.hs, 1)
                        dve.tensor_tensor(dst[:, 1], m.hef[:, half, 0, n], m.hef[:, half, 1, n], ALU.subtract).then_inc(S3.hs, 1)
                dve.wait_ge(S3.back.pe, 2)
                dve.wait_ge(S3.back.act, 1)
                g, h = m.bank[5], m.hpart[:, 0]
                unmix(lambda part, b: m.gb[:, part, b], (g[:, 0:CH], g[:, CH:2 * CH]), (h[:, 0:CH], h[:, CH:2 * CH]), S3.back.dve)
                for n, b in enumerate(OUT_ORDER):
                    dve.wait_ge(S3.inv.pe, n + 1)
                    dve.scalar_tensor_tensor(m.xb[:, b], m.bank[1 + n][:, 0:2 * CH].rearrange("k (t c) -> k t c", t=2),
                                             1.0 / (TOKENS * CH), m.x[:, b], ALU.mult, ALU.add).then_inc(S3.inv.dve, 1)

            dve.memset(m.spare[:], 1.0).then_inc(spare_set, 1)
            dve.memset(m.probs[:, 0, :], 1.0).then_inc(ones_set, 1)
            dve.memset(m.qk_scale[:, 0:1], HD ** -0.5).then_inc(scale_set, 1)
            dve.memset(m.qk_scale[0:64, 1:2], HD ** -0.5).then_inc(scale_set, 1)
            dve.memset(m.qk_scale[64:128, 1:2], 1.0).then_inc(scale_set, 1)
            dve.memset(m.qk_scale[:, 2:3], 1.0).then_inc(scale_set, 1)
            attention(0, lambda b: dve.wait_ge(x_loaded[b], 16))
            spectral1()
            attention(1, add_inverse, lambda: shrink(4))
            spectral3()


def _halves(v):
    return v.reshape(2, HALF).T


def _block_diagonal(blocks):
    n = blocks.shape[-1]
    out = np.zeros((HALF, 2, HALF), blocks.dtype)
    for i in range(8):
        lo = n * (i % 4)
        out[lo:lo + n, i // 4, lo:lo + n] = blocks[i]
    return out


def _laid_out(a):
    out = {"x": a["x"]}
    names = [("norm1_scale", "norm1_bias", "norm2_scale", "norm2_bias"), ("ln1_w", "ln1_b", "ln2_w", "ln2_b")]
    for l, (layer, (s1, b1, s2, b2)) in enumerate(zip(("L0_conv_", "L2_conv_"), names)):
        g = lambda n: a[layer + n]
        qb, kb, vb = g("qkv_b").reshape(3, CH)
        vecs = np.zeros((128, 8 + QK_CHUNKS), np.float32)
        for at, v in ((0, g(s1)), (2, g(b1)), (4 + QK_CHUNKS, g(s2)), (6 + QK_CHUNKS, g(b2))):
            vecs[:HALF, at:at + 2] = _halves(v)
        vecs[:, 4:4 + QK_CHUNKS] = np.concatenate([qb, kb]).reshape(QK_CHUNKS, 128).T
        out[f"vecs{l}"] = vecs
        out[f"qkv{l}"] = g("qkv_w").reshape(2, HALF, 3 * CH).transpose(1, 0, 2)
        for heads in REL_HEADS:
            rel = np.zeros((128, 2, 2 * WIN - 1, heads), np.float32)
            for n, table in enumerate((g("rel_pos_h"), g("rel_pos_w"))):
                for h in range(heads):
                    rel[HD * h:HD * (h + 1), n, :, h] = table[::-1].T
            out[f"rel{heads}{l}"] = rel.reshape(128, 2, -1)
        cols = np.zeros((128, HID_TILES + O_TILES), np.float32)
        cols[:, :HID_TILES] = g("fc1_b").reshape(HID_TILES, 128).T
        proj = np.zeros((128, O_TILES, CH), np.float32)
        for h in range(HEADS):
            at, c = 32 * (h % 4) + HD * (h // 4 % 2), slice(HD * h, HD * (h + 1))
            cols[at:at + HD, HID_TILES + h // 8] = vb[c]
            proj[at:at + HD, h // 8] = g("proj_w")[c]
        out[f"cols{l}"] = cols
        out[f"rows{l}"] = np.broadcast_to(np.stack([g("proj_b"), g("fc2_b")]), (128, 2, CH))
        out[f"proj{l}"] = proj
        out[f"fc1{l}"] = g("fc1_w").reshape(2, HALF, HID).transpose(1, 0, 2)
        out[f"fc2{l}"] = g("fc2_w").reshape(HID_TILES, 128, CH).transpose(1, 0, 2)
    w1, w2 = a["L1_conv_w1"], a["L1_conv_w2"]
    out["f1_w1"] = np.stack([_block_diagonal(w1[..., i]) for i in range(2)], 1)
    out["f1_b1"] = np.stack([_halves(a["L1_conv_b1"][..., i].reshape(-1)) for i in range(2)], 1)
    f1_w2 = np.zeros((HALF + 1, 2, 2, HALF), np.float32)
    for i in range(2):
        f1_w2[:HALF, i] = _block_diagonal(w2[..., i])
        f1_w2[HALF, i] = a["L1_conv_b2"][..., i].reshape(2, HALF)
    out["f1_w2"] = f1_w2
    out["f3_w"] = np.stack([np.stack([_block_diagonal(a[f"L3_conv_{n}"][i]).reshape(HALF, 2 * HALF) for i in range(2)], 1)
                            for n in ("w1", "w2")], 1)
    out["f3_b"] = np.stack([np.stack([_halves(a[f"L3_conv_{n}"][i].reshape(-1)) for i in range(2)], 1)
                            for n in ("b1", "b2")], 1)
    return out


def kernel(**inputs):
    import concourse.bacc as bacc
    from concourse.bass_utils import run_bass_kernel_spmd

    nc = bacc.Bacc("TRN2", target_bir_lowering=False, num_devices=1)
    laid = _laid_out({k: np.asarray(v) for k, v in inputs.items()})
    laid.update(constants())
    arrays, args = {}, {}
    for name, a in laid.items():
        a = np.ascontiguousarray(a)
        arrays[f"in_{name}"] = a
        args[name] = nc.dram_tensor(f"in_{name}", a.shape, mybir.dt.from_np(a.dtype), kind="ExternalInput").ap()
    out = nc.dram_tensor("out", (IMAGES, SIDE, SIDE, CH), F32, kind="ExternalOutput").ap()
    build(nc, args, out)
    result = run_bass_kernel_spmd(nc, [arrays], core_ids=[0])
    return result.results[0]["out"]
```
